# Optimizing a Trainium2 kernel written in Bass

```python
import numpy as np
import jax
import jax.numpy as jnp

def _softmax(x, axis=-1):
    return jax.nn.softmax(x, axis=axis)

def _gelu(x):
    return jax.nn.gelu(x, approximate=True)

def _silu(x):
    return jax.nn.silu(x)

def _sigmoid(x):
    return jax.nn.sigmoid(x)

def _layernorm(x, axis=-1, eps=1e-05):
    m = jnp.mean(x, axis=axis, keepdims=True)
    v = jnp.var(x, axis=axis, keepdims=True)
    return (x - m) / jnp.sqrt(v + eps)

def _scatter_add(tgt, idx, src, axis=0):
    return tgt.at[idx].add(src)

def _segment_sum(src, seg, n):
    return jax.ops.segment_sum(src, seg, n)
kernel_name = 'mk_seq_preln_d1_jaxref_r4_8a8dcb'

def setup_inputs(seed: int=0):
    np.random.seed(seed)
    _w = jnp.asarray

    def _L0_attn_setup():
        import jax, jax.numpy as jnp
        import numpy as np
        IN_FEATURES = 512
        HEAD_NUM = 64
        D = IN_FEATURES // HEAD_NUM
        SCALE = float(np.sqrt(D))
        key = jax.random.key(seed)
        ks = jax.random.split(key, 9)
        F = IN_FEATURES
        x = jax.random.normal(ks[0], (4, 256, F), dtype=jnp.float32)
        w = lambda k: jax.random.normal(k, (F, F), dtype=jnp.float32) * 0.02
        b = lambda k: jax.random.normal(k, (F,), dtype=jnp.float32) * 0.01
        return {'x': x, 'Wq': w(ks[1]), 'bq': b(ks[2]), 'Wk': w(ks[3]), 'bk': b(ks[4]), 'Wv': w(ks[5]), 'bv': b(ks[6]), 'Wo': w(ks[7]), 'bo': b(ks[8])}
    _L0_attn_in = _L0_attn_setup()

    def _L0_ffn_setup():
        import jax, jax.numpy as jnp
        import numpy as np
        _FP4_LUT = jnp.array([0.0, 0.5, 1.0, 1.5, 2.0, 3.0, 4.0, 6.0, -0.0, -0.5, -1.0, -1.5, -2.0, -3.0, -4.0, -6.0], dtype=jnp.float32)
        GROUP_SIZE = 128
        EPS = 1e-06

        def _dequant_fp4(packed_i32, scales_f16, group_size):
            out_f, in_p = packed_i32.shape
            w = packed_i32.astype(jnp.uint32)
            shifts = jnp.arange(8, dtype=jnp.uint32) * 4
            nib = w[:, :, None] >> shifts & jnp.uint32(15)
            vals = _FP4_LUT[nib.astype(jnp.int32)].reshape(out_f, in_p * 8)
            s = scales_f16.astype(jnp.float32).T
            s_full = jnp.repeat(s, group_size, axis=1)
            return vals * s_full
        key = jax.random.key(seed)
        k1, k2, k3, k4, k5 = jax.random.split(key, 5)
        B, S, H, I = (4, 512, 512, 1408)
        x = jax.random.normal(k1, (B, S, H), dtype=jnp.float32)
        gate_up_packed = jax.random.randint(k2, (2 * I, H // 8), 0, 2147483647, dtype=jnp.int32)
        gate_up_scales = jax.random.uniform(k3, (H // GROUP_SIZE, 2 * I), dtype=jnp.float32).astype(jnp.float16)
        down_packed = jax.random.randint(k4, (H, I // 8), 0, 2147483647, dtype=jnp.int32)
        down_scales = jax.random.uniform(k5, (I // GROUP_SIZE, H), dtype=jnp.float32).astype(jnp.float16)
        return {'x': x, 'gate_up_packed': gate_up_packed, 'gate_up_scales': gate_up_scales, 'down_packed': down_packed, 'down_scales': down_scales}
    _L0_ffn_in = _L0_ffn_setup()
    _d = {'L0_attn_x': _L0_attn_in['x'], 'L0_attn_Wq': _L0_attn_in['Wq'], 'L0_attn_bq': _L0_attn_in['bq'], 'L0_attn_Wk': _L0_attn_in['Wk'], 'L0_attn_bk': _L0_attn_in['bk'], 'L0_attn_Wv': _L0_attn_in['Wv'], 'L0_attn_bv': _L0_attn_in['bv'], 'L0_attn_Wo': _L0_attn_in['Wo'], 'L0_attn_bo': _L0_attn_in['bo'], 'L0_ffn_gate_up_packed': _L0_ffn_in['gate_up_packed'], 'L0_ffn_gate_up_scales': _L0_ffn_in['gate_up_scales'], 'L0_ffn_down_packed': _L0_ffn_in['down_packed'], 'L0_ffn_down_scales': _L0_ffn_in['down_scales']}
    _x0 = _d['L0_attn_x']
    _d['L0_attn_x'] = jax.random.normal(jax.random.fold_in(jax.random.key(seed), 1), (4, 1024, 512), dtype=_x0.dtype)
    del _x0
    return _d

def reference(L0_attn_x, L0_attn_Wq, L0_attn_bq, L0_attn_Wk, L0_attn_bk, L0_attn_Wv, L0_attn_bv, L0_attn_Wo, L0_attn_bo, L0_ffn_gate_up_packed, L0_ffn_gate_up_scales, L0_ffn_down_packed, L0_ffn_down_scales):

    def _L0_attn_ref(x, Wq, bq, Wk, bk, Wv, bv, Wo, bo):
        import jax, jax.numpy as jnp
        import numpy as np
        IN_FEATURES = 512
        HEAD_NUM = 64
        D = IN_FEATURES // HEAD_NUM
        SCALE = float(np.sqrt(D))
        B, S, F = x.shape
        d = D
        h = F // d
        q = x @ Wq + bq
        k = x @ Wk + bk
        v = x @ Wv + bv

        def to_heads(t):
            return t.reshape(B, S, d, h).transpose(0, 2, 1, 3)
        q, k, v = (to_heads(q), to_heads(k), to_heads(v))
        scores = jnp.einsum('bdsh,bdth->bdst', q, k) / SCALE
        weights = jax.nn.softmax(scores, axis=-1)
        feats = jnp.einsum('bdst,bdth->bdsh', weights, v)
        feats = feats.transpose(0, 2, 1, 3).reshape(B, S, F)
        return feats @ Wo + bo

    def _L0_ffn_ref(x, gate_up_packed, gate_up_scales, down_packed, down_scales):
        import jax, jax.numpy as jnp
        import numpy as np
        _FP4_LUT = jnp.array([0.0, 0.5, 1.0, 1.5, 2.0, 3.0, 4.0, 6.0, -0.0, -0.5, -1.0, -1.5, -2.0, -3.0, -4.0, -6.0], dtype=jnp.float32)
        GROUP_SIZE = 128
        EPS = 1e-06

        def _dequant_fp4(packed_i32, scales_f16, group_size):
            out_f, in_p = packed_i32.shape
            w = packed_i32.astype(jnp.uint32)
            shifts = jnp.arange(8, dtype=jnp.uint32) * 4
            nib = w[:, :, None] >> shifts & jnp.uint32(15)
            vals = _FP4_LUT[nib.astype(jnp.int32)].reshape(out_f, in_p * 8)
            s = scales_f16.astype(jnp.float32).T
            s_full = jnp.repeat(s, group_size, axis=1)
            return vals * s_full
        I = gate_up_packed.shape[0] // 2
        w_gu = _dequant_fp4(gate_up_packed, gate_up_scales, GROUP_SIZE)
        w_down = _dequant_fp4(down_packed, down_scales, GROUP_SIZE)
        gate_up = jnp.einsum('bsh,oh->bso', x, w_gu)
        gate, up = (gate_up[..., :I], gate_up[..., I:])
        h = jax.nn.silu(gate) * up
        y = jnp.einsum('bsi,hi->bsh', h, w_down)
        rms = jnp.sqrt(jnp.mean(y * y, axis=-1, keepdims=True) + EPS)
        return y / rms
    x = L0_attn_x
    x = x + _L0_attn_ref(_layernorm(x, axis=-1), L0_attn_Wq, L0_attn_bq, L0_attn_Wk, L0_attn_bk, L0_attn_Wv, L0_attn_bv, L0_attn_Wo, L0_attn_bo)
    x = x + _L0_ffn_ref(_layernorm(x, axis=-1), L0_ffn_gate_up_packed, L0_ffn_gate_up_scales, L0_ffn_down_packed, L0_ffn_down_scales)
    return x

_drawn_inputs = setup_inputs


def setup_inputs(seed=0):
    import zlib

    import numpy as np

    out = dict(_drawn_inputs(seed))
    spreads = {}
    factors = {'L0_attn_Wq': 7.01,
     'L0_attn_bq': 8.0,
     'L0_attn_Wk': 7.012,
     'L0_attn_bk': 64.0,
     'L0_attn_Wv': 5.092,
     'L0_attn_bv': 8.0,
     'L0_attn_Wo': 4.187,
     'L0_attn_bo': 24.526}
    for name, (base, spread) in spreads.items():
        noise = np.random.default_rng([zlib.crc32(name.encode()), seed]).standard_normal(out[name].shape)
        drawn = base * np.exp(spread * noise) if base else spread * noise
        out[name] = jnp.asarray(drawn.astype(out[name].dtype))
    for name, factor in factors.items():
        out[name] = (out[name] * factor).astype(out[name].dtype)
    return out
```

```python
from contextlib import ExitStack

import numpy as np

import concourse.bass as bass
from concourse import mybir

P = 128
BATCH, SEQ, F = 4, 1024, 512
HEADS, HD = 8, 64
PAIRS = HEADS // 2
KT = F // P
ST = SEQ // P
NC = 512
FFN = 1408
FI = FFN // P
GROUPS = F // P
NIB = 8
LN_EPS, RMS_EPS = 1e-5, 1e-6
SCORE_SCALE = HEADS ** -0.5
UNITS = PAIRS * ST * 2
PV_UNITS = 4
LAG = 2
CHUNKS = BATCH * SEQ // NC
CT = NC // P
AHEAD = 3


class Ring:

    def __init__(self, uses, banks):
        self.number = {u: n for n, u in enumerate(uses)}
        self.bank = {u: n % banks for n, u in enumerate(uses)}
        self.turn = {u: n // banks for n, u in enumerate(uses)}
        self.total = len(uses)
        self.turns = [len(uses[k::banks]) for k in range(banks)]


def attention_schedule():
    filler = {g: [] for g in range(UNITS)}
    for g in range(4):
        filler[g] += [("v", 2 * g), ("v", 2 * g + 1)]
    for c in range(UNITS // PV_UNITS - 1):
        filler[PV_UNITS * c + PV_UNITS + LAG + 1].append(("pv", c))
    per_pair = UNITS // PAIRS
    for p in range(PAIRS):
        for n, u in enumerate((1, 5, 9, 12) if 0 < p < PAIRS - 1 else (5, 8, 10, 13)):
            filler[per_pair * p + u].append(("qk", (p + 1) % PAIRS, n))
    for i in range(ST):
        filler[per_pair * (PAIRS - 1) - ST // 2 + 1 + i].insert(0, ("xt", i))
    tail = [("pv", UNITS // PV_UNITS - 1)] + [("wo", i) for i in range(ST)]
    return filler, tail


def stats_unit(i):
    return UNITS // PAIRS * (PAIRS - 1) - ST // 2 + 1 + i - 2


def build(nc, x, Wq, bq, Wk, bk, Wv, bv, Wo, bo, gu_packed, gu_scales, d_packed, d_scales, out):
    f32, f32r, i32, f16 = mybir.dt.float32, mybir.dt.float32r, mybir.dt.int32, mybir.dt.float16
    ctx = ExitStack()
    with ctx:
        ffn_values = nc.dram_tensor("ffn_values", (FI, P, 3 * F), f32, kind="Internal").ap()
        x1_scratch = nc.dram_tensor("x1_scratch", (BATCH * ST, P, F), f32, kind="Internal").ap()
        ident = ctx.enter_context(nc.sbuf_tensor("ident", [P, P], f32))
        consts = ctx.enter_context(nc.sbuf_tensor("consts", [P, 2 * P], f32))
        bq_scaled = ctx.enter_context(nc.sbuf_tensor("bq_scaled", [P, PAIRS], f32))
        minus_half = ctx.enter_context(nc.sbuf_tensor("minus_half", [P, 4], f32))
        consts_of = {
            "gu": lambda g, t: consts[:, g * 2 * FI + t:g * 2 * FI + t + 1],
            "down": lambda i, j: consts[:, P + i * KT + j:P + i * KT + j + 1],
            "bk": lambda p: consts[:, P + 96 + p:P + 97 + p],
            "bq": consts[:, P + 64:P + 64 + PAIRS],
        }
        build_prep(nc, gu_packed, gu_scales, d_packed, d_scales, bq, bk, ident, consts, consts_of, bq_scaled,
                   minus_half, ffn_values)
        build_attention(nc, x, Wq, Wk, Wv, bv, Wo, bo, ident, consts_of, bq_scaled, minus_half, x1_scratch)
        build_ffn(nc, x1_scratch, ffn_values, ident, consts_of, minus_half, out)


def build_prep(nc, gu_packed, gu_scales, d_packed, d_scales, bq, bk, ident, consts, consts_of, bq_scaled,
               minus_half, ffn_values):
    f32, i32, f16 = mybir.dt.float32, mybir.dt.int32, mybir.dt.float16
    ALU, ACT = mybir.AluOpType, mybir.ActivationFunctionType
    GW, DW = F // NIB, FFN // NIB
    WORDS = 2 * FI * GW + KT * DW
    HALF_TILES = 16
    SPANS = [(0, HALF_TILES * GW), (HALF_TILES * GW, WORDS)]
    SPAN = max(b - a for a, b in SPANS)
    STEPS = [(s, j) for s in range(len(SPANS)) for j in range(NIB)]
    TILES = [("gu", t) for t in range(2 * FI)] + [("down", i) for i in range(FI)]
    BANKS = 8
    ring = Ring(TILES, BANKS)

    ctx = ExitStack()
    with ctx:
        sb = lambda name, shape, dt: ctx.enter_context(nc.sbuf_tensor(name, shape, dt))
        sem = lambda name: ctx.enter_context(nc.semaphore(name))
        packed = sb("packed", [P, WORDS], i32)
        values = sb("values", [P, WORDS * NIB], f32)
        stage = sb("stage", [P, FI, 3 * F], f32)
        mag = sb("mag", [P, 2, SPAN], i32)
        sign = sb("sign", [P, 2, SPAN], i32)
        over4 = sb("over4", [P, 2, SPAN], f32)
        over6 = sb("over6", [P, 2, SPAN], f32)
        half = sb("half", [P, 2, SPAN], f32)
        twice = sb("twice", [P, 2, SPAN], f32)
        scales16 = sb("scales16", [P, 2, P], f16)
        rows = sb("rows", [P, 2, P], f32)
        psum = ctx.enter_context(nc.psum_tensor("prep_psum", [P, BANKS, NC], f32))

        packed_loaded = [sem(f"packed_loaded{n}") for n in range(2)]
        scales_loaded = sem("scales_loaded")
        biases_loaded = sem("biases_loaded")
        rows_zeroed = sem("rows_zeroed")
        rows_cast = sem("rows_cast")
        ident_zeroed = sem("ident_zeroed")
        ident_ready = sem("ident_ready")
        consts_transposed = sem("consts_transposed")
        consts_ready = sem("consts_ready")
        codes_ready = sem("codes_ready")
        terms_ready = sem("terms_ready")
        mag_over4_ready = sem("mag_over4_ready")
        sum_ready = sem("sum_ready")
        first_sum_ready = sem("first_sum_ready")
        values_done = sem("values_done")
        tiles_transposed = sem("tiles_transposed")
        tile_staged = [sem(f"tile_staged{k}") for k in range(BANKS)]
        values_stored = sem("values_stored")
        block = ctx.enter_context(nc.Block(name="prep"))

        def nibble_view(span, j):
            a, b = SPANS[span]
            return values[:, a * NIB:b * NIB].rearrange("p (w j) -> p w j", j=NIB)[:, :, j]

        def staged(kind, n):
            if kind == "down":
                return stage[:, n, 2 * F:3 * F]
            return stage[:, n % FI, (n // FI) * F:(n // FI) * F + F]

        @block.sync
        def _(sp):
            gu_rows = gu_packed.rearrange("(t p) w -> p t w", p=P)
            sp.dma_start(packed[:, 0:SPANS[0][1]].rearrange("p (t w) -> p t w", w=GW),
                         gu_rows[:, 0:HALF_TILES, :]).then_inc(packed_loaded[0], 16)
            sp.dma_start(packed[:, SPANS[0][1]:2 * FI * GW].rearrange("p (t w) -> p t w", w=GW),
                         gu_rows[:, HALF_TILES:, :]).then_inc(packed_loaded[1], 16)
            sp.dma_start(packed[:, 2 * FI * GW:].rearrange("p (t w) -> p t w", w=DW),
                         d_packed.rearrange("(t p) w -> p t w", p=P)).then_inc(packed_loaded[1], 16)
            sp.dma_start(scales16[0:GROUPS * 2 * FI, 0, :],
                         gu_scales.rearrange("g (t p) -> (g t) p", p=P)).then_inc(scales_loaded, 16)
            sp.dma_start(scales16[0:FI * KT, 1, :],
                         d_scales.rearrange("g (t p) -> (g t) p", p=P)).then_inc(scales_loaded, 16)
            sp.wait_ge(rows_zeroed, 1)
            sp.dma_start(rows[64:64 + PAIRS, 1, :], bq.rearrange("(t p) -> t p", p=P)).then_inc(biases_loaded, 16)
            sp.dma_start(rows[96:96 + PAIRS, 1, :], bk.rearrange("(t p) -> t p", p=P)).then_inc(biases_loaded, 16)
            for i in range(FI):
                for use in (("gu", i), ("gu", FI + i), ("down", i)):
                    sp.wait_ge(tile_staged[ring.bank[use]], ring.turn[use] + 1)
                sp.dma_start(ffn_values[i], stage[:, i, :]).then_inc(values_stored, 16)
            sp.wait_ge(values_stored, 16 * FI)

        @block.gpsimd
        def _(pool):
            nc.gpsimd.memset(minus_half[:], -0.5)
            nc.gpsimd.memset(ident[:], 0.0).then_inc(ident_zeroed, 1)
            pool.wait_ge(ident_zeroed, 1)
            nc.gpsimd.affine_select(out=ident[:], in_=ident[:], compare_op=ALU.not_equal, fill=1.0, base=0,
                                    pattern=[[-1, P]], channel_multiplier=1).then_inc(ident_ready, 1)
            for k, (span, j) in enumerate(STEPS):
                n = SPANS[span][1] - SPANS[span][0]
                pool.wait_ge(terms_ready, k + 1)
                pool.wait_ge(first_sum_ready, k + 1)
                nc.gpsimd.tensor_tensor(twice[:, k % 2, 0:n], twice[:, k % 2, 0:n], over6[:, k % 2, 0:n],
                                        ALU.add).then_inc(sum_ready, 1)

        @block.scalar
        def _(act):
            for k, (span, j) in enumerate(STEPS):
                n = SPANS[span][1] - SPANS[span][0]
                act.wait_ge(codes_ready, k + 1)
                if k >= 2:
                    act.wait_ge(values_done, k - 1)
                s = k % 2
                nc.scalar.activation(over4[:, s, 0:n], mag[:, s, 0:n], ACT.Relu, bias=-4.0).then_inc(mag_over4_ready, 1)
                nc.scalar.activation(over6[:, s, 0:n], mag[:, s, 0:n], ACT.Relu, bias=-12.0, scale=2.0)
                nc.scalar.activation(half[:, s, 0:n], sign[:, s, 0:n], ACT.Copy, bias=0.5,
                                     scale=-0.125).then_inc(terms_ready, 1)
            for n, use in enumerate(TILES):
                if n % 2 == 0:
                    act.wait_ge(tiles_transposed, n + 1)
                    nc.scalar.activation(staged(*use), psum[:, ring.bank[use], :],
                                         ACT.Copy).then_inc(tile_staged[ring.bank[use]], 1)

        @block.vector
        def _(dve):
            def codes(k):
                span, j = STEPS[k]
                a, b = SPANS[span]
                if j == 0:
                    dve.wait_ge(packed_loaded[span], 16 if span == 0 else 32)
                nc.vector.tensor_scalar(mag[:, k % 2, 0:b - a], packed[:, a:b], 4 * j, 7,
                                        ALU.logical_shift_right, ALU.bitwise_and)
                nc.vector.tensor_scalar(sign[:, k % 2, 0:b - a], packed[:, a:b], 4 * j, 8,
                                        ALU.logical_shift_right, ALU.bitwise_and).then_inc(codes_ready, 1)

            nc.vector.memset(rows[:], 0.0).then_inc(rows_zeroed, 1)
            dve.wait_ge(scales_loaded, 32)
            dve.wait_ge(rows_zeroed, 1)
            nc.vector.tensor_copy(rows[0:GROUPS * 2 * FI, 0, :], scales16[0:GROUPS * 2 * FI, 0, :])
            nc.vector.tensor_copy(rows[0:FI * KT, 1, :], scales16[0:FI * KT, 1, :]).then_inc(rows_cast, 1)
            codes(0)
            dve.wait_ge(consts_transposed, 1)
            nc.vector.tensor_copy(consts[:], psum[:, 0, 0:2 * P]).then_inc(consts_ready, 1)
            dve.wait_ge(consts_ready, 1)
            nc.vector.tensor_scalar(bq_scaled[:], consts_of["bq"], SCORE_SCALE, None,
                                    ALU.mult).then_inc(consts_ready, 1)
            for k in range(len(STEPS) + 1):
                if k + 1 < len(STEPS):
                    if k:
                        dve.wait_ge(terms_ready, k)
                        dve.wait_ge(first_sum_ready, k)
                    codes(k + 1)
                if k < len(STEPS):
                    n = SPANS[STEPS[k][0]][1] - SPANS[STEPS[k][0]][0]
                    dve.wait_ge(mag_over4_ready, k + 1)
                    nc.vector.tensor_tensor(twice[:, k % 2, 0:n], mag[:, k % 2, 0:n], over4[:, k % 2, 0:n],
                                            ALU.add).then_inc(first_sum_ready, 1)
                if k:
                    span, j = STEPS[k - 1]
                    n, s = SPANS[span][1] - SPANS[span][0], (k - 1) % 2
                    dve.wait_ge(sum_ready, k)
                    nc.vector.tensor_tensor(nibble_view(span, j), twice[:, s, 0:n], half[:, s, 0:n],
                                            ALU.mult).then_inc(values_done, 1)
            for n, use in enumerate(TILES):
                if n % 2 == 1:
                    dve.wait_ge(tiles_transposed, n + 1)
                    nc.vector.tensor_copy(staged(*use), psum[:, ring.bank[use], :]).then_inc(
                        tile_staged[ring.bank[use]], 1)

        @block.tensor
        def _(pe):
            pe.wait_ge(ident_ready, 1)
            pe.wait_ge(rows_cast, 1)
            pe.wait_ge(biases_loaded, 32)
            nc.tensor.transpose(psum[:, 0, 0:P], rows[:, 0, :], ident[:])
            nc.tensor.transpose(psum[:, 0, P:2 * P], rows[:, 1, :], ident[:]).then_inc(consts_transposed, 1)
            pe.wait_ge(consts_ready, 1)
            for n, (kind, t) in enumerate(TILES):
                if n == 0:
                    pe.wait_ge(values_done, NIB)
                if n == HALF_TILES:
                    pe.wait_ge(values_done, 2 * NIB)
                if ring.turn[kind, t]:
                    pe.wait_ge(tile_staged[ring.bank[kind, t]], ring.turn[kind, t])
                for q in range(4):
                    at = t * F + q * P if kind == "gu" else 2 * FI * F + q * FFN + t * P
                    last = nc.tensor.transpose(psum[:, ring.bank[kind, t], q * P:(q + 1) * P],
                                               values[:, at:at + P], ident[:])
                last.then_inc(tiles_transposed, 1)


def build_attention(nc, x, Wq, Wk, Wv, bv, Wo, bo, ident, consts_of, bq_scaled, minus_half, x1_scratch):
    f32, f32r = mybir.dt.float32, mybir.dt.float32r
    ALU, ACT, AX = mybir.AluOpType, mybir.ActivationFunctionType, mybir.AxisListType
    filler, tail = attention_schedule()
    PER_PAIR = UNITS // PAIRS
    PV_CHUNKS = UNITS // PV_UNITS
    PV_TOKENS = PV_UNITS // 2 * P
    first = Ring([("xt", i) for i in range(ST)] + [("qk", 0, n) for n in range(4)], 2)
    body = Ring([u for g in range(UNITS) for u in filler[g]] + tail, 2)
    assert first.total % 2 == 0 and body.total % 2 == 0
    qk_order = {u: n for n, u in enumerate(u for g in range(UNITS) for u in filler[g] if u[0] == "qk")}
    PROBS = 4

    ctx = ExitStack()
    with ctx:
        sb = lambda name, shape, dt=f32: ctx.enter_context(nc.sbuf_tensor(name, shape, dt))
        sem = lambda name: ctx.enter_context(nc.semaphore(name))
        wq, wk, wv, wo = (sb(n, [P, KT, F]) for n in ("wq", "wk", "wv", "wo"))
        bv_rows, bo_rows = sb("bv_rows", [P, F]), sb("bo_rows", [P, F])
        x_in = sb("x_in", [P, 2, F])
        stats = sb("stats", [P, 2, 6])
        mean_var = sb("mean_var", [P, 2, 2])
        var_eps = sb("var_eps", [P, 2, 1])
        rstd = sb("rstd", [P, 2, 1])
        shift = sb("shift", [P, 2, 1])
        xn = sb("xn", [P, 2, F])
        xnT = sb("xnT", [P, KT, SEQ])
        qk_full = sb("qk_full", [P, 2, NC])
        q_parts = [sb(f"q_parts{n}", [P, 2, SEQ], f32r) for n in range(2)]
        k_high = [sb(f"k_high{n}", [P, 2, SEQ], f32r) for n in range(2)]
        k_low = [sb(f"k_low{n}", [P, 2, SEQ], f32r) for n in range(2)]
        v = sb("v", [P, ST, F])
        neg_max = sb("neg_max", [P, PROBS, 1])
        sums = sb("sums", [P, 2, PV_UNITS])
        recip = sb("recip", [P, 2, PV_UNITS])
        recip_wide = sb("recip_wide", [P, 2, PV_UNITS, HD])
        probs = sb("probs", [P, PROBS, SEQ])
        probsT = sb("probsT", [P, 2, ST, 2, PV_TOKENS])
        recip_cols = sb("recip_cols", [P, 2, PV_TOKENS])
        featsT = sb("featsT", [P, PAIRS, SEQ])
        residual = sb("residual", [P, 2, F])
        x1_out = sb("x1_out", [P, 2, F])
        score_psum = ctx.enter_context(nc.psum_tensor("score_psum", [P, 2, SEQ], f32))
        transpose_psum = ctx.enter_context(nc.psum_tensor("transpose_psum", [P, 2, NC], f32))
        general_psum = ctx.enter_context(nc.psum_tensor("general_psum", [P, 2, NC], f32))

        wqk_loaded, wv_loaded, wo_loaded = sem("wqk_loaded"), sem("wv_loaded"), sem("wo_loaded")
        x_loaded = [sem(f"x_loaded{n}") for n in range(2)]
        residual_loaded = [sem(f"residual_loaded{n}") for n in range(2)]
        stored = [sem(f"x1_stored{n}") for n in range(2)]
        last_row_stored = sem("last_row_stored")
        residual_ready = sem("residual_ready")
        stats_step, stats_seen = sem("stats_step"), sem("stats_seen")
        var_ready = sem("var_ready")
        rstd_ready = sem("rstd_ready")
        shift_ready = sem("shift_ready")
        norm_done = sem("norm_done")
        high_ready = sem("high_ready")
        low_ready = sem("low_ready")
        scores_done = sem("scores_done")
        max_ready = sem("max_ready")
        exp_done = sem("exp_done")
        transposed = sem("transposed")
        copied_low = sem("copied_low")
        copied_high = sem("copied_high")
        recip_step = sem("recip_step")
        recip_ready = sem("recip_ready")
        cols_ready = sem("cols_ready")
        general_done = sem("general_done")
        emptied = [sem(f"general_emptied{n}") for n in range(2)]
        block = ctx.enter_context(nc.Block(name="attention"))

        def done(use, b=None):
            if b is None:
                return first.number[use] + 1
            return b * body.total + (first.total + body.number[use] + 1)

        def empty(use, b=None):
            if b is None:
                return first.turn[use] + 1
            return b * body.turns[0] + (first.turns[0] + body.turn[use] + 1)

        QK_ROW = 4 * PAIRS

        def low_ops(n):
            return n // 4 * 12 + (0, 2, 4, 8)[n % 4]

        def unit(g):
            return g // PER_PAIR, g % PER_PAIR // 2, g % 2

        def place(c):
            p, n = c // (PV_CHUNKS // PAIRS), c % (PV_CHUNKS // PAIRS)
            return p, slice(n * PV_TOKENS, (n + 1) * PV_TOKENS)

        x_tiles = x.rearrange("b (t p) f -> (b t) p f", p=P)

        def tile_at(ap, n):
            return ap[bass.ds(n, 1)].rearrange("a p f -> (a p) f")

        @block.sync
        def _(sp):
            def load_x(i, source, free):
                if free is not None:
                    sp.wait_ge(norm_done, free)
                sp.dma_start(x_in[:, i % 2, :], source).then_inc(x_loaded[i % 2], 16)

            load_x(0, x_tiles[0], None)
            load_x(1, x_tiles[1], None)
            sp.dma_start(wq[:], Wq.rearrange("(t p) n -> p t n", p=P)).then_inc(wqk_loaded, 16)
            sp.dma_start(wk[:], Wk.rearrange("(t p) n -> p t n", p=P)).then_inc(wqk_loaded, 16)
            for i in range(2, ST):
                load_x(i, x_tiles[i], i - 1)
            sp.dma_start(wv[:], Wv.rearrange("(t p) n -> p t n", p=P)).then_inc(wv_loaded, 16)
            sp.dma_start(bv_rows[:], bv.rearrange("(a n) -> a n", a=1).to_broadcast([P, F])).then_inc(wv_loaded, 16)
            sp.dma_start(wo[:], Wo.rearrange("(t p) n -> p t n", p=P)).then_inc(wo_loaded, 16)
            sp.dma_start(bo_rows[:], bo.rearrange("(a n) -> a n", a=1).to_broadcast([P, F])).then_inc(wo_loaded, 16)
            sp.sem_inc(last_row_stored, 1)
            with sp.Fori(0, BATCH) as b:
                for i in range(2):
                    sp.dma_start(residual[:, i, :], tile_at(x_tiles, b * ST + i)).then_inc(residual_loaded[i], 16)
                for i in range(ST):
                    load_x(i, tile_at(x_tiles, (b + 1) % BATCH * ST + i), b * ST + (ST + i - 1))
                for i in range(ST):
                    use = ("wo", i)
                    sp.wait_ge(emptied[body.bank[use]], empty(use, b))
                    sp.dma_start(tile_at(x1_scratch, b * ST + i), x1_out[:, i % 2, :]).then_inc(stored[i % 2], 16)
                    if i + 2 < ST:
                        sp.dma_start(residual[:, i % 2, :],
                                     tile_at(x_tiles, b * ST + (i + 2))).then_inc(residual_loaded[i % 2], 16)
                for n in range(2):
                    sp.wait_ge(stored[n], b * (16 * ST // 2) + 16 * ST // 2)
                sp.sem_inc(last_row_stored, 1)

        @block.gpsimd
        def _(pool):
            def inverse_std(i, count):
                pool.wait_ge(var_ready, count)
                nc.gpsimd.tensor_tensor(rstd[:, i % 2, :], var_eps[:, i % 2, :], minus_half[:, 0:1],
                                        ALU.pow).then_inc(rstd_ready, 1)

            def low_parts(use, count, ops_before):
                _, p, n = use
                s, tok = p % 2, slice(n % 2 * NC, (n % 2 + 1) * NC)
                pool.wait_ge(high_ready, count)
                parts = q_parts[s] if n < 2 else k_high[s]
                low = q_parts[s] if n < 2 else k_low[s]
                for h in range(2):
                    own, other = slice(h * HD, (h + 1) * HD), slice((1 - h) * HD, (2 - h) * HD)
                    for m, rows in enumerate((other,) if n < 2 else (own, other)):
                        nc.gpsimd.tensor_tensor(low[rows, h, tok], qk_full[own, n % 2, :],
                                                parts[own, h, tok].bitcast(f32), ALU.subtract
                                                ).then_inc(low_ready, 1)
                        pool.wait_ge(low_ready, ops_before + ((1 if n < 2 else 2) * h + m + 1))

            for i in range(ST):
                inverse_std(i, i + 1)
            for n in range(4):
                low_parts(("qk", 0, n), n + 1, low_ops(n))
            pool.wait_ge(wo_loaded, 32)
            with pool.Fori(0, BATCH) as b:
                for g in range(UNITS):
                    for i in range(ST):
                        if stats_unit(i) == g:
                            inverse_std(i, b * ST + (ST + i + 1))
                    for use in filler[g]:
                        if use[0] == "qk":
                            low_parts(use, b * QK_ROW + (4 + qk_order[use] + 1),
                                      b * low_ops(QK_ROW) + low_ops(4 + qk_order[use]))
                for i in range(ST):
                    pool.wait_ge(residual_loaded[i % 2], b * (16 * ST // 2) + 16 * (i // 2 + 1))
                    nc.gpsimd.tensor_tensor(residual[:, i % 2, :], residual[:, i % 2, :], bo_rows[:],
                                            ALU.add).then_inc(residual_ready, 1)

        @block.scalar
        def _(act):
            def copy_out(use, b=None, split=None):
                kind = use[0]
                ring = first if b is None else body
                bank = ring.bank[use]
                if kind == "xt":
                    act.wait_ge(general_done, done(use, b))
                    i = use[1]
                    nc.scalar.activation(xnT[:, :, i * P:(i + 1) * P], general_psum[:, bank, :].rearrange(
                        "p (k t) -> p k t", k=KT), ACT.Copy).then_inc(emptied[bank], 1)
                if kind == "qk":
                    _, p, n = use
                    act.wait_ge(general_done, done(use, b))
                    if split is not None:
                        act.wait_ge(low_ready, split)
                    bias, scale = (bq_scaled[:, p:p + 1], SCORE_SCALE) if n < 2 else (consts_of["bk"](p), 1.0)
                    nc.scalar.activation(qk_full[:, n % 2, :], general_psum[:, bank, :], ACT.Identity, bias=bias,
                                         scale=scale).then_inc(emptied[bank], 1)
                if kind == "pv":
                    c = use[1]
                    act.wait_ge(general_done, done(use, b))
                    nc.scalar.activation(recip_cols[:, c % 2, :], general_psum[:, bank, PV_TOKENS:],
                                         ACT.Copy).then_inc(cols_ready, 1)

            def copy_transposed(g, b):
                _, st, h = unit(g)
                c = g // PV_UNITS
                act.wait_ge(transposed, b * (2 * UNITS) + (2 * PROBS + 2 * g + 1))
                nc.scalar.activation(probsT[:, c % 2, 0:4, h, st % 2 * P:(st % 2 + 1) * P],
                                     transpose_psum[:, 0, :].rearrange("p (k t) -> p k t", k=4),
                                     ACT.Copy).then_inc(copied_low, 1)

            act.sem_inc(exp_done, 2)
            act.sem_inc(copied_low, 1)
            for i in range(ST):
                copy_out(("xt", i))
            for n in range(4):
                copy_out(("qk", 0, n), None, low_ops(n - 1) if n >= 2 else None)
            with act.Fori(0, BATCH) as b:
                for g in range(UNITS + LAG):
                    short = g >= UNITS or not filler[g]
                    if g >= LAG and short:
                        copy_transposed(g - LAG, b)
                    if g < UNITS:
                        act.wait_ge(max_ready, b * UNITS + (g + 1))
                        act.wait_ge(transposed, b * (2 * UNITS) + (2 * g + 2))
                        nc.scalar.activation(probs[:, g % PROBS, :], score_psum[:, g % 2, :], ACT.Exp,
                                             bias=neg_max[:, g % PROBS, :],
                                             accum_out=sums[:, g // PV_UNITS % 2, g % PV_UNITS:g % PV_UNITS + 1],
                                             ).then_inc(exp_done, 1)
                        for use in filler[g]:
                            copy_out(use, b, b * low_ops(QK_ROW) + low_ops(3 + qk_order[use])
                                     if use[0] == "qk" else None)
                    if g >= LAG and not short:
                        copy_transposed(g - LAG, b)
                copy_out(tail[0], b)

        @block.vector
        def _(dve):
            def tile_stats(i, loads, tile):
                s = i % 2
                dve.wait_ge(x_loaded[s], loads)
                nc.vector.bn_stats(stats[:, s, :], x_in[:, s, :]).then_inc(stats_step, 1)
                dve.wait_ge(stats_step, tile * 2 + 1)
                dve.sem_inc(stats_seen, 1)
                nc.vector.bn_aggr(mean_var[:, s, :], stats[:, s, :]).then_inc(stats_step, 1)
                dve.wait_ge(stats_step, tile * 2 + 2)
                nc.vector.tensor_scalar(var_eps[:, s, :], mean_var[:, s, 1:2], LN_EPS, None,
                                        ALU.add).then_inc(var_ready, 1)

            def normalise(i, tile, slot_read=None):
                s = i % 2
                dve.wait_ge(rstd_ready, tile + 1)
                nc.vector.scalar_tensor_tensor(shift[:, s, :], mean_var[:, s, 0:1], -1.0, rstd[:, s, :], ALU.mult,
                                               ALU.mult).then_inc(shift_ready, 1)
                dve.wait_ge(shift_ready, tile + 1)
                if slot_read is not None:
                    dve.wait_ge(general_done, slot_read)
                nc.vector.tensor_scalar(xn[:, s, :], x_in[:, s, :], rstd[:, s, :], shift[:, s, :], ALU.mult,
                                        ALU.add).then_inc(norm_done, 1)

            def high_parts(use, b=None):
                _, p, n = use
                s, tok = p % 2, slice(n % 2 * NC, (n % 2 + 1) * NC)
                ring = first if b is None else body
                dve.wait_ge(emptied[ring.bank[use]], empty(use, b))
                high = q_parts[s] if n < 2 else k_high[s]
                for h in range(2):
                    own, other = slice(h * HD, (h + 1) * HD), slice((1 - h) * HD, (2 - h) * HD)
                    for rows in ((own,) if n < 2 else (own, other)):
                        last = nc.vector.tensor_copy(high[rows, h, tok], qk_full[own, n % 2, :])
                last.then_inc(high_ready, 1)

            def copy_out(use, b):
                kind, bank = use[0], body.bank[use]
                if kind == "v":
                    dve.wait_ge(general_done, done(use, b))
                    nc.vector.tensor_tensor(v[:, use[1], :], general_psum[:, bank, :], bv_rows[:],
                                            ALU.add).then_inc(emptied[bank], 1)
                if kind == "pv":
                    c = use[1]
                    p, tok = place(c)
                    dve.wait_ge(cols_ready, b * PV_CHUNKS + (c + 1))
                    nc.vector.tensor_tensor(featsT[:, p, tok], general_psum[:, bank, 0:PV_TOKENS],
                                            recip_cols[:, c % 2, :], ALU.mult).then_inc(emptied[bank], 1)
                if kind == "wo":
                    i = use[1]
                    dve.wait_ge(general_done, done(use, b))
                    dve.wait_ge(residual_ready, b * ST + (i + 1))
                    if i < 2:
                        dve.wait_ge(last_row_stored, b + 1)
                    else:
                        dve.wait_ge(stored[i % 2], b * (16 * ST // 2) + 16 * (i // 2))
                    nc.vector.tensor_tensor(x1_out[:, i % 2, :], general_psum[:, bank, :], residual[:, i % 2, :],
                                            ALU.add).then_inc(emptied[bank], 1)

            def copy_transposed(g, b):
                _, st, h = unit(g)
                c = g // PV_UNITS
                dve.wait_ge(transposed, b * (2 * UNITS) + (2 * PROBS + 2 * g + 2))
                nc.vector.tensor_copy(probsT[:, c % 2, 4:8, h, st % 2 * P:(st % 2 + 1) * P],
                                      transpose_psum[:, 1, :].rearrange("p (k t) -> p k t", k=4)
                                      ).then_inc(copied_high, 1)
                if g % PV_UNITS == PV_UNITS - 1:
                    dve.wait_ge(exp_done, b * UNITS + (2 + g + 1))
                    nc.vector.reciprocal(recip[:, c % 2, :], sums[:, c % 2, :]).then_inc(recip_step, 1)
                    dve.wait_ge(recip_step, b * PV_CHUNKS + (c + 1))
                    nc.vector.tensor_copy(recip_wide[:, c % 2], recip[:, c % 2, :].rearrange(
                        "p (u o) -> p u o", o=1).to_broadcast([P, PV_UNITS, HD])).then_inc(recip_ready, 1)

            dve.sem_inc(copied_high, 1)
            for i in range(ST + 1):
                if i < ST:
                    tile_stats(i, 16 * (i // 2 + 1), i)
                if i:
                    normalise(i - 1, i - 1, done(("xt", i - 3)) if i >= 3 else None)
            for n in range(4):
                high_parts(("qk", 0, n))
            dve.wait_ge(wv_loaded, 32)
            with dve.Fori(0, BATCH) as b:
                for g in range(UNITS + LAG):
                    if g < UNITS:
                        dve.wait_ge(scores_done, b * UNITS + (g + 1))
                        nc.vector.tensor_reduce(neg_max[:, g % PROBS, :], score_psum[:, g % 2, :], AX.X, ALU.max,
                                                negate=True).then_inc(max_ready, 1)
                        for i in range(ST):
                            if stats_unit(i) == g:
                                tile_stats(i, b * (16 * ST // 2) + 16 * (ST // 2 + i // 2 + 1), b * ST + (ST + i))
                            if stats_unit(i) + 1 == g:
                                normalise(i, b * ST + (ST + i))
                        for use in filler[g]:
                            copy_out(use, b)
                    if g >= LAG:
                        copy_transposed(g - LAG, b)
                    if g < UNITS:
                        for use in filler[g]:
                            if use[0] == "qk":
                                high_parts(use, b)
                for use in tail:
                    copy_out(use, b)

        @block.tensor
        def _(pe):
            def project(use, b=None):
                ring = first if b is None else body
                bank = ring.bank[use]
                out_bank = general_psum[:, bank, :]
                if b is not None:
                    pe.wait_ge(emptied[bank], b * body.turns[0] + (first.turns[0] + body.turn[use]))
                elif first.turn[use]:
                    pe.wait_ge(emptied[bank], first.turn[use])
                kind = use[0]
                if kind == "xt":
                    i = use[1]
                    pe.wait_ge(norm_done, (i + 1) if b is None else b * ST + (ST + i + 1))
                    for k in range(KT):
                        last = nc.tensor.transpose(out_bank[:, k * P:(k + 1) * P], xn[:, i % 2, k * P:(k + 1) * P],
                                                   ident[:])
                elif kind == "qk":
                    _, p, n = use
                    w = wq if n < 2 else wk
                    for k in range(KT):
                        last = nc.tensor.matmul(out_bank, w[:, k, p * P:(p + 1) * P],
                                                xnT[:, k, n % 2 * NC:(n % 2 + 1) * NC], start=k == 0,
                                                stop=k == KT - 1)
                elif kind == "v":
                    i = use[1]
                    for k in range(KT):
                        last = nc.tensor.matmul(out_bank, xnT[:, k, i * P:(i + 1) * P], wv[:, k, :], start=k == 0,
                                                stop=k == KT - 1)
                elif kind == "pv":
                    c = use[1]
                    p, _ = place(c)
                    g = c * PV_UNITS + PV_UNITS - 1
                    pe.wait_ge(copied_low, b * UNITS + (1 + g + 1))
                    pe.wait_ge(copied_high, b * UNITS + (1 + g + 1))
                    for t in range(ST):
                        for h in range(2):
                            nc.tensor.matmul(out_bank[h * HD:(h + 1) * HD, 0:PV_TOKENS],
                                             v[:, t, p * P + h * HD:p * P + (h + 1) * HD],
                                             probsT[:, c % 2, t, h, :], start=t == 0, stop=t == ST - 1)
                    pe.wait_ge(recip_ready, b * PV_CHUNKS + (c + 1))
                    for m in range(PV_UNITS // 2):
                        last = nc.tensor.transpose(out_bank[:, PV_TOKENS + m * P:PV_TOKENS + (m + 1) * P],
                                                   recip_wide[:, c % 2, 2 * m:2 * m + 2, :].rearrange(
                                                       "p u d -> p (u d)"), ident[:])
                elif kind == "wo":
                    i = use[1]
                    if i == 0:
                        feats = ("pv", PV_CHUNKS - 1)
                        pe.wait_ge(emptied[body.bank[feats]], empty(feats, b))
                    for p in range(PAIRS):
                        last = nc.tensor.matmul(out_bank, featsT[:, p, i * P:(i + 1) * P], wo[:, p, :],
                                                start=p == 0, stop=p == PAIRS - 1)
                last.then_inc(general_done, 1)

            def scores(g, b):
                p, st, h = unit(g)
                s = p % 2
                if g % PER_PAIR == 0:
                    pe.wait_ge(low_ready, b * low_ops(QK_ROW) + low_ops(4 * (p + 1)))
                pe.wait_ge(exp_done, b * UNITS + (g + 1))
                for n in range(2):
                    for k_part in (k_high, k_low):
                        last = nc.tensor.matmul(score_psum[:, g % 2, n * NC:(n + 1) * NC],
                                                q_parts[s][:, h, st * P:(st + 1) * P],
                                                k_part[s][:, h, n * NC:(n + 1) * NC], start=k_part is k_high,
                                                stop=k_part is k_low)
                last.then_inc(scores_done, 1)

            def transposes(g, b):
                pe.wait_ge(exp_done, b * UNITS + (2 + g + 1))
                for n, copied in enumerate((copied_low, copied_high)):
                    pe.wait_ge(copied, b * UNITS + (g + 1))
                    for k in range(4):
                        t = 4 * n + k
                        last = nc.tensor.transpose(transpose_psum[:, n, k * P:(k + 1) * P],
                                                   probs[:, g % PROBS, t * P:(t + 1) * P], ident[:])
                    last.then_inc(transposed, 1)

            pe.sem_inc(transposed, 2 * PROBS)
            for i in range(ST):
                project(("xt", i))
            pe.wait_ge(emptied[first.bank["xt", ST - 1]], empty(("xt", ST - 1)))
            pe.wait_ge(wqk_loaded, 32)
            for n in range(4):
                project(("qk", 0, n))
            pe.wait_ge(wv_loaded, 32)
            pe.wait_ge(wo_loaded, 32)
            with pe.Fori(0, BATCH) as b:
                for g in range(UNITS + LAG):
                    if g < UNITS:
                        scores(g, b)
                        for use in filler[g]:
                            if use == ("qk", 0, 0):
                                rows = ("xt", ST - 1)
                                pe.wait_ge(emptied[body.bank[rows]], empty(rows, b))
                            project(use, b)
                    if g >= LAG:
                        transposes(g - LAG, b)
                for use in tail:
                    project(use, b)


def ffn_uses():
    gate_up = lambda i: [("gate_up", i, n) for n in range(2 * GROUPS)]
    down = lambda i: [("down", i, j) for j in range(KT)]
    transposed = [("xt", r) for r in range(CT)]
    back = [("y", r) for r in range(CT)]
    first = transposed + [u for i in range(AHEAD) for u in gate_up(i)]
    shared = down(0) + [u for i in range(AHEAD, FI - 1) for u in gate_up(i) + down(i - 2)] + gate_up(FI - 1)
    body = (shared + transposed + down(FI - 3) + down(FI - 2) + gate_up(0) + down(FI - 1) + gate_up(1) + back
            + gate_up(2))
    last = shared + down(FI - 3) + down(FI - 2) + down(FI - 1) + back
    return first, body, last


def build_ffn(nc, x1_scratch, ffn_values, ident, consts_of, minus_half, out):
    f32, f32r = mybir.dt.float32, mybir.dt.float32r
    ALU, ACT, AX = mybir.AluOpType, mybir.ActivationFunctionType, mybir.AxisListType
    BANKS = 8
    first_uses, body_uses, last_uses = ffn_uses()
    first, body, last_ring = Ring(first_uses, BANKS), Ring(body_uses, BANKS), Ring(last_uses, BANKS)
    BODIES = CHUNKS - 1
    SLOTS = 3
    LN_TILE = 5
    out_tiles = out.rearrange("b (t p) f -> (b t) p f", p=P)

    ctx = ExitStack()
    with ctx:
        sb = lambda name, shape, dt=f32: ctx.enter_context(nc.sbuf_tensor(name, shape, dt))
        sem = lambda name: ctx.enter_context(nc.semaphore(name))
        w = sb("w", [P, FI, 3 * KT, P], f32r)
        x1 = sb("x1", [P, CT, F])
        residual = sb("residual2", [P, 2, F])
        stats = sb("stats2", [P, CT, 6])
        mean_var = sb("mean_var2", [P, CT, 2])
        var_eps = sb("var_eps2", [P, CT])
        rstd = sb("rstd2", [P, CT])
        shift = sb("shift2", [P, CT])
        xn = sb("xn2", [P, CT, F])
        x_high = sb("x_high", [P, KT, NC], f32r)
        x_low = sb("x_low", [P, KT, NC], f32r)
        part = sb("part", [P, SLOTS, 4, NC])
        gate_up_sum = sb("gate_up_sum", [P, SLOTS, 2, NC])
        silu = sb("silu", [P, SLOTS, NC])
        h = sb("h", [P, SLOTS, NC])
        h_high = sb("h_high", [P, SLOTS, NC], f32r)
        h_low = sb("h_low", [P, SLOTS, NC], f32r)
        down_part = sb("down_part", [P, SLOTS, 2, NC])
        yT = sb("yT", [P, KT, NC])
        y = sb("y", [P, CT, F])
        square = sb("square", [P, F])
        square_sum = sb("square_sum", [P, CT])
        mean_square = sb("mean_square", [P, CT])
        inv_rms = sb("inv_rms", [P, CT])
        out_tile = sb("out_tile", [P, 2, F])
        psum = ctx.enter_context(nc.psum_tensor("ffn_psum", [P, BANKS, NC], f32))

        w_loaded = [sem(f"w_loaded{i}") for i in range(FI)]
        x1_loaded = sem("x1_loaded")
        residual_loaded = [sem(f"residual2_loaded{n}") for n in range(2)]
        stats_done, stats_seen = sem("stats_done2"), sem("stats_seen2")
        aggregated = sem("aggregated2")
        var_ready = sem("var_ready2")
        rstd_ready = sem("rstd_ready2")
        shift_ready = sem("shift_ready2")
        norm_done = sem("norm_done2")
        products_done = sem("products_done")
        emptied = [sem(f"bank_emptied{n}") for n in range(BANKS)]
        x_high_ready = sem("x_high_ready")
        gate_sum_ready = sem("gate_sum_ready")
        up_sum_ready = sem("up_sum_ready")
        silu_ready = sem("silu_ready")
        h_ready = sem("h_ready")
        h_high_ready = sem("h_high_ready")
        h_low_ready = sem("h_low_ready")
        odd_added = sem("odd_added")
        square_ready = sem("square_ready")
        mean_ready = sem("mean_ready")
        inv_rms_ready = sem("inv_rms_ready")
        out_ready = sem("out_ready")
        out_slots_free = sem("out_slots_free")
        out_stored = [sem(f"out_stored{n}") for n in range(2)]
        block = ctx.enter_context(nc.Block(name="ffn"))

        def tile_at(ap, n):
            return ap[bass.ds(n, 1)].rearrange("a p f -> (a p) f")

        class Phase:

            def __init__(self, c, ring, chunk):
                self.c, self.ring, self.chunk = c, ring, chunk

            def bank(self, use):
                return self.ring.bank[use]

            def done(self, use):
                return self.total(body.total, first.total) + self.ring.number[use] + 1

            def turn(self, use):
                bank = self.ring.bank[use]
                return self.total(body.turns[bank], first.turns[bank]) + self.ring.turn[use]

            def total(self, per_body, before):
                if self.ring is first:
                    return 0
                return self.chunk * per_body + before

            def tile(self, use):
                kind, i = use[0], use[1]
                if self.ring is first:
                    return i
                own = self.chunk * FI + i
                return own + FI if kind == "gate_up" and i < AHEAD and self.ring is body else own

        def phases(eng, program):
            program(Phase(None, first, 0), first_uses)
            with eng.Fori(0, BODIES) as c:
                program(Phase(c, body, c), body_uses)
            program(Phase(None, last_ring, BODIES), last_uses)


        def emptied_value(ph, use):
            return ph.turn(use) + 1

        def xt_chunk(ph):
            return ph.chunk + 1 if ph.ring is body else ph.chunk

        def freed(i, count):
            back = 2 if i <= 2 else SLOTS
            return None if isinstance(count, int) and count < back else count - (back - 1)

        def wait_freed(eng, semaphore, i, count):
            value = freed(i, count)
            if value is not None:
                eng.wait_ge(semaphore, value)

        def group_scale(use):
            _, i, n = use
            return consts_of["gu"](n % GROUPS, i + FI * (n // GROUPS))

        @block.sync
        def _(sp):
            x1_chunks = x1_scratch.rearrange("(c r) p f -> c p r f", r=CT)
            sp.dma_start(x1[:], x1_chunks[0]).then_inc(x1_loaded, 16)
            for i in range(FI):
                sp.dma_start(w[:, i].rearrange("p k n -> p (k n)").bitcast(f32),
                             ffn_values[i]).then_inc(w_loaded[i], 16)

            def finish_chunk(ph):
                for r in range(2):
                    sp.dma_start(residual[:, r, :], tile_at(x1_scratch, ph.chunk * CT + r)
                                 ).then_inc(residual_loaded[r], 16)
                for r in range(CT):
                    sp.wait_ge(out_ready, ph.chunk * CT + (r + 1))
                    sp.dma_start(tile_at(out_tiles, ph.chunk * CT + r), out_tile[:, r % 2, :]
                                 ).then_inc(out_stored[r % 2], 16)
                    if r + 2 < CT:
                        sp.dma_start(residual[:, r % 2, :], tile_at(x1_scratch, ph.chunk * CT + (r + 2))
                                     ).then_inc(residual_loaded[r % 2], 16)
                for n in range(2):
                    sp.wait_ge(out_stored[n], ph.chunk * (8 * CT) + 8 * CT)
                sp.sem_inc(out_slots_free, 1)

            sp.sem_inc(out_slots_free, 1)
            with sp.Fori(0, BODIES) as c:
                sp.wait_ge(norm_done, c * CT + CT)
                sp.dma_start(x1[:], x1_chunks[bass.ds(c + 1, 1)].rearrange("a p r f -> (a p) r f")
                             ).then_inc(x1_loaded, 16)
                finish_chunk(Phase(c, body, c))
            finish_chunk(Phase(None, last_ring, BODIES))

        @block.gpsimd
        def _(pool):
            def program(ph, uses):
                for use in uses:
                    kind = use[0]
                    if kind == "gate_up":
                        _, i, n = use
                        s, which = i % SLOTS, n // GROUPS
                        if n % GROUPS == GROUPS - 1:
                            tile = ph.tile(use)
                            pool.wait_ge(emptied[ph.bank(use)], emptied_value(ph, use))
                            wait_freed(pool, (silu_ready, h_ready)[which], i, tile)
                            nc.gpsimd.tensor_tensor(gate_up_sum[:, s, which, :], part[:, s, 2 * which, :],
                                                    part[:, s, 2 * which + 1, :], ALU.add
                                                    ).then_inc((gate_sum_ready, up_sum_ready)[which], 1)
                        if ph.ring is body and n == 0 and i == LN_TILE + 1:
                            inverse_std(xt_chunk(ph))
                        if ph.ring is body and i == AHEAD - 1 and n == 2:
                            inverse_rms(ph.chunk)
                    elif kind == "down":
                        _, i, j = use
                        if i and j % 2:
                            before = ph.chunk * (2 * (FI - 1)) + 2 * (i - 1) + j // 2
                            pool.wait_ge(emptied[ph.bank(use)], emptied_value(ph, use))
                            if i == 1:
                                own = ("down", 0, j)
                                pool.wait_ge(emptied[ph.bank(own)], emptied_value(ph, own))
                            else:
                                pool.wait_ge(odd_added, before - 1)
                            nc.gpsimd.tensor_tensor(yT[:, j, :], yT[:, j, :], down_part[:, i % SLOTS, j // 2, :],
                                                    ALU.add).then_inc(odd_added, 1)
                if ph.ring is last_ring:
                    inverse_rms(ph.chunk)

            def inverse_rms(chunk):
                pool.wait_ge(mean_ready, chunk + 1)
                nc.gpsimd.tensor_tensor(inv_rms[:], mean_square[:], minus_half[:, 0:CT], ALU.pow
                                        ).then_inc(inv_rms_ready, 1)

            def inverse_std(chunk):
                pool.wait_ge(var_ready, chunk + 1)
                nc.gpsimd.tensor_tensor(rstd[:], var_eps[:], minus_half[:, 0:CT], ALU.pow).then_inc(rstd_ready, 1)

            inverse_std(0)
            phases(pool, program)

        @block.scalar
        def _(act):
            def program(ph, uses):
                for use in uses:
                    kind, bank = use[0], ph.bank(use)
                    if kind == "gate_up":
                        _, i, n = use
                        s = i % SLOTS
                        if n % 2 == 0:
                            wait_freed(act, gate_sum_ready if n < GROUPS else up_sum_ready, i, ph.tile(use))
                            act.wait_ge(products_done, ph.done(use))
                            nc.scalar.activation(part[:, s, n // 2, :], psum[:, bank, :], ACT.Copy,
                                                 scale=group_scale(use)).then_inc(emptied[bank], 1)
                        if n == 2 * GROUPS - 2 and not (ph.ring is first and i == 0):
                            round_h(i - 1 if i else FI - 1, ph.tile(use) - 1)
                        if n == 2 * GROUPS - 1 and ph.ring is body and i == LN_TILE + 3:
                            normalise(xt_chunk(ph))
                        if n == 2 * GROUPS - 1:
                            act.wait_ge(gate_sum_ready, ph.tile(use) + 1)
                            nc.scalar.activation(silu[:, s, :], gate_up_sum[:, s, 0, :],
                                                 ACT.Silu).then_inc(silu_ready, 1)
                            if ph.ring is last_ring and i == FI - 1:
                                round_h(i, ph.tile(use))
                    elif kind == "down":
                        _, i, j = use
                        if j % 2:
                            target = down_part[:, i % SLOTS, j // 2, :] if i else yT[:, j, :]
                            if i > SLOTS:
                                act.wait_ge(odd_added, ph.chunk * (2 * (FI - 1)) + 2 * (i - SLOTS))
                            act.wait_ge(products_done, ph.done(use))
                            nc.scalar.activation(target, psum[:, bank, :], ACT.Copy,
                                                 scale=consts_of["down"](i, j)).then_inc(emptied[bank], 1)
                    elif kind == "xt":
                        r = use[1]
                        act.wait_ge(products_done, ph.done(use))
                        nc.scalar.activation(x_high[:, :, r * P:(r + 1) * P], psum[:, bank, :].rearrange(
                            "p (k t) -> p k t", k=KT), ACT.Copy).then_inc(x_high_ready, 1)
                    elif kind == "y":
                        r = use[1]
                        act.wait_ge(products_done, ph.done(use))
                        nc.scalar.activation(y[:, r, :], psum[:, bank, :], ACT.Copy).then_inc(emptied[bank], 1)
                        if r == CT - 1:
                            for m in range(CT):
                                before = ("y", m)
                                act.wait_ge(emptied[ph.bank(before)], emptied_value(ph, before))
                                if m or ph.ring is last_ring:
                                    act.wait_ge(square_ready, ph.chunk * CT + m)
                                nc.scalar.activation(square[:], y[:, m, :], ACT.Square, scale=F ** -0.5,
                                                     accum_out=square_sum[:, m:m + 1]).then_inc(square_ready, 1)

            def normalise(chunk):
                act.wait_ge(shift_ready, chunk + 1)
                for r in range(CT):
                    nc.scalar.activation(xn[:, r, :], x1[:, r, :], ACT.Identity, bias=shift[:, r:r + 1],
                                         scale=rstd[:, r:r + 1]).then_inc(norm_done, 1)

            def round_h(i, tile):
                act.wait_ge(h_ready, tile + 1)
                nc.scalar.activation(h_high[:, i % SLOTS, :], h[:, i % SLOTS, :],
                                     ACT.Copy).then_inc(h_high_ready, 1)

            normalise(0)
            phases(act, program)

        @block.vector
        def _(dve):
            def multiply_h(i, tile):
                dve.wait_ge(silu_ready, tile + 1)
                dve.wait_ge(up_sum_ready, tile + 1)
                nc.vector.tensor_tensor(h[:, i % SLOTS, :], silu[:, i % SLOTS, :], gate_up_sum[:, i % SLOTS, 1, :],
                                        ALU.mult).then_inc(h_ready, 1)

            def low_h(i, tile):
                dve.wait_ge(h_high_ready, tile + 1)
                nc.vector.tensor_tensor(h_low[:, i % SLOTS, :], h[:, i % SLOTS, :],
                                        h_high[:, i % SLOTS, :].bitcast(f32), ALU.subtract
                                        ).then_inc(h_low_ready, 1)

            def chunk_stats(chunk):
                dve.wait_ge(x1_loaded, chunk * 16 + 16)
                for r in range(CT):
                    nc.vector.bn_stats(stats[:, r, :], x1[:, r, :]).then_inc(stats_done, 1)
                for r in range(CT):
                    dve.wait_ge(stats_done, chunk * CT + (r + 1))
                    dve.sem_inc(stats_seen, 1)
                    nc.vector.bn_aggr(mean_var[:, r, :], stats[:, r, :]).then_inc(aggregated, 1)
                dve.wait_ge(aggregated, chunk * CT + CT)
                nc.vector.tensor_scalar(var_eps[:], mean_var[:, :, 1], LN_EPS, None, ALU.add
                                        ).then_inc(var_ready, 1)

            def chunk_shift(chunk):
                dve.wait_ge(rstd_ready, chunk + 1)
                nc.vector.scalar_tensor_tensor(shift[:], mean_var[:, :, 0], -1.0, rstd[:], ALU.mult,
                                               ALU.mult).then_inc(shift_ready, 1)

            def add_eps(chunk):
                dve.wait_ge(square_ready, chunk * CT + CT)
                nc.vector.tensor_scalar(mean_square[:], square_sum[:], RMS_EPS, None, ALU.add
                                        ).then_inc(mean_ready, 1)

            def finish(chunk):
                dve.wait_ge(inv_rms_ready, chunk + 1)
                for r in range(CT):
                    dve.wait_ge(residual_loaded[r % 2], chunk * (8 * CT) + 16 * (r // 2 + 1))
                    if r < 2:
                        dve.wait_ge(out_slots_free, chunk + 1)
                    else:
                        dve.wait_ge(out_stored[r % 2], chunk * (8 * CT) + 16 * (r // 2))
                    nc.vector.scalar_tensor_tensor(out_tile[:, r % 2, :], y[:, r, :], inv_rms[:, r:r + 1],
                                                   residual[:, r % 2, :], ALU.mult, ALU.add).then_inc(out_ready, 1)

            def program(ph, uses):
                for use in uses:
                    kind, bank = use[0], ph.bank(use)
                    if kind == "gate_up":
                        _, i, n = use
                        s = i % SLOTS
                        not_first = not (ph.ring is first and i == 0)
                        before, tile = (i - 1 if i else FI - 1), ph.tile(use)
                        if n % 2:
                            pair = ("gate_up", i, n - 1)
                            dve.wait_ge(emptied[ph.bank(pair)], emptied_value(ph, pair))
                            dve.wait_ge(products_done, ph.done(use))
                            nc.vector.scalar_tensor_tensor(part[:, s, n // 2, :], psum[:, bank, :],
                                                           group_scale(use), part[:, s, n // 2, :], ALU.mult,
                                                           ALU.add).then_inc(emptied[bank], 1)
                        if n == GROUPS - 1 and not_first:
                            multiply_h(before, tile - 1)
                        if ph.ring is body and n == 2 and i == AHEAD - 1:
                            add_eps(ph.chunk)
                        if n == 2 * GROUPS - 1:
                            if not_first and (i < AHEAD or i == FI - 1):
                                low_h(before, tile - 1)
                            if ph.ring is last_ring and i == FI - 1:
                                multiply_h(i, tile)
                                low_h(i, tile)
                            if ph.ring is body and i == LN_TILE:
                                chunk_stats(xt_chunk(ph))
                            if ph.ring is body and i == LN_TILE + 2:
                                chunk_shift(xt_chunk(ph))
                            if ph.ring is body and i == AHEAD - 1:
                                finish(ph.chunk)
                    elif kind == "down":
                        _, i, j = use
                        if j % 2 == 0:
                            scale = consts_of["down"](i, j)
                            dve.wait_ge(products_done, ph.done(use))
                            if i == 0:
                                op = nc.vector.tensor_scalar(yT[:, j, :], psum[:, bank, :], scale, None, ALU.mult)
                            else:
                                own = ("down", i - 1, j)
                                dve.wait_ge(emptied[ph.bank(own)], emptied_value(ph, own))
                                op = nc.vector.scalar_tensor_tensor(yT[:, j, :], psum[:, bank, :], scale,
                                                                    yT[:, j, :], ALU.mult, ALU.add)
                            op.then_inc(emptied[bank], 1)
                            if j == KT - 2 and AHEAD - 2 <= i < FI - 3:
                                low_h(i + 1, ph.chunk * FI + (i + 1))
                    elif kind == "xt":
                        r = use[1]
                        dve.wait_ge(x_high_ready, xt_chunk(ph) * CT + (r + 1))
                        tok = slice(r * P, (r + 1) * P)
                        nc.vector.tensor_tensor(x_low[:, :, tok], psum[:, bank, :].rearrange(
                            "p (k t) -> p k t", k=KT), x_high[:, :, tok].bitcast(f32), ALU.subtract
                            ).then_inc(emptied[bank], 1)
                if ph.ring is last_ring:
                    add_eps(ph.chunk)
                    finish(ph.chunk)

            chunk_stats(0)
            chunk_shift(0)
            phases(dve, program)

        @block.tensor
        def _(pe):
            def program(ph, uses):
                for use in uses:
                    kind, bank = use[0], ph.bank(use)
                    if not (ph.ring is first and first.turn[use] == 0):
                        pe.wait_ge(emptied[bank], ph.turn(use))
                    if kind == "gate_up":
                        _, i, n = use
                        which, k = n // GROUPS, n % GROUPS
                        if n == 0 and i == 0:
                            for r in range(CT):
                                xt = ("xt", r)
                                pe.wait_ge(emptied[ph.bank(xt)], emptied_value(ph, xt))
                        if n == 0 and not (ph.ring is body and i < AHEAD):
                            pe.wait_ge(w_loaded[i], 16)
                        for moving in (x_high, x_low):
                            last = nc.tensor.matmul(psum[:, bank, :], w[:, i, which * KT + k, :], moving[:, k, :],
                                                    start=moving is x_high, stop=moving is x_low)
                    elif kind == "down":
                        _, i, j = use
                        if j == 0:
                            pe.wait_ge(h_low_ready, ph.chunk * FI + (i + 1))
                        for moving in (h_high, h_low):
                            last = nc.tensor.matmul(psum[:, bank, :], w[:, i, 2 * KT + j, :],
                                                    moving[:, i % SLOTS, :], start=moving is h_high,
                                                    stop=moving is h_low)
                    elif kind == "xt":
                        r = use[1]
                        pe.wait_ge(norm_done, xt_chunk(ph) * CT + (r + 1))
                        for k in range(KT):
                            last = nc.tensor.transpose(psum[:, bank, k * P:(k + 1) * P],
                                                       xn[:, r, k * P:(k + 1) * P], ident[:])
                    elif kind == "y":
                        r = use[1]
                        if r == 0:
                            for j in range(0, KT, 2):
                                own = ("down", FI - 1, j)
                                pe.wait_ge(emptied[ph.bank(own)], emptied_value(ph, own))
                            pe.wait_ge(odd_added, ph.chunk * (2 * (FI - 1)) + 2 * (FI - 1))
                        for j in range(KT):
                            last = nc.tensor.transpose(psum[:, bank, j * P:(j + 1) * P],
                                                       yT[:, j, r * P:(r + 1) * P], ident[:])
                    last.then_inc(products_done, 1)

            phases(pe, program)


_OUTS = [((BATCH, SEQ, F), "float32")]
_INS = ["L0_attn_x", "L0_attn_Wq", "L0_attn_bq", "L0_attn_Wk", "L0_attn_bk", "L0_attn_Wv", "L0_attn_bv", "L0_attn_Wo",
        "L0_attn_bo", "L0_ffn_gate_up_packed", "L0_ffn_gate_up_scales", "L0_ffn_down_packed", "L0_ffn_down_scales"]


def kernel(**inputs):
    import numpy as _np
    import concourse.bacc as _bacc
    from concourse import mybir as _mybir
    from concourse.bass_utils import run_bass_kernel_spmd as _run

    nc = _bacc.Bacc("TRN2", target_bir_lowering=False, num_devices=1)
    arrays, args = {}, []
    for name in _INS:
        a = _np.ascontiguousarray(inputs[name])
        arrays[f"in_{name}_dram"] = a
        args.append(nc.dram_tensor(f"in_{name}_dram", a.shape, _mybir.dt.from_np(a.dtype), kind="ExternalInput").ap())
    for i, (shape, dtype) in enumerate(_OUTS):
        dt = _mybir.dt.from_np(_np.dtype(dtype))
        args.append(nc.dram_tensor(f"out_{i}_dram", shape, dt, kind="ExternalOutput").ap())
    build(nc, *args)
    r = _run(nc, [arrays], core_ids=[0])
    return r.results[0]["out_0_dram"]
```

```python
from contextlib import ExitStack

import numpy as np

import concourse.bass as bass
from concourse import mybir

P = 128
BATCH, SEQ, F = 4, 1024, 512
HEADS, HD = 8, 64
PAIRS = HEADS // 2
KT = F // P
ST = SEQ // P
NC = 512
FFN = 1408
FI = FFN // P
GROUPS = F // P
NIB = 8
LN_EPS, RMS_EPS = 1e-5, 1e-6
SCORE_SCALE = HEADS ** -0.5
UNITS = PAIRS * ST * 2
PV_UNITS = 4
LAG = 2
CHUNKS = BATCH * SEQ // NC
CT = NC // P
EARLY_V = 2
AHEAD = 9

LATE_DOWN = AHEAD - 3


def on_gpsimd(j):
    return j % 2 == 1


class Ring:

    def __init__(self, uses, banks):
        self.number = {u: n for n, u in enumerate(uses)}
        self.bank = {u: n % banks for n, u in enumerate(uses)}
        self.turn = {u: n // banks for n, u in enumerate(uses)}
        self.total = len(uses)
        self.turns = [len(uses[k::banks]) for k in range(banks)]


def attention_schedule():
    filler = {g: [] for g in range(UNITS)}
    for i in range(EARLY_V, ST):
        filler[i - EARLY_V].append(("v", i))
    for c in range(UNITS // PV_UNITS - 1):
        filler[PV_UNITS * c + PV_UNITS + LAG + 1].append(("pv", c))
    per_pair = UNITS // PAIRS
    for p in range(PAIRS):
        for n, u in enumerate((1, 5, 9, 12) if 0 < p < PAIRS - 1 else (5, 8, 10, 13)):
            filler[per_pair * p + u].append(("qk", (p + 1) % PAIRS, n))
    for i in range(ST):
        filler[per_pair * (PAIRS - 1) - ST // 2 + 1 + i].insert(0, ("xt", i))
    tail = [("pv", UNITS // PV_UNITS - 1)]
    for i in range(ST + 2):
        tail.append(("wo", i) if i < ST else ("v", i - ST))
        if i >= 2:
            tail.append(("x1t", i - 2))
    return filler, tail


def stats_unit(i):
    return UNITS // PAIRS * (PAIRS - 1) - ST // 2 + 1 + i - 2


def build(nc, x, Wq, bq, Wk, bk, Wv, bv, Wo, bo, gu_packed, gu_scales, d_packed, d_scales, out):
    f32, f32r, i32, f16 = mybir.dt.float32, mybir.dt.float32r, mybir.dt.int32, mybir.dt.float16
    ctx = ExitStack()
    with ctx:
        ffn_values = nc.dram_tensor("ffn_values", (FI, P, 3 * F), f32, kind="Internal").ap()
        x1_scratch = nc.dram_tensor("x1_scratch", (BATCH * ST, P, F), f32, kind="Internal").ap()
        x_parts_scratch = nc.dram_tensor("x_parts_scratch", (CHUNKS, P, 2, KT, NC), f32, kind="Internal").ap()
        ident = ctx.enter_context(nc.sbuf_tensor("ident", [P, P], f32))
        consts = ctx.enter_context(nc.sbuf_tensor("consts", [P, 2 * P], f32))
        bq_scaled = ctx.enter_context(nc.sbuf_tensor("bq_scaled", [P, PAIRS], f32))
        minus_half = ctx.enter_context(nc.sbuf_tensor("minus_half", [P, 4], f32))
        consts_of = {
            "gu": lambda g, t: consts[:, g * 2 * FI + t:g * 2 * FI + t + 1],
            "down": lambda i, j: consts[:, P + i * KT + j:P + i * KT + j + 1],
            "bk": lambda p: consts[:, P + 96 + p:P + 97 + p],
            "bq": consts[:, P + 64:P + 64 + PAIRS],
        }
        build_prep(nc, gu_packed, gu_scales, d_packed, d_scales, bq, bk, ident, consts, consts_of, bq_scaled,
                   minus_half, ffn_values)
        build_attention(nc, x, Wq, Wk, Wv, bv, Wo, bo, ident, consts_of, bq_scaled, minus_half, x1_scratch,
                        x_parts_scratch)
        build_ffn(nc, x1_scratch, x_parts_scratch, ffn_values, ident, consts_of, minus_half, out)


def build_prep(nc, gu_packed, gu_scales, d_packed, d_scales, bq, bk, ident, consts, consts_of, bq_scaled,
               minus_half, ffn_values):
    f32, i32, f16 = mybir.dt.float32, mybir.dt.int32, mybir.dt.float16
    ALU, ACT = mybir.AluOpType, mybir.ActivationFunctionType
    GW, DW = F // NIB, FFN // NIB
    WORDS = 2 * FI * GW + KT * DW
    HALF_TILES = 16
    SPANS = [(0, HALF_TILES * GW), (HALF_TILES * GW, WORDS)]
    SPAN = max(b - a for a, b in SPANS)
    STEPS = [(s, j) for s in range(len(SPANS)) for j in range(NIB)]
    TILES = [("gu", t) for t in range(2 * FI)] + [("down", i) for i in range(FI)]
    BANKS = 8
    ring = Ring(TILES, BANKS)

    ctx = ExitStack()
    with ctx:
        sb = lambda name, shape, dt: ctx.enter_context(nc.sbuf_tensor(name, shape, dt))
        sem = lambda name: ctx.enter_context(nc.semaphore(name))
        packed = sb("packed", [P, WORDS], i32)
        values = sb("values", [P, WORDS * NIB], f32)
        stage = sb("stage", [P, FI, 3 * F], f32)
        mag = sb("mag", [P, 2, SPAN], i32)
        sign = sb("sign", [P, 2, SPAN], i32)
        over4 = sb("over4", [P, 2, SPAN], f32)
        over6 = sb("over6", [P, 2, SPAN], f32)
        half = sb("half", [P, 2, SPAN], f32)
        twice = sb("twice", [P, 2, SPAN], f32)
        scales16 = sb("scales16", [P, 2, P], f16)
        rows = sb("rows", [P, 2, P], f32)
        psum = ctx.enter_context(nc.psum_tensor("prep_psum", [P, BANKS, NC], f32))

        packed_loaded = [sem(f"packed_loaded{n}") for n in range(2)]
        scales_loaded = sem("scales_loaded")
        biases_loaded = sem("biases_loaded")
        rows_zeroed = sem("rows_zeroed")
        rows_cast = sem("rows_cast")
        ident_zeroed = sem("ident_zeroed")
        ident_ready = sem("ident_ready")
        consts_transposed = sem("consts_transposed")
        consts_ready = sem("consts_ready")
        codes_ready = sem("codes_ready")
        terms_ready = sem("terms_ready")
        mag_over4_ready = sem("mag_over4_ready")
        sum_ready = sem("sum_ready")
        first_sum_ready = sem("first_sum_ready")
        values_done = sem("values_done")
        tiles_transposed = sem("tiles_transposed")
        tile_staged = [sem(f"tile_staged{k}") for k in range(BANKS)]
        values_stored = sem("values_stored")
        block = ctx.enter_context(nc.Block(name="prep"))

        def nibble_view(span, j):
            a, b = SPANS[span]
            return values[:, a * NIB:b * NIB].rearrange("p (w j) -> p w j", j=NIB)[:, :, j]

        def staged(kind, n):
            if kind == "down":
                return stage[:, n, 2 * F:3 * F]
            return stage[:, n % FI, (n // FI) * F:(n // FI) * F + F]

        @block.sync
        def _(sp):
            gu_rows = gu_packed.rearrange("(t p) w -> p t w", p=P)
            sp.dma_start(packed[:, 0:SPANS[0][1]].rearrange("p (t w) -> p t w", w=GW),
                         gu_rows[:, 0:HALF_TILES, :]).then_inc(packed_loaded[0], 16)
            sp.dma_start(packed[:, SPANS[0][1]:2 * FI * GW].rearrange("p (t w) -> p t w", w=GW),
                         gu_rows[:, HALF_TILES:, :]).then_inc(packed_loaded[1], 16)
            sp.dma_start(packed[:, 2 * FI * GW:].rearrange("p (t w) -> p t w", w=DW),
                         d_packed.rearrange("(t p) w -> p t w", p=P)).then_inc(packed_loaded[1], 16)
            sp.dma_start(scales16[0:GROUPS * 2 * FI, 0, :],
                         gu_scales.rearrange("g (t p) -> (g t) p", p=P)).then_inc(scales_loaded, 16)
            sp.dma_start(scales16[0:FI * KT, 1, :],
                         d_scales.rearrange("g (t p) -> (g t) p", p=P)).then_inc(scales_loaded, 16)
            sp.wait_ge(rows_zeroed, 1)
            sp.dma_start(rows[64:64 + PAIRS, 1, :], bq.rearrange("(t p) -> t p", p=P)).then_inc(biases_loaded, 16)
            sp.dma_start(rows[96:96 + PAIRS, 1, :], bk.rearrange("(t p) -> t p", p=P)).then_inc(biases_loaded, 16)
            for use in TILES:
                kind, t = use
                i, third = (t, 2) if kind == "down" else (t % FI, t // FI)
                sp.wait_ge(tile_staged[ring.bank[use]], ring.turn[use] + 1)
                sp.dma_start(ffn_values[i][:, third * F:(third + 1) * F], staged(*use)).then_inc(values_stored, 16)
            sp.wait_ge(values_stored, 16 * len(TILES))

        @block.gpsimd
        def _(pool):
            nc.gpsimd.memset(minus_half[:], -0.5)
            nc.gpsimd.memset(ident[:], 0.0).then_inc(ident_zeroed, 1)
            pool.wait_ge(ident_zeroed, 1)
            nc.gpsimd.affine_select(out=ident[:], in_=ident[:], compare_op=ALU.not_equal, fill=1.0, base=0,
                                    pattern=[[-1, P]], channel_multiplier=1).then_inc(ident_ready, 1)
            for k, (span, j) in enumerate(STEPS):
                n = SPANS[span][1] - SPANS[span][0]
                pool.wait_ge(terms_ready, k + 1)
                pool.wait_ge(first_sum_ready, k + 1)
                nc.gpsimd.tensor_tensor(twice[:, k % 2, 0:n], twice[:, k % 2, 0:n], over6[:, k % 2, 0:n],
                                        ALU.add).then_inc(sum_ready, 1)

        @block.scalar
        def _(act):
            for k, (span, j) in enumerate(STEPS):
                n = SPANS[span][1] - SPANS[span][0]
                act.wait_ge(codes_ready, k + 1)
                if k >= 2:
                    act.wait_ge(values_done, k - 1)
                s = k % 2
                nc.scalar.activation(over4[:, s, 0:n], mag[:, s, 0:n], ACT.Relu, bias=-4.0).then_inc(mag_over4_ready, 1)
                nc.scalar.activation(over6[:, s, 0:n], mag[:, s, 0:n], ACT.Relu, bias=-12.0, scale=2.0)
                nc.scalar.activation(half[:, s, 0:n], sign[:, s, 0:n], ACT.Copy, bias=0.5,
                                     scale=-0.125).then_inc(terms_ready, 1)
            for n, use in enumerate(TILES):
                if n % 2 == 0:
                    act.wait_ge(tiles_transposed, n + 1)
                    nc.scalar.activation(staged(*use), psum[:, ring.bank[use], :],
                                         ACT.Copy).then_inc(tile_staged[ring.bank[use]], 1)

        @block.vector
        def _(dve):
            def codes(k):
                span, j = STEPS[k]
                a, b = SPANS[span]
                if j == 0:
                    dve.wait_ge(packed_loaded[span], 16 if span == 0 else 32)
                nc.vector.tensor_scalar(mag[:, k % 2, 0:b - a], packed[:, a:b], 4 * j, 7,
                                        ALU.logical_shift_right, ALU.bitwise_and)
                nc.vector.tensor_scalar(sign[:, k % 2, 0:b - a], packed[:, a:b], 4 * j, 8,
                                        ALU.logical_shift_right, ALU.bitwise_and).then_inc(codes_ready, 1)

            nc.vector.memset(rows[:], 0.0).then_inc(rows_zeroed, 1)
            dve.wait_ge(scales_loaded, 32)
            dve.wait_ge(rows_zeroed, 1)
            nc.vector.tensor_copy(rows[0:GROUPS * 2 * FI, 0, :], scales16[0:GROUPS * 2 * FI, 0, :])
            nc.vector.tensor_copy(rows[0:FI * KT, 1, :], scales16[0:FI * KT, 1, :]).then_inc(rows_cast, 1)
            codes(0)
            dve.wait_ge(consts_transposed, 1)
            nc.vector.tensor_copy(consts[:], psum[:, 0, 0:2 * P]).then_inc(consts_ready, 1)
            dve.wait_ge(consts_ready, 1)
            nc.vector.tensor_scalar(bq_scaled[:], consts_of["bq"], SCORE_SCALE, None,
                                    ALU.mult).then_inc(consts_ready, 1)
            for k in range(len(STEPS) + 1):
                if k + 1 < len(STEPS):
                    if k:
                        dve.wait_ge(terms_ready, k)
                        dve.wait_ge(first_sum_ready, k)
                    codes(k + 1)
                if k < len(STEPS):
                    n = SPANS[STEPS[k][0]][1] - SPANS[STEPS[k][0]][0]
                    dve.wait_ge(mag_over4_ready, k + 1)
                    nc.vector.tensor_tensor(twice[:, k % 2, 0:n], mag[:, k % 2, 0:n], over4[:, k % 2, 0:n],
                                            ALU.add).then_inc(first_sum_ready, 1)
                if k:
                    span, j = STEPS[k - 1]
                    n, s = SPANS[span][1] - SPANS[span][0], (k - 1) % 2
                    dve.wait_ge(sum_ready, k)
                    nc.vector.tensor_tensor(nibble_view(span, j), twice[:, s, 0:n], half[:, s, 0:n],
                                            ALU.mult).then_inc(values_done, 1)
            for n, use in enumerate(TILES):
                if n % 2 == 1:
                    dve.wait_ge(tiles_transposed, n + 1)
                    nc.vector.tensor_copy(staged(*use), psum[:, ring.bank[use], :]).then_inc(
                        tile_staged[ring.bank[use]], 1)

        @block.tensor
        def _(pe):
            pe.wait_ge(ident_ready, 1)
            pe.wait_ge(rows_cast, 1)
            pe.wait_ge(biases_loaded, 32)
            nc.tensor.transpose(psum[:, 0, 0:P], rows[:, 0, :], ident[:])
            nc.tensor.transpose(psum[:, 0, P:2 * P], rows[:, 1, :], ident[:]).then_inc(consts_transposed, 1)
            pe.wait_ge(consts_ready, 1)
            for n, (kind, t) in enumerate(TILES):
                if n == 0:
                    pe.wait_ge(values_done, NIB)
                if n == HALF_TILES:
                    pe.wait_ge(values_done, 2 * NIB)
                if ring.turn[kind, t]:
                    pe.wait_ge(tile_staged[ring.bank[kind, t]], ring.turn[kind, t])
                for q in range(4):
                    at = t * F + q * P if kind == "gu" else 2 * FI * F + q * FFN + t * P
                    last = nc.tensor.transpose(psum[:, ring.bank[kind, t], q * P:(q + 1) * P],
                                               values[:, at:at + P], ident[:])
                last.then_inc(tiles_transposed, 1)


def build_attention(nc, x, Wq, Wk, Wv, bv, Wo, bo, ident, consts_of, bq_scaled, minus_half, x1_scratch,
                    x_parts_scratch):
    f32, f32r = mybir.dt.float32, mybir.dt.float32r
    ALU, ACT, AX = mybir.AluOpType, mybir.ActivationFunctionType, mybir.AxisListType
    filler, tail = attention_schedule()
    PER_PAIR = UNITS // PAIRS
    PV_CHUNKS = UNITS // PV_UNITS
    PV_TOKENS = PV_UNITS // 2 * P
    first = Ring([("xt", i) for i in range(ST)] + [("qk", 0, n) for n in range(4)]
                 + [("v", i) for i in range(EARLY_V)], 2)
    body = Ring([u for g in range(UNITS) for u in filler[g]] + tail, 2)
    assert first.total % 2 == 0 and body.total % 2 == 0
    qk_order = {u: n for n, u in enumerate(u for g in range(UNITS) for u in filler[g] if u[0] == "qk")}
    PROBS = 4

    ctx = ExitStack()
    with ctx:
        sb = lambda name, shape, dt=f32: ctx.enter_context(nc.sbuf_tensor(name, shape, dt))
        sem = lambda name: ctx.enter_context(nc.semaphore(name))
        wq, wk, wv, wo = (sb(n, [P, KT, F]) for n in ("wq", "wk", "wv", "wo"))
        bv_rows, bo_rows = sb("bv_rows", [P, F]), sb("bo_rows", [P, F])
        x_in = sb("x_in", [P, 2, F])
        stats = sb("stats", [P, 2, 6])
        mean_var = sb("mean_var", [P, 2, 2])
        var_eps = sb("var_eps", [P, 2, 1])
        rstd = sb("rstd", [P, 2, 1])
        shift = sb("shift", [P, 2, 1])
        xn = sb("xn", [P, 2, F])
        xnT = sb("xnT", [P, KT, SEQ])
        qk_full = sb("qk_full", [P, 2, NC])
        q_parts = [sb(f"q_parts{n}", [P, 2, SEQ], f32r) for n in range(2)]
        k_high = [sb(f"k_high{n}", [P, 2, SEQ], f32r) for n in range(2)]
        k_low = [sb(f"k_low{n}", [P, 2, SEQ], f32r) for n in range(2)]
        v = sb("v", [P, ST, F])
        neg_max = sb("neg_max", [P, PROBS, 1])
        sums = sb("sums", [P, 2, PV_UNITS])
        recip = sb("recip", [P, 2, PV_UNITS])
        recip_wide = sb("recip_wide", [P, 2, PV_UNITS, HD])
        probs = sb("probs", [P, PROBS, SEQ])
        probsT = sb("probsT", [P, 2, ST, 2, PV_TOKENS])
        recip_cols = sb("recip_cols", [P, 2, PV_TOKENS])
        featsT = sb("featsT", [P, PAIRS, SEQ])
        x_first = featsT[:].rearrange("p a (b f) -> p (a b) f", f=F)
        first_stats = sb("first_stats", [P, ST, 6])
        first_mean_var = sb("first_mean_var", [P, ST, 2])
        first_var_eps = sb("first_var_eps", [P, ST])
        first_rstd = sb("first_rstd", [P, ST])
        first_shift = sb("first_shift", [P, ST])
        residual = sb("residual", [P, 2, F])
        x1_out = sb("x1_out", [P, 2, F])
        x1_stats = sb("x1_stats", [P, 2, 6])
        x1_mean_var = sb("x1_mean_var", [P, 2, 2])
        x1_var_eps = sb("x1_var_eps", [P, 2, 1])
        x1_minus_mean = sb("x1_minus_mean", [P, 2, 1])
        x1_rstd = sb("x1_rstd", [P, 2, 1])
        x1_shift = sb("x1_shift", [P, 2, 1])
        x1n = xn
        x1_parts = probs[:, PROBS - 2:, :].bitcast(f32r).rearrange("p s (n k t) -> p s n k t", n=2, k=KT)
        score_psum = ctx.enter_context(nc.psum_tensor("score_psum", [P, 2, SEQ], f32))
        transpose_psum = ctx.enter_context(nc.psum_tensor("transpose_psum", [P, 2, NC], f32))
        general_psum = ctx.enter_context(nc.psum_tensor("general_psum", [P, 2, NC], f32))

        wqk_loaded, wv_loaded, wo_loaded = sem("wqk_loaded"), sem("wv_loaded"), sem("wo_loaded")
        x_loaded = [sem(f"x_loaded{n}") for n in range(2)]
        x_first_loaded = [sem(f"x_first_loaded{n}") for n in range(2)]
        first_step = sem("first_step")
        first_var_ready = sem("first_var_ready")
        first_rstd_ready = sem("first_rstd_ready")
        first_shift_ready = sem("first_shift_ready")
        residual_loaded = [sem(f"residual_loaded{n}") for n in range(2)]
        stored = [sem(f"x1_stored{n}") for n in range(2)]
        last_row_stored = sem("last_row_stored")
        parts_stored = [sem(f"x1_parts_stored{n}") for n in range(2)]
        x1_step, x1_stats_seen = sem("x1_step"), sem("x1_stats_seen")
        x1_rstd_ready = sem("x1_rstd_ready")
        x1_shift_ready = sem("x1_shift_ready")
        x1_norm_done = sem("x1_norm_done")
        x1_high_ready = sem("x1_high_ready")
        residual_ready = sem("residual_ready")
        stats_step, stats_seen = sem("stats_step"), sem("stats_seen")
        var_ready = sem("var_ready")
        rstd_ready = sem("rstd_ready")
        shift_ready = sem("shift_ready")
        norm_done = sem("norm_done")
        high_ready = sem("high_ready")
        low_ready = sem("low_ready")
        scores_done = sem("scores_done")
        max_ready = sem("max_ready")
        exp_done = sem("exp_done")
        transposed = sem("transposed")
        copied_low = sem("copied_low")
        copied_high = sem("copied_high")
        recip_step = sem("recip_step")
        recip_ready = sem("recip_ready")
        cols_ready = sem("cols_ready")
        general_done = sem("general_done")
        emptied = [sem(f"general_emptied{n}") for n in range(2)]
        block = ctx.enter_context(nc.Block(name="attention"))

        def done(use, b=None):
            if b is None:
                return first.number[use] + 1
            return b * body.total + (first.total + body.number[use] + 1)

        def empty(use, b=None):
            if b is None:
                return first.turn[use] + 1
            return b * body.turns[0] + (first.turns[0] + body.turn[use] + 1)

        QK_ROW = 4 * PAIRS

        def low_ops(n):
            return n // 4 * 12 + (0, 2, 4, 8)[n % 4]

        def unit(g):
            return g // PER_PAIR, g % PER_PAIR // 2, g % 2

        def place(c):
            p, n = c // (PV_CHUNKS // PAIRS), c % (PV_CHUNKS // PAIRS)
            return p, slice(n * PV_TOKENS, (n + 1) * PV_TOKENS)

        x_tiles = x.rearrange("b (t p) f -> (b t) p f", p=P)

        def tile_at(ap, n):
            return ap[bass.ds(n, 1)].rearrange("a p f -> (a p) f")

        @block.sync
        def _(sp):
            def load_x(i, source, free):
                sp.wait_ge(norm_done, free)
                sp.dma_start(x_in[:, i % 2, :], source).then_inc(x_loaded[i % 2], 16)

            def store_parts(b, i):
                use = ("x1t", i)
                sp.wait_ge(emptied[body.bank[use]], empty(use, b))
                chunk = x_parts_scratch[bass.ds(b * (ST // CT) + i // CT, 1)].rearrange("a p n k t -> (a p) n k t")
                for part in range(2):
                    sp.dma_start(chunk[:, part, :, i % CT * P:(i % CT + 1) * P],
                                 x1_parts[:, i % 2, part].bitcast(f32)).then_inc(parts_stored[i % 2], 16)

            for half in range(2):
                tiles = slice(half * ST // 2, (half + 1) * ST // 2)
                sp.dma_start(x_first[:, tiles, :], x_tiles[tiles].rearrange("t p f -> p t f")
                             ).then_inc(x_first_loaded[half], 16)
            sp.dma_start(wq[:], Wq.rearrange("(t p) n -> p t n", p=P)).then_inc(wqk_loaded, 16)
            sp.dma_start(wk[:], Wk.rearrange("(t p) n -> p t n", p=P)).then_inc(wqk_loaded, 16)
            sp.dma_start(wv[:], Wv.rearrange("(t p) n -> p t n", p=P)).then_inc(wv_loaded, 16)
            sp.dma_start(bv_rows[:], bv.rearrange("(a n) -> a n", a=1).to_broadcast([P, F])).then_inc(wv_loaded, 16)
            sp.dma_start(wo[:], Wo.rearrange("(t p) n -> p t n", p=P)).then_inc(wo_loaded, 16)
            sp.dma_start(bo_rows[:], bo.rearrange("(a n) -> a n", a=1).to_broadcast([P, F])).then_inc(wo_loaded, 16)
            sp.sem_inc(last_row_stored, 1)
            with sp.Fori(0, BATCH) as b:
                for i in range(2):
                    sp.dma_start(residual[:, i, :], tile_at(x_tiles, b * ST + i)).then_inc(residual_loaded[i], 16)
                for i in range(ST):
                    load_x(i, tile_at(x_tiles, (b + 1) % BATCH * ST + i), b * ST + (ST + i - 1))
                for i in range(ST):
                    use = ("wo", i)
                    sp.wait_ge(emptied[body.bank[use]], empty(use, b))
                    sp.dma_start(tile_at(x1_scratch, b * ST + i), x1_out[:, i % 2, :]).then_inc(stored[i % 2], 16)
                    if i + 2 < ST:
                        sp.dma_start(residual[:, i % 2, :],
                                     tile_at(x_tiles, b * ST + (i + 2))).then_inc(residual_loaded[i % 2], 16)
                    if i >= 2:
                        store_parts(b, i - 2)
                for i in range(ST - 2, ST):
                    store_parts(b, i)
                for n in range(2):
                    sp.wait_ge(stored[n], b * (16 * ST // 2) + 16 * ST // 2)
                    sp.wait_ge(parts_stored[n], b * (32 * ST // 2) + 32 * ST // 2)
                sp.sem_inc(last_row_stored, 1)

        @block.gpsimd
        def _(pool):
            def inverse_std(i, count):
                pool.wait_ge(var_ready, count)
                nc.gpsimd.tensor_tensor(rstd[:, i % 2, :], var_eps[:, i % 2, :], minus_half[:, 0:1],
                                        ALU.pow).then_inc(rstd_ready, 1)

            def low_parts(use, count, ops_before):
                _, p, n = use
                s, tok = p % 2, slice(n % 2 * NC, (n % 2 + 1) * NC)
                pool.wait_ge(high_ready, count)
                parts = q_parts[s] if n < 2 else k_high[s]
                low = q_parts[s] if n < 2 else k_low[s]
                for h in range(2):
                    own, other = slice(h * HD, (h + 1) * HD), slice((1 - h) * HD, (2 - h) * HD)
                    for m, rows in enumerate((other,) if n < 2 else (own, other)):
                        nc.gpsimd.tensor_tensor(low[rows, h, tok], qk_full[own, n % 2, :],
                                                parts[own, h, tok].bitcast(f32), ALU.subtract
                                                ).then_inc(low_ready, 1)
                        pool.wait_ge(low_ready, ops_before + ((1 if n < 2 else 2) * h + m + 1))

            def scale_of_x1(i, b):
                s = i % 2
                pool.wait_ge(x1_step, b * (4 * ST) + (4 * i + 4))
                nc.gpsimd.tensor_tensor(x1_rstd[:, s, :], x1_var_eps[:, s, :], minus_half[:, 0:1],
                                        ALU.pow).then_inc(x1_rstd_ready, 1)
                pool.wait_ge(x1_rstd_ready, b * ST + (i + 1))
                nc.gpsimd.tensor_tensor(x1_shift[:, s, :], x1_minus_mean[:, s, :], x1_rstd[:, s, :],
                                        ALU.mult).then_inc(x1_shift_ready, 1)

            for half in range(2):
                tiles = slice(half * ST // 2, (half + 1) * ST // 2)
                pool.wait_ge(first_var_ready, half + 1)
                nc.gpsimd.tensor_tensor(first_rstd[:, tiles], first_var_eps[:, tiles], minus_half[:], ALU.pow
                                        ).then_inc(first_rstd_ready, 1)
            for n in range(4):
                low_parts(("qk", 0, n), n + 1, low_ops(n))
            pool.wait_ge(wo_loaded, 32)
            with pool.Fori(0, BATCH) as b:
                for g in range(UNITS):
                    for i in range(ST):
                        if stats_unit(i) == g:
                            inverse_std(i, b * ST + (i + 1))
                    for use in filler[g]:
                        if use[0] == "qk":
                            low_parts(use, b * QK_ROW + (4 + qk_order[use] + 1),
                                      b * low_ops(QK_ROW) + low_ops(4 + qk_order[use]))
                for i in range(ST + 1):
                    if i < ST:
                        pool.wait_ge(residual_loaded[i % 2], b * (16 * ST // 2) + 16 * (i // 2 + 1))
                        nc.gpsimd.tensor_tensor(residual[:, i % 2, :], residual[:, i % 2, :], bo_rows[:],
                                                ALU.add).then_inc(residual_ready, 1)
                    if i:
                        scale_of_x1(i - 1, b)

        @block.scalar
        def _(act):
            def copy_out(use, b=None, split=None):
                kind = use[0]
                ring = first if b is None else body
                bank = ring.bank[use]
                if kind == "xt":
                    act.wait_ge(general_done, done(use, b))
                    i = use[1]
                    nc.scalar.activation(xnT[:, :, i * P:(i + 1) * P], general_psum[:, bank, :].rearrange(
                        "p (k t) -> p k t", k=KT), ACT.Copy).then_inc(emptied[bank], 1)
                if kind == "qk":
                    _, p, n = use
                    act.wait_ge(general_done, done(use, b))
                    if split is not None:
                        act.wait_ge(low_ready, split)
                    bias, scale = (bq_scaled[:, p:p + 1], SCORE_SCALE) if n < 2 else (consts_of["bk"](p), 1.0)
                    nc.scalar.activation(qk_full[:, n % 2, :], general_psum[:, bank, :], ACT.Identity, bias=bias,
                                         scale=scale).then_inc(emptied[bank], 1)
                if kind == "pv":
                    c = use[1]
                    act.wait_ge(general_done, done(use, b))
                    nc.scalar.activation(recip_cols[:, c % 2, :], general_psum[:, bank, PV_TOKENS:],
                                         ACT.Copy).then_inc(cols_ready, 1)

            def copy_transposed(g, b):
                _, st, h = unit(g)
                c = g // PV_UNITS
                act.wait_ge(transposed, b * (2 * UNITS) + (2 * PROBS + 2 * g + 1))
                nc.scalar.activation(probsT[:, c % 2, 0:4, h, st % 2 * P:(st % 2 + 1) * P],
                                     transpose_psum[:, 0, :].rearrange("p (k t) -> p k t", k=4),
                                     ACT.Copy).then_inc(copied_low, 1)

            def normalise_x1(i, b):
                act.wait_ge(x1_shift_ready, b * ST + (i + 1))
                nc.scalar.activation(x1n[:, i % 2, :], x1_out[:, i % 2, :], ACT.Identity, bias=x1_shift[:, i % 2, :],
                                     scale=x1_rstd[:, i % 2, :]).then_inc(x1_norm_done, 1)

            def high_x1(i, b):
                use = ("x1t", i)
                if i < 2:
                    act.wait_ge(last_row_stored, b + 1)
                else:
                    act.wait_ge(parts_stored[i % 2], b * (32 * ST // 2) + 32 * (i // 2))
                act.wait_ge(general_done, done(use, b))
                nc.scalar.activation(x1_parts[:, i % 2, 0], general_psum[:, body.bank[use], :].rearrange(
                    "p (k t) -> p k t", k=KT), ACT.Copy).then_inc(x1_high_ready, 1)

            act.sem_inc(exp_done, 2)
            act.sem_inc(copied_low, 1)
            for i in range(ST):
                copy_out(("xt", i))
            for n in range(4):
                copy_out(("qk", 0, n), None, low_ops(n - 1) if n >= 2 else None)
            with act.Fori(0, BATCH) as b:
                for g in range(UNITS + LAG):
                    short = g >= UNITS or not filler[g]
                    if g >= LAG and short:
                        copy_transposed(g - LAG, b)
                    if g < UNITS:
                        act.wait_ge(max_ready, b * UNITS + (g + 1))
                        if g == PROBS - 2:
                            act.wait_ge(last_row_stored, b + 1)
                        act.wait_ge(transposed, b * (2 * UNITS) + (2 * g + 2))
                        nc.scalar.activation(probs[:, g % PROBS, :], score_psum[:, g % 2, :], ACT.Exp,
                                             bias=neg_max[:, g % PROBS, :],
                                             accum_out=sums[:, g // PV_UNITS % 2, g % PV_UNITS:g % PV_UNITS + 1],
                                             ).then_inc(exp_done, 1)
                        for use in filler[g]:
                            copy_out(use, b, b * low_ops(QK_ROW) + low_ops(3 + qk_order[use])
                                     if use[0] == "qk" else None)
                    if g >= LAG and not short:
                        copy_transposed(g - LAG, b)
                copy_out(tail[0], b)
                for n, use in enumerate(tail):
                    if use[0] == "x1t":
                        high_x1(use[1], b)
                    if n and tail[n - 1][0] == "wo":
                        normalise_x1(tail[n - 1][1], b)

        @block.vector
        def _(dve):
            def tile_stats(i, loads, tile):
                s = i % 2
                dve.wait_ge(x_loaded[s], loads)
                nc.vector.bn_stats(stats[:, s, :], x_in[:, s, :]).then_inc(stats_step, 1)
                dve.wait_ge(stats_step, tile * 2 + 1)
                dve.sem_inc(stats_seen, 1)
                nc.vector.bn_aggr(mean_var[:, s, :], stats[:, s, :]).then_inc(stats_step, 1)
                dve.wait_ge(stats_step, tile * 2 + 2)
                nc.vector.tensor_scalar(var_eps[:, s, :], mean_var[:, s, 1:2], LN_EPS, None,
                                        ALU.add).then_inc(var_ready, 1)

            def normalise(i, tile):
                s = i % 2
                dve.wait_ge(rstd_ready, tile + 1)
                nc.vector.scalar_tensor_tensor(shift[:, s, :], mean_var[:, s, 0:1], -1.0, rstd[:, s, :], ALU.mult,
                                               ALU.mult).then_inc(shift_ready, 1)
                dve.wait_ge(shift_ready, tile + 1)
                nc.vector.tensor_scalar(xn[:, s, :], x_in[:, s, :], rstd[:, s, :], shift[:, s, :], ALU.mult,
                                        ALU.add).then_inc(norm_done, 1)

            def high_parts(use, b=None):
                _, p, n = use
                s, tok = p % 2, slice(n % 2 * NC, (n % 2 + 1) * NC)
                ring = first if b is None else body
                dve.wait_ge(emptied[ring.bank[use]], empty(use, b))
                high = q_parts[s] if n < 2 else k_high[s]
                for h in range(2):
                    own, other = slice(h * HD, (h + 1) * HD), slice((1 - h) * HD, (2 - h) * HD)
                    for rows in ((own,) if n < 2 else (own, other)):
                        last = nc.vector.tensor_copy(high[rows, h, tok], qk_full[own, n % 2, :])
                last.then_inc(high_ready, 1)

            def copy_out(use, b=None):
                kind, bank = use[0], (first if b is None else body).bank[use]
                if kind == "v":
                    dve.wait_ge(general_done, done(use, b))
                    nc.vector.tensor_tensor(v[:, use[1], :], general_psum[:, bank, :], bv_rows[:],
                                            ALU.add).then_inc(emptied[bank], 1)
                if kind == "pv":
                    c = use[1]
                    p, tok = place(c)
                    dve.wait_ge(cols_ready, b * PV_CHUNKS + (c + 1))
                    nc.vector.tensor_tensor(featsT[:, p, tok], general_psum[:, bank, 0:PV_TOKENS],
                                            recip_cols[:, c % 2, :], ALU.mult).then_inc(emptied[bank], 1)
                if kind == "wo":
                    i = use[1]
                    dve.wait_ge(general_done, done(use, b))
                    dve.wait_ge(residual_ready, b * ST + (i + 1))
                    if i < 2:
                        dve.wait_ge(last_row_stored, b + 1)
                    else:
                        dve.wait_ge(stored[i % 2], b * (16 * ST // 2) + 16 * (i // 2))
                        dve.wait_ge(x1_norm_done, b * ST + (i - 1))
                    nc.vector.tensor_tensor(x1_out[:, i % 2, :], general_psum[:, bank, :], residual[:, i % 2, :],
                                            ALU.add).then_inc(emptied[bank], 1)
                    stats_of_x1(use, b)
                if kind == "x1t":
                    i = use[1]
                    dve.wait_ge(x1_high_ready, b * ST + (i + 1))
                    nc.vector.tensor_tensor(x1_parts[:, i % 2, 1], general_psum[:, bank, :].rearrange(
                        "p (k t) -> p k t", k=KT), x1_parts[:, i % 2, 0].bitcast(f32), ALU.subtract
                        ).then_inc(emptied[bank], 1)

            def stats_of_x1(use, b):
                i = use[1]
                s, before = i % 2, b * (4 * ST) + 4 * i
                dve.wait_ge(emptied[body.bank[use]], empty(use, b))
                nc.vector.bn_stats(x1_stats[:, s, :], x1_out[:, s, :]).then_inc(x1_step, 1)
                dve.wait_ge(x1_step, before + 1)
                dve.sem_inc(x1_stats_seen, 1)
                nc.vector.bn_aggr(x1_mean_var[:, s, :], x1_stats[:, s, :]).then_inc(x1_step, 1)
                dve.wait_ge(x1_step, before + 2)
                nc.vector.tensor_scalar(x1_var_eps[:, s, :], x1_mean_var[:, s, 1:2], LN_EPS, None,
                                        ALU.add).then_inc(x1_step, 1)
                nc.vector.tensor_scalar(x1_minus_mean[:, s, :], x1_mean_var[:, s, 0:1], -1.0, None,
                                        ALU.mult).then_inc(x1_step, 1)

            def copy_transposed(g, b):
                _, st, h = unit(g)
                c = g // PV_UNITS
                dve.wait_ge(transposed, b * (2 * UNITS) + (2 * PROBS + 2 * g + 2))
                nc.vector.tensor_copy(probsT[:, c % 2, 4:8, h, st % 2 * P:(st % 2 + 1) * P],
                                      transpose_psum[:, 1, :].rearrange("p (k t) -> p k t", k=4)
                                      ).then_inc(copied_high, 1)
                if g % PV_UNITS == PV_UNITS - 1:
                    dve.wait_ge(exp_done, b * UNITS + (2 + g + 1))
                    nc.vector.reciprocal(recip[:, c % 2, :], sums[:, c % 2, :]).then_inc(recip_step, 1)
                    dve.wait_ge(recip_step, b * PV_CHUNKS + (c + 1))
                    nc.vector.tensor_copy(recip_wide[:, c % 2], recip[:, c % 2, :].rearrange(
                        "p (u o) -> p u o", o=1).to_broadcast([P, PV_UNITS, HD])).then_inc(recip_ready, 1)

            dve.sem_inc(copied_high, 1)
            def first_statistics(half):
                tiles = range(half * ST // 2, (half + 1) * ST // 2)
                span = slice(tiles[0], tiles[-1] + 1)
                dve.wait_ge(x_first_loaded[half], 16)
                for i in tiles:
                    nc.vector.bn_stats(first_stats[:, i, :], x_first[:, i, :]).then_inc(first_step, 1)
                dve.wait_ge(first_step, half * ST + ST // 2)
                for i in tiles:
                    nc.vector.bn_aggr(first_mean_var[:, i, :], first_stats[:, i, :]).then_inc(first_step, 1)
                dve.wait_ge(first_step, half * ST + ST)
                nc.vector.tensor_scalar(first_var_eps[:, span], first_mean_var[:, span, 1], LN_EPS, None,
                                        ALU.add).then_inc(first_var_ready, 1)

            def first_normalise(half):
                tiles = range(half * ST // 2, (half + 1) * ST // 2)
                span = slice(tiles[0], tiles[-1] + 1)
                dve.wait_ge(first_rstd_ready, half + 1)
                nc.vector.scalar_tensor_tensor(first_shift[:, span], first_mean_var[:, span, 0], -1.0,
                                               first_rstd[:, span], ALU.mult, ALU.mult).then_inc(first_shift_ready, 1)
                dve.wait_ge(first_shift_ready, half + 1)
                for i in tiles:
                    if i >= 2:
                        dve.wait_ge(general_done, done(("xt", i - 2)))
                    nc.vector.tensor_scalar(xn[:, i % 2, :], x_first[:, i, :], first_rstd[:, i:i + 1],
                                            first_shift[:, i:i + 1], ALU.mult, ALU.add).then_inc(norm_done, 1)

            for half in range(2):
                first_statistics(half)
            for half in range(2):
                first_normalise(half)
            for n in range(4):
                high_parts(("qk", 0, n))
            dve.wait_ge(wv_loaded, 32)
            for i in range(EARLY_V):
                copy_out(("v", i))
            with dve.Fori(0, BATCH) as b:
                for g in range(UNITS + LAG):
                    if g < UNITS:
                        dve.wait_ge(scores_done, b * UNITS + (g + 1))
                        nc.vector.tensor_reduce(neg_max[:, g % PROBS, :], score_psum[:, g % 2, :], AX.X, ALU.max,
                                                negate=True).then_inc(max_ready, 1)
                        for i in range(ST):
                            if stats_unit(i) == g:
                                tile_stats(i, b * (16 * ST // 2) + 16 * (i // 2 + 1), b * ST + i)
                            if stats_unit(i) + 1 == g:
                                normalise(i, b * ST + i)
                        for use in filler[g]:
                            copy_out(use, b)
                    if g >= LAG:
                        copy_transposed(g - LAG, b)
                    if g < UNITS:
                        for use in filler[g]:
                            if use[0] == "qk":
                                high_parts(use, b)
                for use in tail:
                    copy_out(use, b)

        @block.tensor
        def _(pe):
            def project(use, b=None):
                ring = first if b is None else body
                bank = ring.bank[use]
                out_bank = general_psum[:, bank, :]
                if b is not None:
                    pe.wait_ge(emptied[bank], b * body.turns[0] + (first.turns[0] + body.turn[use]))
                elif first.turn[use]:
                    pe.wait_ge(emptied[bank], first.turn[use])
                kind = use[0]
                if kind == "xt":
                    i = use[1]
                    pe.wait_ge(norm_done, (i + 1) if b is None else b * ST + (ST + i + 1))
                    for k in range(KT):
                        last = nc.tensor.transpose(out_bank[:, k * P:(k + 1) * P], xn[:, i % 2, k * P:(k + 1) * P],
                                                   ident[:])
                elif kind == "qk":
                    _, p, n = use
                    w = wq if n < 2 else wk
                    for k in range(KT):
                        last = nc.tensor.matmul(out_bank, w[:, k, p * P:(p + 1) * P],
                                                xnT[:, k, n % 2 * NC:(n % 2 + 1) * NC], start=k == 0,
                                                stop=k == KT - 1)
                elif kind == "v":
                    i = use[1]
                    for k in range(KT):
                        last = nc.tensor.matmul(out_bank, xnT[:, k, i * P:(i + 1) * P], wv[:, k, :], start=k == 0,
                                                stop=k == KT - 1)
                elif kind == "pv":
                    c = use[1]
                    p, _ = place(c)
                    g = c * PV_UNITS + PV_UNITS - 1
                    pe.wait_ge(copied_low, b * UNITS + (1 + g + 1))
                    pe.wait_ge(copied_high, b * UNITS + (1 + g + 1))
                    for t in range(ST):
                        for h in range(2):
                            nc.tensor.matmul(out_bank[h * HD:(h + 1) * HD, 0:PV_TOKENS],
                                             v[:, t, p * P + h * HD:p * P + (h + 1) * HD],
                                             probsT[:, c % 2, t, h, :], start=t == 0, stop=t == ST - 1)
                    pe.wait_ge(recip_ready, b * PV_CHUNKS + (c + 1))
                    for m in range(PV_UNITS // 2):
                        last = nc.tensor.transpose(out_bank[:, PV_TOKENS + m * P:PV_TOKENS + (m + 1) * P],
                                                   recip_wide[:, c % 2, 2 * m:2 * m + 2, :].rearrange(
                                                       "p u d -> p (u d)"), ident[:])
                elif kind == "x1t":
                    i = use[1]
                    pe.wait_ge(x1_norm_done, b * ST + (i + 1))
                    for k in range(KT):
                        last = nc.tensor.transpose(out_bank[:, k * P:(k + 1) * P], x1n[:, i % 2, k * P:(k + 1) * P],
                                                   ident[:])
                elif kind == "wo":
                    i = use[1]
                    if i == 0:
                        feats = ("pv", PV_CHUNKS - 1)
                        pe.wait_ge(emptied[body.bank[feats]], empty(feats, b))
                    for p in range(PAIRS):
                        last = nc.tensor.matmul(out_bank, featsT[:, p, i * P:(i + 1) * P], wo[:, p, :],
                                                start=p == 0, stop=p == PAIRS - 1)
                last.then_inc(general_done, 1)

            def scores(g, b):
                p, st, h = unit(g)
                s = p % 2
                if g % PER_PAIR == 0:
                    pe.wait_ge(low_ready, b * low_ops(QK_ROW) + low_ops(4 * (p + 1)))
                pe.wait_ge(exp_done, b * UNITS + (g + 1))
                for n in range(2):
                    for k_part in (k_high, k_low):
                        last = nc.tensor.matmul(score_psum[:, g % 2, n * NC:(n + 1) * NC],
                                                q_parts[s][:, h, st * P:(st + 1) * P],
                                                k_part[s][:, h, n * NC:(n + 1) * NC], start=k_part is k_high,
                                                stop=k_part is k_low)
                last.then_inc(scores_done, 1)

            def transposes(g, b):
                pe.wait_ge(exp_done, b * UNITS + (2 + g + 1))
                for n, copied in enumerate((copied_low, copied_high)):
                    pe.wait_ge(copied, b * UNITS + (g + 1))
                    for k in range(4):
                        t = 4 * n + k
                        last = nc.tensor.transpose(transpose_psum[:, n, k * P:(k + 1) * P],
                                                   probs[:, g % PROBS, t * P:(t + 1) * P], ident[:])
                    last.then_inc(transposed, 1)

            pe.sem_inc(transposed, 2 * PROBS)
            for i in range(ST):
                project(("xt", i))
            pe.wait_ge(emptied[first.bank["xt", ST - 1]], empty(("xt", ST - 1)))
            pe.wait_ge(wqk_loaded, 32)
            for n in range(4):
                project(("qk", 0, n))
            pe.wait_ge(wv_loaded, 32)
            for i in range(EARLY_V):
                project(("v", i))
            pe.wait_ge(wo_loaded, 32)
            with pe.Fori(0, BATCH) as b:
                for g in range(UNITS + LAG):
                    if g < UNITS:
                        scores(g, b)
                        for use in filler[g]:
                            if use == ("qk", 0, 0):
                                rows = ("xt", ST - 1)
                                pe.wait_ge(emptied[body.bank[rows]], empty(rows, b))
                            project(use, b)
                    if g >= LAG:
                        transposes(g - LAG, b)
                for use in tail:
                    project(use, b)


def ffn_uses():
    gate_up = lambda i: [("gate_up", i, n) for n in range(2 * GROUPS)]
    down = lambda i: [("down", i, j) for j in range(KT)]
    back = [("y", r) for r in range(CT)]
    start = down(0) + [u for i in range(3, AHEAD) for u in gate_up(i) + down(i - 2)]
    start = start[:-KT]
    shared = down(LATE_DOWN) + [u for i in range(AHEAD, FI) for u in gate_up(i) + down(i - 2)]
    first = gate_up(0) + gate_up(1) + gate_up(2) + start
    body = shared + gate_up(0) + down(FI - 2) + gate_up(1) + down(FI - 1) + gate_up(2) + back + start
    last = shared + down(FI - 2) + down(FI - 1) + back
    return first, body, last


def build_ffn(nc, x1_scratch, x_parts_scratch, ffn_values, ident, consts_of, minus_half, out):
    f32, f32r = mybir.dt.float32, mybir.dt.float32r
    ALU, ACT, AX = mybir.AluOpType, mybir.ActivationFunctionType, mybir.AxisListType
    BANKS = 8
    first_uses, body_uses, last_uses = ffn_uses()
    first, body, last_ring = Ring(first_uses, BANKS), Ring(body_uses, BANKS), Ring(last_uses, BANKS)
    BODIES = CHUNKS - 1
    SLOTS = 3
    out_tiles = out.rearrange("b (t p) f -> (b t) p f", p=P)

    ctx = ExitStack()
    with ctx:
        sb = lambda name, shape, dt=f32: ctx.enter_context(nc.sbuf_tensor(name, shape, dt))
        sem = lambda name: ctx.enter_context(nc.semaphore(name))
        w = sb("w", [P, FI, 3 * KT, P], f32r)
        residual = sb("residual2", [P, CT, F])
        x_parts = sb("x_parts", [P, 2, 2, KT, NC], f32r)
        part = sb("part", [P, SLOTS, 4, NC])
        gate_up_sum = sb("gate_up_sum", [P, SLOTS, 2, NC])
        silu = sb("silu", [P, SLOTS, NC])
        h = sb("h", [P, SLOTS, NC])
        h_high = sb("h_high", [P, SLOTS, NC], f32r)
        h_low = sb("h_low", [P, SLOTS, NC], f32r)
        down_part = sb("down_part", [P, SLOTS, KT // 2, NC])
        yT = sb("yT", [P, KT, NC])
        y = sb("y", [P, CT, F])
        square = sb("square", [P, F])
        square_sum = sb("square_sum", [P, CT])
        mean_square = sb("mean_square", [P, CT])
        inv_rms = sb("inv_rms", [P, CT])
        psum = ctx.enter_context(nc.psum_tensor("ffn_psum", [P, BANKS, NC], f32))

        w_loaded = [sem(f"w_loaded{i}") for i in range(FI)]
        x_loaded = sem("x_parts_loaded")
        residual_loaded = sem("residual2_loaded")
        products_done = sem("products_done")
        emptied = [sem(f"bank_emptied{n}") for n in range(BANKS)]
        gate_sum_ready = sem("gate_sum_ready")
        up_sum_ready = sem("up_sum_ready")
        silu_ready = sem("silu_ready")
        h_ready = sem("h_ready")
        h_high_ready = sem("h_high_ready")
        h_low_ready = sem("h_low_ready")
        y_added = sem("y_added")
        square_ready = sem("square_ready")
        mean_ready = sem("mean_ready")
        inv_rms_ready = sem("inv_rms_ready")
        out_ready = sem("out_ready")
        y_free = sem("y_free")
        out_stored = sem("out_stored")
        block = ctx.enter_context(nc.Block(name="ffn"))

        def tile_at(ap, n):
            return ap[bass.ds(n, 1)].rearrange("a p f -> (a p) f")

        class Phase:

            def __init__(self, c, ring, chunk):
                self.c, self.ring, self.chunk = c, ring, chunk

            def bank(self, use):
                return self.ring.bank[use]

            def done(self, use):
                return self.total(body.total, first.total) + self.ring.number[use] + 1

            def turn(self, use):
                bank = self.ring.bank[use]
                return self.total(body.turns[bank], first.turns[bank]) + self.ring.turn[use]

            def total(self, per_body, before):
                if self.ring is first:
                    return 0
                return self.chunk * per_body + before

            def chunk_of(self, use):
                kind, i = use[0], use[1]
                if self.ring is body and (kind == "gate_up" and i < AHEAD or kind == "down" and i < LATE_DOWN):
                    return self.chunk + 1
                return self.chunk

            def tile(self, use):
                return self.chunk_of(use) * FI + use[1]

        def phases(eng, program):
            program(Phase(None, first, 0), first_uses)
            with eng.Fori(0, BODIES) as c:
                program(Phase(c, body, c), body_uses)
            program(Phase(None, last_ring, BODIES), last_uses)


        def emptied_value(ph, use):
            return ph.turn(use) + 1

        def added(chunk, i, j):
            return chunk * ((FI - 1) * KT // 2) + ((i - 1) * KT // 2 + j // 2 + 1)

        def down_slot(i, j):
            return down_part[:, i % SLOTS, j // 2, :]

        def freed(i, count):
            back = {0: FI % SLOTS, 1: FI % SLOTS, 2: FI % SLOTS + SLOTS}.get(i, SLOTS)
            return None if isinstance(count, int) and count < back else count - (back - 1)

        def wait_freed(eng, semaphore, i, count):
            value = freed(i, count)
            if value is not None:
                eng.wait_ge(semaphore, value)

        def group_scale(use):
            _, i, n = use
            return consts_of["gu"](n % GROUPS, i + FI * (n // GROUPS))

        @block.sync
        def _(sp):
            x1_chunks = x1_scratch.rearrange("(c r) p f -> c p r f", r=CT)

            def chunk_at(c):
                return x1_chunks[c] if isinstance(c, int) else \
                    x1_chunks[bass.ds(c, 1)].rearrange("a p r f -> (a p) r f")

            def load_x(c):
                source = x_parts_scratch[c] if isinstance(c, int) else \
                    x_parts_scratch[bass.ds(c, 1)].rearrange("a p n k t -> (a p) n k t")
                slot = x_parts[:, c] if isinstance(c, int) else \
                    x_parts[:, bass.ds(c % 2, 1)].rearrange("p a n k t -> p (a n) k t")
                sp.dma_start(slot.bitcast(f32), source).then_inc(x_loaded, 16)

            def load_residual(c):
                sp.dma_start(residual[:], chunk_at(c)).then_inc(residual_loaded, 16)

            def store(c):
                for r in range(CT):
                    sp.wait_ge(out_ready, c * CT + (r + 1))
                    sp.dma_start(tile_at(out_tiles, c * CT + r), y[:, r, :]).then_inc(out_stored, 16)
                sp.wait_ge(out_stored, c * (16 * CT) + 16 * CT)
                sp.sem_inc(y_free, 1)

            def load_w(i):
                sp.dma_start(w[:, i].rearrange("p k n -> p (k n)").bitcast(f32),
                             ffn_values[i]).then_inc(w_loaded[i], 16)

            load_w(0)
            load_x(0)
            for i in range(1, FI):
                load_w(i)
            sp.sem_inc(y_free, 1)
            load_residual(0)
            sp.wait_ge(x_loaded, 16)
            load_x(1)
            with sp.Fori(0, BODIES - 1) as c:
                sp.wait_ge(products_done, Phase(c, body, c).done(("gate_up", FI - 1, 2 * GROUPS - 1)))
                sp.wait_ge(x_loaded, c * 16 + 32)
                load_x(c + 2)
                store(c)
                load_residual(c + 1)
            store(BODIES - 1)
            load_residual(BODIES)
            store(BODIES)

        @block.gpsimd
        def _(pool):
            def program(ph, uses):
                for use in uses:
                    kind = use[0]
                    if kind == "gate_up":
                        _, i, n = use
                        s, which = i % SLOTS, n // GROUPS
                        if n % GROUPS == GROUPS - 1:
                            tile = ph.tile(use)
                            pool.wait_ge(emptied[ph.bank(use)], emptied_value(ph, use))
                            wait_freed(pool, (silu_ready, h_ready)[which], i, tile)
                            nc.gpsimd.tensor_tensor(gate_up_sum[:, s, which, :], part[:, s, 2 * which, :],
                                                    part[:, s, 2 * which + 1, :], ALU.add
                                                    ).then_inc((gate_sum_ready, up_sum_ready)[which], 1)
                        if ph.ring is body and (i, n) == (5, 2):
                            inverse_rms(ph.chunk)
                    elif kind == "down":
                        _, i, j = use
                        if i and on_gpsimd(j):
                            pool.wait_ge(emptied[ph.bank(use)], emptied_value(ph, use))
                            if i > 1:
                                pool.wait_ge(y_added, added(ph.chunk_of(use), i - 1, j))
                            nc.gpsimd.tensor_tensor(yT[:, j, :], yT[:, j, :], down_slot(i, j), ALU.add
                                                    ).then_inc(y_added, 1)
                if ph.ring is last_ring:
                    inverse_rms(ph.chunk)

            def inverse_rms(chunk):
                pool.wait_ge(mean_ready, chunk + 1)
                nc.gpsimd.tensor_tensor(inv_rms[:], mean_square[:], minus_half[:, 0:CT], ALU.pow
                                        ).then_inc(inv_rms_ready, 1)

            phases(pool, program)

        @block.scalar
        def _(act):
            def program(ph, uses):
                for use in uses:
                    kind, bank = use[0], ph.bank(use)
                    if kind == "gate_up":
                        _, i, n = use
                        s = i % SLOTS
                        if n % 2 == 0:
                            wait_freed(act, gate_sum_ready if n < GROUPS else up_sum_ready, i, ph.tile(use))
                            act.wait_ge(products_done, ph.done(use))
                            nc.scalar.activation(part[:, s, n // 2, :], psum[:, bank, :], ACT.Copy,
                                                 scale=group_scale(use)).then_inc(emptied[bank], 1)
                        if n == 2 * GROUPS - 2 and (i or ph.ring is body):
                            round_h((i - 1) % FI, ph.tile(use) - 1)
                        if ph.ring is body and (i, n) in SQUARE_AT:
                            square_y(ph, SQUARE_AT.index((i, n)))
                        if n == 2 * GROUPS - 1:
                            act.wait_ge(gate_sum_ready, ph.tile(use) + 1)
                            nc.scalar.activation(silu[:, s, :], gate_up_sum[:, s, 0, :],
                                                 ACT.Silu).then_inc(silu_ready, 1)
                    elif kind == "down":
                        _, i, j = use
                        if on_gpsimd(j):
                            target = down_slot(i, j) if i else yT[:, j, :]
                            if i > SLOTS and on_gpsimd(j):
                                act.wait_ge(y_added, added(ph.chunk_of(use), i - SLOTS, j))
                            act.wait_ge(products_done, ph.done(use))
                            nc.scalar.activation(target, psum[:, bank, :], ACT.Copy,
                                                 scale=consts_of["down"](i, j)).then_inc(emptied[bank], 1)
                        if ph.ring is last_ring and (i, j) == (FI - 3, KT - 1):
                            round_h(FI - 1, ph.chunk * FI + (FI - 1))
                    elif kind == "y":
                        r = use[1]
                        act.wait_ge(products_done, ph.done(use))
                        if r == 0:
                            act.wait_ge(y_free, ph.chunk + 1)
                        nc.scalar.activation(y[:, r, :], psum[:, bank, :], ACT.Copy).then_inc(emptied[bank], 1)
                if ph.ring is last_ring:
                    for r in range(CT):
                        square_y(ph, r)

            SQUARE_AT = ((3, 1), (3, 5), (4, 1), (4, 5))

            def square_y(ph, r):
                use = ("y", r)
                act.wait_ge(emptied[ph.bank(use)], emptied_value(ph, use))
                if r or ph.ring is last_ring:
                    act.wait_ge(square_ready, ph.chunk * CT + r)
                nc.scalar.activation(square[:], y[:, r, :], ACT.Square, scale=F ** -0.5,
                                     accum_out=square_sum[:, r:r + 1]).then_inc(square_ready, 1)

            def round_h(i, tile):
                act.wait_ge(h_ready, tile + 1)
                nc.scalar.activation(h_high[:, i % SLOTS, :], h[:, i % SLOTS, :],
                                     ACT.Copy).then_inc(h_high_ready, 1)

            phases(act, program)

        @block.vector
        def _(dve):
            def multiply_h(i, tile):
                dve.wait_ge(silu_ready, tile + 1)
                dve.wait_ge(up_sum_ready, tile + 1)
                nc.vector.tensor_tensor(h[:, i % SLOTS, :], silu[:, i % SLOTS, :], gate_up_sum[:, i % SLOTS, 1, :],
                                        ALU.mult).then_inc(h_ready, 1)

            def low_h(i, tile):
                dve.wait_ge(h_high_ready, tile + 1)
                nc.vector.tensor_tensor(h_low[:, i % SLOTS, :], h[:, i % SLOTS, :],
                                        h_high[:, i % SLOTS, :].bitcast(f32), ALU.subtract
                                        ).then_inc(h_low_ready, 1)

            def add_eps(chunk):
                dve.wait_ge(square_ready, chunk * CT + CT)
                nc.vector.tensor_scalar(mean_square[:], square_sum[:], RMS_EPS, None, ALU.add
                                        ).then_inc(mean_ready, 1)

            def finish(chunk, r):
                dve.wait_ge(inv_rms_ready, chunk + 1)
                dve.wait_ge(residual_loaded, chunk * 16 + 16)
                nc.vector.scalar_tensor_tensor(y[:, r, :], y[:, r, :], inv_rms[:, r:r + 1], residual[:, r, :],
                                               ALU.mult, ALU.add).then_inc(out_ready, 1)

            def program(ph, uses):
                for use in uses:
                    kind, bank = use[0], ph.bank(use)
                    if kind == "gate_up":
                        _, i, n = use
                        s = i % SLOTS
                        tile = ph.tile(use)
                        if n % 2:
                            pair = ("gate_up", i, n - 1)
                            dve.wait_ge(emptied[ph.bank(pair)], emptied_value(ph, pair))
                            dve.wait_ge(products_done, ph.done(use))
                            nc.vector.scalar_tensor_tensor(part[:, s, n // 2, :], psum[:, bank, :],
                                                           group_scale(use), part[:, s, n // 2, :], ALU.mult,
                                                           ALU.add).then_inc(emptied[bank], 1)
                        if n == GROUPS - 1 and (i or ph.ring is body):
                            multiply_h((i - 1) % FI, tile - 1)
                        if n == 2 * GROUPS - 1 and i == 1 and ph.ring is first:
                            low_h(0, 0)
                        if ph.ring is body:
                            if (i, n) == (5, 0):
                                add_eps(ph.chunk)
                            if i in range(5, AHEAD) and n == 2 * GROUPS - 1:
                                finish(ph.chunk, i - 5)
                    elif kind == "down":
                        _, i, j = use
                        if not on_gpsimd(j):
                            scale = consts_of["down"](i, j)
                            if ph.ring is last_ring and i >= FI - 2:
                                own = ("down", i - 1, j)
                                dve.wait_ge(emptied[ph.bank(own)], emptied_value(ph, own))
                            dve.wait_ge(products_done, ph.done(use))
                            if i == 0:
                                op = nc.vector.tensor_scalar(yT[:, j, :], psum[:, bank, :], scale, None, ALU.mult)
                            else:
                                op = nc.vector.scalar_tensor_tensor(yT[:, j, :], psum[:, bank, :], scale,
                                                                    yT[:, j, :], ALU.mult, ALU.add)
                            op.then_inc(emptied[bank], 1)
                        if j == KT - 1:
                            if ph.ring is last_ring and i == FI - 3:
                                multiply_h(FI - 1, ph.chunk * FI + (FI - 1))
                                low_h(FI - 2, ph.chunk * FI + (FI - 2))
                            elif i < FI - 1 or ph.ring is body:
                                low_h((i + 1) % FI, ph.tile(use) + 1)
                if ph.ring is last_ring:
                    add_eps(ph.chunk)
                    for r in range(CT):
                        finish(ph.chunk, r)

            phases(dve, program)

        @block.tensor
        def _(pe):
            def program(ph, uses):
                for use in uses:
                    kind, bank = use[0], ph.bank(use)
                    if not (ph.ring is first and first.turn[use] == 0):
                        pe.wait_ge(emptied[bank], ph.turn(use))
                    if kind == "gate_up":
                        _, i, n = use
                        which, k = n // GROUPS, n % GROUPS
                        if n == 0 and i == 0:
                            pe.wait_ge(x_loaded, ph.chunk_of(use) * 16 + 16)
                        if n == 0 and not (ph.ring is body and i < AHEAD):
                            pe.wait_ge(w_loaded[i], 16)
                        for part in range(2):
                            last = nc.tensor.matmul(psum[:, bank, :], w[:, i, which * KT + k, :],
                                                    x_part(ph.chunk_of(use), part, k), start=part == 0,
                                                    stop=part == 1)
                    elif kind == "down":
                        _, i, j = use
                        if j == 0:
                            pe.wait_ge(h_low_ready, ph.tile(use) + 1)
                        for moving in (h_high, h_low):
                            last = nc.tensor.matmul(psum[:, bank, :], w[:, i, 2 * KT + j, :],
                                                    moving[:, i % SLOTS, :], start=moving is h_high,
                                                    stop=moving is h_low)
                    elif kind == "y":
                        r = use[1]
                        if r == 0:
                            for j in range(KT):
                                if on_gpsimd(j):
                                    pe.wait_ge(y_added, added(ph.chunk, FI - 1, j))
                                else:
                                    own = ("down", FI - 1, j)
                                    pe.wait_ge(emptied[ph.bank(own)], emptied_value(ph, own))
                        for j in range(KT):
                            last = nc.tensor.transpose(psum[:, bank, j * P:(j + 1) * P],
                                                       yT[:, j, r * P:(r + 1) * P], ident[:])
                    last.then_inc(products_done, 1)

            def x_part(chunk, part, k):
                if isinstance(chunk, int):
                    return x_parts[:, chunk % 2, part, k, :]
                return x_parts[:, bass.ds(chunk % 2, 1), part, k, :].rearrange("p a t -> p (a t)")

            phases(pe, program)


_OUTS = [((BATCH, SEQ, F), "float32")]
_INS = ["L0_attn_x", "L0_attn_Wq", "L0_attn_bq", "L0_attn_Wk", "L0_attn_bk", "L0_attn_Wv", "L0_attn_bv", "L0_attn_Wo",
        "L0_attn_bo", "L0_ffn_gate_up_packed", "L0_ffn_gate_up_scales", "L0_ffn_down_packed", "L0_ffn_down_scales"]


def kernel(**inputs):
    import numpy as _np
    import concourse.bacc as _bacc
    from concourse import mybir as _mybir
    from concourse.bass_utils import run_bass_kernel_spmd as _run

    nc = _bacc.Bacc("TRN2", target_bir_lowering=False, num_devices=1)
    arrays, args = {}, []
    for name in _INS:
        a = _np.ascontiguousarray(inputs[name])
        arrays[f"in_{name}_dram"] = a
        args.append(nc.dram_tensor(f"in_{name}_dram", a.shape, _mybir.dt.from_np(a.dtype), kind="ExternalInput").ap())
    for i, (shape, dtype) in enumerate(_OUTS):
        dt = _mybir.dt.from_np(_np.dtype(dtype))
        args.append(nc.dram_tensor(f"out_{i}_dram", shape, dt, kind="ExternalOutput").ap())
    build(nc, *args)
    r = _run(nc, [arrays], core_ids=[0])
    return r.results[0]["out_0_dram"]
```

```python
from contextlib import ExitStack

import numpy as np

import concourse.bass as bass
from concourse import mybir

P = 128
BATCH, SEQ, F = 4, 1024, 512
HEADS, HD = 8, 64
PAIRS = HEADS // 2
KT = F // P
ST = SEQ // P
NC = 512
FFN = 1408
FI = FFN // P
GROUPS = F // P
NIB = 8
LN_EPS, RMS_EPS = 1e-5, 1e-6
SCORE_SCALE = HEADS ** -0.5
UNITS = PAIRS * ST * 2
PV_UNITS = 4
LAG = 2
CHUNKS = BATCH * SEQ // NC
CT = NC // P
EARLY_V = 2
STATS_UNITS = tuple(2 + 4 * i for i in range(ST))
SCALES_UNIT = STATS_UNITS[-1] + 2
XT_UNITS = (43, 45, 46, 47, 49, 50, 51, 52)
AHEAD = 9
LATE_DOWN = AHEAD - 3


def on_gpsimd(j):
    return j % 2 == 1


class Ring:

    def __init__(self, uses, banks):
        self.number = {u: n for n, u in enumerate(uses)}
        self.bank = {u: n % banks for n, u in enumerate(uses)}
        self.turn = {u: n // banks for n, u in enumerate(uses)}
        self.total = len(uses)
        self.turns = [len(uses[k::banks]) for k in range(banks)]


def attention_schedule(last):
    filler = {g: [] for g in range(UNITS)}
    for i in range(EARLY_V, ST):
        filler[i - EARLY_V].append(("v", i))
    for c in range(UNITS // PV_UNITS - 1):
        filler[PV_UNITS * c + PV_UNITS + LAG + 1].append(("pv", c))
    per_pair = UNITS // PAIRS
    for p in range(PAIRS - 1 if last else PAIRS):
        for n, u in enumerate(((5, 8, 9, 12), (1, 5, 8, 12), (1, 4, 6, 9), (0, 6, 9, 13))[p]):
            filler[per_pair * p + u].append(("qk", (p + 1) % PAIRS, n))
    if not last:
        for i in range(ST):
            filler[XT_UNITS[i]].insert(0, ("xt", i))
    tail = []
    for i in range(ST + 2):
        if i == 2:
            tail.append(("pv", UNITS // PV_UNITS - 1))
        if i < ST:
            tail.append(("wo", i))
        elif not last:
            tail.append(("v", i - ST))
        if i >= 2:
            tail.append(("x1t", i - 2))
    return filler, tail


def build(nc, x, Wq, bq, Wk, bk, Wv, bv, Wo, bo, gu_packed, gu_scales, d_packed, d_scales, out):
    f32, f32r, i32, f16 = mybir.dt.float32, mybir.dt.float32r, mybir.dt.int32, mybir.dt.float16
    ctx = ExitStack()
    with ctx:
        ffn_values = nc.dram_tensor("ffn_values", (FI, P, 3 * F), f32, kind="Internal").ap()
        x1_scratch = nc.dram_tensor("x1_scratch", (BATCH * ST, P, F), f32, kind="Internal").ap()
        x_parts_scratch = nc.dram_tensor("x_parts_scratch", (CHUNKS, P, 2, KT, NC), f32, kind="Internal").ap()
        ident = ctx.enter_context(nc.sbuf_tensor("ident", [P, P], f32))
        consts = ctx.enter_context(nc.sbuf_tensor("consts", [P, 2 * P], f32))
        bq_scaled = ctx.enter_context(nc.sbuf_tensor("bq_scaled", [P, PAIRS], f32))
        minus_half = ctx.enter_context(nc.sbuf_tensor("minus_half", [P, 4], f32))
        consts_of = {
            "gu": lambda g, t: consts[:, g * 2 * FI + t:g * 2 * FI + t + 1],
            "down": lambda i, j: consts[:, P + i * KT + j:P + i * KT + j + 1],
            "bk": lambda p: consts[:, P + 96 + p:P + 97 + p],
            "bq": consts[:, P + 64:P + 64 + PAIRS],
        }
        with nc.sbuf_tensor("featsT", [P, PAIRS, SEQ], f32) as featsT:
            x_first = featsT[:].rearrange("p a (b f) -> p (a b) f", f=F)
            build_prep(nc, x, x_first, gu_packed, gu_scales, d_packed, d_scales, bq, bk, ident, consts, consts_of,
                       bq_scaled, minus_half, ffn_values)
            build_attention(nc, x, x_first, featsT, Wq, Wk, Wv, bv, Wo, bo, ident, consts_of, bq_scaled, minus_half,
                            x1_scratch, x_parts_scratch)
        build_ffn(nc, x1_scratch, x_parts_scratch, ffn_values, ident, consts_of, minus_half, out)


def build_prep(nc, x, x_first, gu_packed, gu_scales, d_packed, d_scales, bq, bk, ident, consts, consts_of,
               bq_scaled, minus_half, ffn_values):
    f32, i32, f16 = mybir.dt.float32, mybir.dt.int32, mybir.dt.float16
    ALU, ACT = mybir.AluOpType, mybir.ActivationFunctionType
    GW, DW = F // NIB, FFN // NIB
    WORDS = 2 * FI * GW + KT * DW
    HALF_TILES = 16
    SPANS = [(0, HALF_TILES * GW), (HALF_TILES * GW, WORDS)]
    SPAN = max(b - a for a, b in SPANS)
    STEPS = [(s, j) for s in range(len(SPANS)) for j in range(NIB)]
    TILES = [("gu", t) for t in range(2 * FI)] + [("down", i) for i in range(FI)]
    EARLY_STAGED = 2 * (NIB - 1)
    BANKS = 8
    ring = Ring(TILES, BANKS)

    ctx = ExitStack()
    with ctx:
        sb = lambda name, shape, dt: ctx.enter_context(nc.sbuf_tensor(name, shape, dt))
        sem = lambda name: ctx.enter_context(nc.semaphore(name))
        packed = sb("packed", [P, WORDS], i32)
        values = sb("values", [P, WORDS * NIB], f32)
        stage = sb("stage", [P, FI, 3 * F], f32)
        mag = sb("mag", [P, 2, SPAN], i32)
        sign = sb("sign", [P, 2, SPAN], i32)
        excess = sb("excess", [P, 2, SPAN], f32)
        factor = sb("factor", [P, 2, SPAN], f32)
        grid = sb("grid", [P, 2, SPAN], f32)
        scales16 = sb("scales16", [P, 2, P], f16)
        rows = sb("rows", [P, 2, P], f32)
        psum = ctx.enter_context(nc.psum_tensor("prep_psum", [P, BANKS, NC], f32))

        packed_loaded = [sem(f"packed_loaded{n}") for n in range(2)]
        scales_loaded = sem("scales_loaded")
        biases_loaded = sem("biases_loaded")
        rows_zeroed = sem("rows_zeroed")
        rows_cast = sem("rows_cast")
        ident_zeroed = sem("ident_zeroed")
        ident_ready = sem("ident_ready")
        consts_transposed = sem("consts_transposed")
        consts_ready = sem("consts_ready")
        codes_ready = sem("codes_ready")
        terms_ready = sem("terms_ready")
        grid_ready = sem("grid_ready")
        sum_ready = sem("sum_ready")
        values_done = sem("values_done")
        tiles_transposed = sem("tiles_transposed")
        tile_staged = [sem(f"tile_staged{k}") for k in range(BANKS)]
        values_stored = sem("values_stored")
        x_first_loaded = sem("x_first_loaded")
        block = ctx.enter_context(nc.Block(name="prep"))

        def nibble_view(span, j):
            a, b = SPANS[span]
            return values[:, a * NIB:b * NIB].rearrange("p (w j) -> p w j", j=NIB)[:, :, j]

        def staged(kind, n):
            if kind == "down":
                return stage[:, n, 2 * F:3 * F]
            return stage[:, n % FI, (n // FI) * F:(n // FI) * F + F]

        @block.sync
        def _(sp):
            gu_rows = gu_packed.rearrange("(t p) w -> p t w", p=P)
            sp.dma_start(packed[:, 0:SPANS[0][1]].rearrange("p (t w) -> p t w", w=GW),
                         gu_rows[:, 0:HALF_TILES, :]).then_inc(packed_loaded[0], 16)
            sp.dma_start(packed[:, SPANS[0][1]:2 * FI * GW].rearrange("p (t w) -> p t w", w=GW),
                         gu_rows[:, HALF_TILES:, :]).then_inc(packed_loaded[1], 16)
            sp.dma_start(packed[:, 2 * FI * GW:].rearrange("p (t w) -> p t w", w=DW),
                         d_packed.rearrange("(t p) w -> p t w", p=P)).then_inc(packed_loaded[1], 16)
            sp.dma_start(scales16[0:GROUPS * 2 * FI, 0, :],
                         gu_scales.rearrange("g (t p) -> (g t) p", p=P)).then_inc(scales_loaded, 16)
            sp.dma_start(scales16[0:FI * KT, 1, :],
                         d_scales.rearrange("g (t p) -> (g t) p", p=P)).then_inc(scales_loaded, 16)
            sp.wait_ge(rows_zeroed, 1)
            sp.dma_start(rows[64:64 + PAIRS, 1, :], bq.rearrange("(t p) -> t p", p=P)).then_inc(biases_loaded, 16)
            sp.dma_start(rows[96:96 + PAIRS, 1, :], bk.rearrange("(t p) -> t p", p=P)).then_inc(biases_loaded, 16)
            sp.dma_start(x_first[:], x[0].rearrange("(t p) f -> p t f", p=P)).then_inc(x_first_loaded, 16)
            for use in TILES:
                kind, t = use
                i, third = (t, 2) if kind == "down" else (t % FI, t // FI)
                sp.wait_ge(tile_staged[ring.bank[use]], ring.turn[use] + 1)
                sp.dma_start(ffn_values[i][:, third * F:(third + 1) * F], staged(*use)).then_inc(values_stored, 16)
            sp.wait_ge(values_stored, 16 * len(TILES))
            sp.wait_ge(x_first_loaded, 16)

        @block.gpsimd
        def _(pool):
            nc.gpsimd.memset(minus_half[:], -0.5)
            nc.gpsimd.memset(ident[:], 0.0).then_inc(ident_zeroed, 1)
            pool.wait_ge(ident_zeroed, 1)
            nc.gpsimd.affine_select(out=ident[:], in_=ident[:], compare_op=ALU.not_equal, fill=1.0, base=0,
                                    pattern=[[-1, P]], channel_multiplier=1).then_inc(ident_ready, 1)
            for k, (span, j) in enumerate(STEPS):
                n = SPANS[span][1] - SPANS[span][0]
                pool.wait_ge(terms_ready, k + 1)
                pool.wait_ge(grid_ready, k + 1)
                nc.gpsimd.tensor_tensor(grid[:, k % 2, 0:n], grid[:, k % 2, 0:n], excess[:, k % 2, 0:n],
                                        ALU.subtract).then_inc(sum_ready, 1)

        @block.scalar
        def _(act):
            def stage_tile(n):
                use = TILES[n]
                act.wait_ge(tiles_transposed, n + 1)
                nc.scalar.activation(staged(*use), psum[:, ring.bank[use], :],
                                     ACT.Copy).then_inc(tile_staged[ring.bank[use]], 1)

            for k, (span, j) in enumerate(STEPS):
                n = SPANS[span][1] - SPANS[span][0]
                act.wait_ge(codes_ready, k + 1)
                if k >= 2:
                    act.wait_ge(values_done, k - 1)
                s = k % 2
                nc.scalar.activation(excess[:, s, 0:n], mag[:, s, 0:n], ACT.Relu, bias=0.125, scale=-0.0625)
                nc.scalar.activation(factor[:, s, 0:n], sign[:, s, 0:n], ACT.Copy, bias=4.0,
                                     scale=-1.0).then_inc(terms_ready, 1)
                if k > NIB:
                    for n in range(2 * (k - NIB - 1), 2 * (k - NIB)):
                        stage_tile(n)
            for n in range(EARLY_STAGED, len(TILES), 2):
                stage_tile(n)

        @block.vector
        def _(dve):
            def codes(k):
                span, j = STEPS[k]
                a, b = SPANS[span]
                if j == 0:
                    dve.wait_ge(packed_loaded[span], 16 if span == 0 else 32)
                nc.vector.tensor_scalar(mag[:, k % 2, 0:b - a], packed[:, a:b], 4 * j, 7,
                                        ALU.logical_shift_right, ALU.bitwise_and)
                nc.vector.tensor_scalar(sign[:, k % 2, 0:b - a], packed[:, a:b], 4 * j, 8,
                                        ALU.logical_shift_right, ALU.bitwise_and).then_inc(codes_ready, 1)

            def stage_tile(n):
                use = TILES[n]
                dve.wait_ge(tiles_transposed, n + 1)
                nc.vector.tensor_copy(staged(*use), psum[:, ring.bank[use], :]).then_inc(
                    tile_staged[ring.bank[use]], 1)

            nc.vector.memset(rows[:], 0.0).then_inc(rows_zeroed, 1)
            dve.wait_ge(scales_loaded, 32)
            dve.wait_ge(rows_zeroed, 1)
            nc.vector.tensor_copy(rows[0:GROUPS * 2 * FI, 0, :], scales16[0:GROUPS * 2 * FI, 0, :])
            nc.vector.tensor_copy(rows[0:FI * KT, 1, :], scales16[0:FI * KT, 1, :]).then_inc(rows_cast, 1)
            codes(0)
            dve.wait_ge(consts_transposed, 1)
            nc.vector.tensor_copy(consts[:], psum[:, 0, 0:2 * P]).then_inc(consts_ready, 1)
            dve.wait_ge(consts_ready, 1)
            nc.vector.tensor_scalar(bq_scaled[:], consts_of["bq"], SCORE_SCALE, None,
                                    ALU.mult).then_inc(consts_ready, 1)
            for k in range(len(STEPS) + 1):
                if k + 1 < len(STEPS):
                    if k:
                        dve.wait_ge(terms_ready, k)
                        dve.wait_ge(grid_ready, k)
                    codes(k + 1)
                if k < len(STEPS):
                    n = SPANS[STEPS[k][0]][1] - SPANS[STEPS[k][0]][0]
                    dve.wait_ge(codes_ready, k + 1)
                    if k >= 2:
                        dve.wait_ge(values_done, k - 1)
                    nc.vector.tensor_scalar(grid[:, k % 2, 0:n].bitcast(i32), mag[:, k % 2, 0:n], 22, 124 << 23,
                                            ALU.logical_shift_left, ALU.bitwise_or).then_inc(grid_ready, 1)
                if k:
                    span, j = STEPS[k - 1]
                    n, s = SPANS[span][1] - SPANS[span][0], (k - 1) % 2
                    dve.wait_ge(sum_ready, k)
                    nc.vector.tensor_tensor(nibble_view(span, j), grid[:, s, 0:n], factor[:, s, 0:n],
                                            ALU.mult).then_inc(values_done, 1)
            for n in range(EARLY_STAGED + 1, len(TILES), 2):
                stage_tile(n)

        @block.tensor
        def _(pe):
            pe.wait_ge(ident_ready, 1)
            pe.wait_ge(rows_cast, 1)
            pe.wait_ge(biases_loaded, 32)
            nc.tensor.transpose(psum[:, 0, 0:P], rows[:, 0, :], ident[:])
            nc.tensor.transpose(psum[:, 0, P:2 * P], rows[:, 1, :], ident[:]).then_inc(consts_transposed, 1)
            pe.wait_ge(consts_ready, 1)
            for n, (kind, t) in enumerate(TILES):
                if n == 0:
                    pe.wait_ge(values_done, NIB)
                if n == HALF_TILES:
                    pe.wait_ge(values_done, 2 * NIB)
                if ring.turn[kind, t]:
                    pe.wait_ge(tile_staged[ring.bank[kind, t]], ring.turn[kind, t])
                for q in range(4):
                    at = t * F + q * P if kind == "gu" else 2 * FI * F + q * FFN + t * P
                    last = nc.tensor.transpose(psum[:, ring.bank[kind, t], q * P:(q + 1) * P],
                                               values[:, at:at + P], ident[:])
                last.then_inc(tiles_transposed, 1)


def build_attention(nc, x, x_first, featsT, Wq, Wk, Wv, bv, Wo, bo, ident, consts_of, bq_scaled, minus_half,
                    x1_scratch, x_parts_scratch):
    f32, f32r = mybir.dt.float32, mybir.dt.float32r
    ALU, ACT, AX = mybir.AluOpType, mybir.ActivationFunctionType, mybir.AxisListType
    schedule, last_schedule = attention_schedule(False), attention_schedule(True)
    PER_PAIR = UNITS // PAIRS
    PV_CHUNKS = UNITS // PV_UNITS
    PV_TOKENS = PV_UNITS // 2 * P
    first = Ring([("xt", i) for i in range(ST)] + [("qk", 0, n) for n in range(4)]
                 + [("v", i) for i in range(EARLY_V)], 2)
    body, last_row = (Ring([u for g in range(UNITS) for u in filler[g]] + [u for u in tail if u[0] != "x1t"], 2)
                      for filler, tail in (schedule, last_schedule))
    assert first.total % 2 == 0 and body.total % 2 == 0
    qk_order = {u: n for n, u in enumerate(u for g in range(UNITS) for u in schedule[0][g] if u[0] == "qk")}
    PROBS = 4

    ctx = ExitStack()
    with ctx:
        sb = lambda name, shape, dt=f32: ctx.enter_context(nc.sbuf_tensor(name, shape, dt))
        sem = lambda name: ctx.enter_context(nc.semaphore(name))
        wq, wk, wv, wo = (sb(n, [P, KT, F]) for n in ("wq", "wk", "wv", "wo"))
        bv_rows, bo_rows = sb("bv_rows", [P, F]), sb("bo_rows", [P, F])
        x_in = sb("x_in", [P, 2, F])
        stats = sb("stats", [P, ST, 6])
        mean_var = sb("mean_var", [P, ST, 2])
        var_eps = sb("var_eps", [P, ST])
        rstd = sb("rstd", [P, ST])
        shift = sb("shift", [P, ST])
        xn = sb("xn", [P, 2, F])
        xnT = sb("xnT", [P, KT, SEQ])
        qk_full = sb("qk_full", [P, 2, NC])
        q_parts = [sb(f"q_parts{n}", [P, 2, SEQ], f32r) for n in range(2)]
        k_high = [sb(f"k_high{n}", [P, 2, SEQ], f32r) for n in range(2)]
        k_low = [sb(f"k_low{n}", [P, 2, SEQ], f32r) for n in range(2)]
        v = sb("v", [P, ST, F])
        neg_max = sb("neg_max", [P, PROBS, 1])
        sums = sb("sums", [P, 2, PV_UNITS])
        recip = sb("recip", [P, 2, PV_UNITS])
        recip_wide = sb("recip_wide", [P, 2, PV_UNITS, HD])
        probs = sb("probs", [P, PROBS, SEQ])
        probsT = sb("probsT", [P, 2, ST, 2, PV_TOKENS])
        recip_cols = sb("recip_cols", [P, 2, PV_TOKENS])
        residual = sb("residual", [P, 2, F])
        x1_out = sb("x1_out", [P, 2, F])
        x1_stats = sb("x1_stats", [P, 2, 6])
        x1_mean_var = sb("x1_mean_var", [P, 2, 2])
        x1_var_eps = sb("x1_var_eps", [P, 2, 1])
        x1_minus_mean = sb("x1_minus_mean", [P, 2, 1])
        x1_rstd = sb("x1_rstd", [P, 2, 1])
        x1_shift = sb("x1_shift", [P, 2, 1])
        x1n = xn
        x1_parts = probs[:, PROBS - 2:, :].bitcast(f32r).rearrange("p s (n k t) -> p s n k t", n=2, k=KT)
        score_psum = ctx.enter_context(nc.psum_tensor("score_psum", [P, 2, SEQ], f32))
        transpose_psum = ctx.enter_context(nc.psum_tensor("transpose_psum", [P, 2, NC], f32))
        general_psum = ctx.enter_context(nc.psum_tensor("general_psum", [P, 2, NC], f32))

        wqk_loaded, wv_loaded, wo_loaded = sem("wqk_loaded"), sem("wv_loaded"), sem("wo_loaded")
        x_loaded = [sem(f"x_loaded{n}") for n in range(2)]
        first_step = sem("first_step")
        first_var_ready = sem("first_var_ready")
        first_rstd_ready = sem("first_rstd_ready")
        first_shift_ready = sem("first_shift_ready")
        residual_loaded = [sem(f"residual_loaded{n}") for n in range(2)]
        stored = [sem(f"x1_stored{n}") for n in range(2)]
        last_row_stored = sem("last_row_stored")
        parts_stored = [sem(f"x1_parts_stored{n}") for n in range(2)]
        x1_step, x1_stats_seen = sem("x1_step"), sem("x1_stats_seen")
        x1_rstd_ready = sem("x1_rstd_ready")
        x1_shift_ready = sem("x1_shift_ready")
        x1_norm_done = sem("x1_norm_done")
        x1_transposed = sem("x1_transposed")
        x1_high_ready = sem("x1_high_ready")
        x1_split = sem("x1_split")
        residual_ready = sem("residual_ready")
        stats_step, stats_seen = sem("stats_step"), sem("stats_seen")
        var_ready = sem("var_ready")
        rstd_ready = sem("rstd_ready")
        shift_ready = sem("shift_ready")
        norm_done = sem("norm_done")
        high_ready = sem("high_ready")
        low_ready = sem("low_ready")
        scores_done = sem("scores_done")
        max_ready = sem("max_ready")
        exp_done = sem("exp_done")
        transposed = sem("transposed")
        copied_low = sem("copied_low")
        copied_high = sem("copied_high")
        recip_step = sem("recip_step")
        recip_ready = sem("recip_ready")
        cols_ready = sem("cols_ready")
        general_done = sem("general_done")
        emptied = [sem(f"general_emptied{n}") for n in range(2)]
        block = ctx.enter_context(nc.Block(name="attention"))

        def ring_of(b):
            return first if b is None else last_row if isinstance(b, int) else body

        def done(use, b=None):
            if b is None:
                return first.number[use] + 1
            return b * body.total + (first.total + ring_of(b).number[use] + 1)

        def empty(use, b=None):
            if b is None:
                return first.turn[use] + 1
            return b * body.turns[0] + (first.turns[0] + ring_of(b).turn[use] + 1)

        def batch_rows(eng, program):
            with eng.Fori(0, BATCH - 1) as b:
                program(b, *schedule)
            program(BATCH - 1, *last_schedule)

        QK_ROW = 4 * PAIRS

        def low_ops(n):
            return n // 4 * 12 + (0, 2, 4, 8)[n % 4]

        def unit(g):
            return g // PER_PAIR, g % PER_PAIR // 2, g % 2

        def place(c):
            p, n = c // (PV_CHUNKS // PAIRS), c % (PV_CHUNKS // PAIRS)
            return p, slice(n * PV_TOKENS, (n + 1) * PV_TOKENS)

        x_tiles = x.rearrange("b (t p) f -> (b t) p f", p=P)

        def tile_at(ap, n):
            return ap[bass.ds(n, 1)].rearrange("a p f -> (a p) f")

        @block.sync
        def _(sp):
            def load_x(m, b):
                if m < 2:
                    sp.wait_ge(norm_done, b * ST + (ST + m - 1))
                elif m < ST + 2:
                    sp.wait_ge(stats_step, b * (2 * ST) + (2 * (m - 2) + 1))
                else:
                    sp.wait_ge(norm_done, b * ST + (ST + (m - 2 - ST) + 1))
                sp.dma_start(x_in[:, m % 2, :], tile_at(x_tiles, (b + 1) * ST + m % ST)).then_inc(x_loaded[m % 2], 16)

            def store_parts(b, i):
                sp.wait_ge(x1_split, b * ST + (1 + i + 1))
                chunk = x_parts_scratch[bass.ds(b * (ST // CT) + i // CT, 1)].rearrange("a p n k t -> (a p) n k t")
                for part in range(2):
                    sp.dma_start(chunk[:, part, :, i % CT * P:(i % CT + 1) * P],
                                 x1_parts[:, i % 2, part].bitcast(f32)).then_inc(parts_stored[i % 2], 16)

            sp.dma_start(wq[:], Wq.rearrange("(t p) n -> p t n", p=P)).then_inc(wqk_loaded, 16)
            sp.dma_start(wk[:], Wk.rearrange("(t p) n -> p t n", p=P)).then_inc(wqk_loaded, 16)
            sp.dma_start(wv[:], Wv.rearrange("(t p) n -> p t n", p=P)).then_inc(wv_loaded, 16)
            sp.dma_start(bv_rows[:], bv.rearrange("(a n) -> a n", a=1).to_broadcast([P, F])).then_inc(wv_loaded, 16)
            sp.dma_start(wo[:], Wo.rearrange("(t p) n -> p t n", p=P)).then_inc(wo_loaded, 16)
            sp.dma_start(bo_rows[:], bo.rearrange("(a n) -> a n", a=1).to_broadcast([P, F])).then_inc(wo_loaded, 16)
            sp.sem_inc(last_row_stored, 1)
            def program(b, filler, tail):
                for i in range(2):
                    sp.dma_start(residual[:, i, :], tile_at(x_tiles, b * ST + i)).then_inc(residual_loaded[i], 16)
                if not isinstance(b, int):
                    for m in range(2 * ST):
                        load_x(m, b)
                for i in range(ST):
                    use = ("wo", i)
                    sp.wait_ge(emptied[ring_of(b).bank[use]], empty(use, b))
                    sp.dma_start(tile_at(x1_scratch, b * ST + i), x1_out[:, i % 2, :]).then_inc(stored[i % 2], 16)
                    if i + 2 < ST:
                        sp.dma_start(residual[:, i % 2, :],
                                     tile_at(x_tiles, b * ST + (i + 2))).then_inc(residual_loaded[i % 2], 16)
                    if i >= 2:
                        store_parts(b, i - 2)
                for i in range(ST - 2, ST):
                    store_parts(b, i)
                for n in range(2):
                    sp.wait_ge(stored[n], b * (16 * ST // 2) + 16 * ST // 2)
                    sp.wait_ge(parts_stored[n], b * (32 * ST // 2) + 32 * ST // 2)
                sp.sem_inc(last_row_stored, 1)

            batch_rows(sp, program)

        @block.gpsimd
        def _(pool):
            def low_parts(use, count, ops_before):
                _, p, n = use
                s, tok = p % 2, slice(n % 2 * NC, (n % 2 + 1) * NC)
                pool.wait_ge(high_ready, count)
                parts = q_parts[s] if n < 2 else k_high[s]
                low = q_parts[s] if n < 2 else k_low[s]
                for h in range(2):
                    own, other = slice(h * HD, (h + 1) * HD), slice((1 - h) * HD, (2 - h) * HD)
                    for m, rows in enumerate((other,) if n < 2 else (own, other)):
                        nc.gpsimd.tensor_tensor(low[rows, h, tok], qk_full[own, n % 2, :],
                                                parts[own, h, tok].bitcast(f32), ALU.subtract
                                                ).then_inc(low_ready, 1)
                        pool.wait_ge(low_ready, ops_before + ((1 if n < 2 else 2) * h + m + 1))

            def scale_of_x1(i, b):
                s = i % 2
                pool.wait_ge(x1_step, b * (4 * ST) + (4 * i + 4))
                nc.gpsimd.tensor_tensor(x1_rstd[:, s, :], x1_var_eps[:, s, :], minus_half[:, 0:1],
                                        ALU.pow).then_inc(x1_rstd_ready, 1)
                pool.wait_ge(x1_rstd_ready, b * ST + (i + 1))
                nc.gpsimd.tensor_tensor(x1_shift[:, s, :], x1_minus_mean[:, s, :], x1_rstd[:, s, :],
                                        ALU.mult).then_inc(x1_shift_ready, 1)

            for half in range(2):
                tiles = slice(half * ST // 2, (half + 1) * ST // 2)
                pool.wait_ge(first_var_ready, half + 1)
                nc.gpsimd.tensor_tensor(rstd[:, tiles], var_eps[:, tiles], minus_half[:], ALU.pow
                                        ).then_inc(first_rstd_ready, 1)
            for n in range(4):
                low_parts(("qk", 0, n), n + 1, low_ops(n))
            pool.wait_ge(wo_loaded, 32)
            def program(b, filler, tail):
                for g in range(UNITS):
                    if g == SCALES_UNIT and not isinstance(b, int):
                        for half in range(2):
                            tiles = slice(half * ST // 2, (half + 1) * ST // 2)
                            pool.wait_ge(var_ready, b + 1)
                            nc.gpsimd.tensor_tensor(rstd[:, tiles], var_eps[:, tiles], minus_half[:], ALU.pow
                                                    ).then_inc(rstd_ready, 1)
                        pool.wait_ge(rstd_ready, b * 2 + 2)
                    for use in filler[g]:
                        if use[0] == "qk":
                            low_parts(use, b * QK_ROW + (4 + qk_order[use] + 1),
                                      b * low_ops(QK_ROW) + low_ops(4 + qk_order[use]))
                for i in range(ST + 1):
                    if i < ST:
                        pool.wait_ge(residual_loaded[i % 2], b * (16 * ST // 2) + 16 * (i // 2 + 1))
                        nc.gpsimd.tensor_tensor(residual[:, i % 2, :], residual[:, i % 2, :], bo_rows[:],
                                                ALU.add).then_inc(residual_ready, 1)
                    if i:
                        scale_of_x1(i - 1, b)

            batch_rows(pool, program)

        @block.scalar
        def _(act):
            def copy_out(use, b=None, split=None):
                kind = use[0]
                bank = ring_of(b).bank[use]
                if kind == "xt":
                    act.wait_ge(general_done, done(use, b))
                    i = use[1]
                    nc.scalar.activation(xnT[:, :, i * P:(i + 1) * P], general_psum[:, bank, :].rearrange(
                        "p (k t) -> p k t", k=KT), ACT.Copy).then_inc(emptied[bank], 1)
                if kind == "qk":
                    _, p, n = use
                    act.wait_ge(general_done, done(use, b))
                    if split is not None:
                        act.wait_ge(low_ready, split)
                    bias, scale = (bq_scaled[:, p:p + 1], SCORE_SCALE) if n < 2 else (consts_of["bk"](p), 1.0)
                    nc.scalar.activation(qk_full[:, n % 2, :], general_psum[:, bank, :], ACT.Identity, bias=bias,
                                         scale=scale).then_inc(emptied[bank], 1)
                if kind == "pv":
                    c = use[1]
                    act.wait_ge(general_done, done(use, b))
                    nc.scalar.activation(recip_cols[:, c % 2, :], general_psum[:, bank, PV_TOKENS:],
                                         ACT.Copy).then_inc(cols_ready, 1)

            def copy_transposed(g, b):
                _, st, h = unit(g)
                c = g // PV_UNITS
                act.wait_ge(transposed, b * (2 * UNITS) + (2 * PROBS + 2 * g + 1))
                nc.scalar.activation(probsT[:, c % 2, 0:4, h, st % 2 * P:(st % 2 + 1) * P],
                                     transpose_psum[:, 0, :].rearrange("p (k t) -> p k t", k=4),
                                     ACT.Copy).then_inc(copied_low, 1)

            def normalise_x1(i, b):
                act.wait_ge(x1_shift_ready, b * ST + (i + 1))
                nc.scalar.activation(x1n[:, i % 2, :], x1_out[:, i % 2, :], ACT.Identity, bias=x1_shift[:, i % 2, :],
                                     scale=x1_rstd[:, i % 2, :]).then_inc(x1_norm_done, 1)

            def high_x1(i, b):
                if i < 2:
                    act.wait_ge(last_row_stored, b + 1)
                else:
                    act.wait_ge(parts_stored[i % 2], b * (32 * ST // 2) + 32 * (i // 2))
                act.wait_ge(x1_transposed, b * ST + (i + 1))
                nc.scalar.activation(x1_parts[:, i % 2, 0], transpose_psum[:, i % 2, :].rearrange(
                    "p (k t) -> p k t", k=KT), ACT.Copy).then_inc(x1_high_ready, 1)

            act.sem_inc(exp_done, 2)
            act.sem_inc(copied_low, 1)
            for i in range(ST):
                copy_out(("xt", i))
            for n in range(4):
                copy_out(("qk", 0, n), None, low_ops(n - 1) if n >= 2 else None)
            def program(b, filler, tail):
                for g in range(UNITS + LAG):
                    short = g >= UNITS or not filler[g]
                    if g >= LAG and short:
                        copy_transposed(g - LAG, b)
                    if g < UNITS:
                        act.wait_ge(max_ready, b * UNITS + (g + 1))
                        if g == PROBS - 2:
                            act.wait_ge(last_row_stored, b + 1)
                        act.wait_ge(transposed, b * (2 * UNITS) + (2 * g + 2))
                        nc.scalar.activation(probs[:, g % PROBS, :], score_psum[:, g % 2, :], ACT.Exp,
                                             bias=neg_max[:, g % PROBS, :],
                                             accum_out=sums[:, g // PV_UNITS % 2, g % PV_UNITS:g % PV_UNITS + 1],
                                             ).then_inc(exp_done, 1)
                        for use in filler[g]:
                            copy_out(use, b, b * low_ops(QK_ROW) + low_ops(3 + qk_order[use])
                                     if use[0] == "qk" else None)
                    if g >= LAG and not short:
                        copy_transposed(g - LAG, b)
                for n, use in enumerate(tail):
                    if use[0] == "pv":
                        copy_out(use, b)
                    if use[0] == "x1t":
                        high_x1(use[1], b)
                    if n and tail[n - 1][0] == "wo":
                        normalise_x1(tail[n - 1][1], b)

            batch_rows(act, program)

        @block.vector
        def _(dve):
            def tile_stats(i, b):
                step = b * (2 * ST) + 2 * i
                dve.wait_ge(x_loaded[i % 2], b * (16 * ST) + 16 * (i // 2 + 1))
                nc.vector.bn_stats(stats[:, i, :], x_in[:, i % 2, :]).then_inc(stats_step, 1)
                dve.wait_ge(stats_step, step + 1)
                dve.sem_inc(stats_seen, 1)
                nc.vector.bn_aggr(mean_var[:, i, :], stats[:, i, :]).then_inc(stats_step, 1)

            def variances(b):
                dve.wait_ge(stats_step, b * (2 * ST) + 2 * ST)
                nc.vector.tensor_scalar(var_eps[:], mean_var[:, :, 1], LN_EPS, None, ALU.add).then_inc(var_ready, 1)

            def shifts(b):
                dve.wait_ge(rstd_ready, b * 2 + 2)
                nc.vector.scalar_tensor_tensor(shift[:], mean_var[:, :, 0], -1.0, rstd[:], ALU.mult,
                                               ALU.mult).then_inc(shift_ready, 1)

            def normalise(i, b):
                dve.wait_ge(x_loaded[i % 2], b * (16 * ST) + 16 * (ST // 2 + i // 2 + 1))
                if i == 0:
                    dve.wait_ge(shift_ready, b + 1)
                if i >= 2:
                    dve.wait_ge(general_done, done(("xt", i - 2), b))
                nc.vector.tensor_scalar(xn[:, i % 2, :], x_in[:, i % 2, :], rstd[:, i:i + 1], shift[:, i:i + 1],
                                        ALU.mult, ALU.add).then_inc(norm_done, 1)

            def high_parts(use, b=None):
                _, p, n = use
                s, tok = p % 2, slice(n % 2 * NC, (n % 2 + 1) * NC)
                dve.wait_ge(emptied[ring_of(b).bank[use]], empty(use, b))
                high = q_parts[s] if n < 2 else k_high[s]
                for h in range(2):
                    own, other = slice(h * HD, (h + 1) * HD), slice((1 - h) * HD, (2 - h) * HD)
                    for rows in ((own,) if n < 2 else (own, other)):
                        last = nc.vector.tensor_copy(high[rows, h, tok], qk_full[own, n % 2, :])
                last.then_inc(high_ready, 1)

            def copy_out(use, b=None):
                kind, bank = use[0], ring_of(b).bank.get(use)
                if kind == "v":
                    dve.wait_ge(general_done, done(use, b))
                    nc.vector.tensor_tensor(v[:, use[1], :], general_psum[:, bank, :], bv_rows[:],
                                            ALU.add).then_inc(emptied[bank], 1)
                if kind == "pv":
                    c = use[1]
                    p, tok = place(c)
                    dve.wait_ge(cols_ready, b * PV_CHUNKS + (c + 1))
                    nc.vector.tensor_tensor(featsT[:, p, tok], general_psum[:, bank, 0:PV_TOKENS],
                                            recip_cols[:, c % 2, :], ALU.mult).then_inc(emptied[bank], 1)
                if kind == "wo":
                    i = use[1]
                    dve.wait_ge(general_done, done(use, b))
                    dve.wait_ge(residual_ready, b * ST + (i + 1))
                    if i < 2:
                        dve.wait_ge(last_row_stored, b + 1)
                    else:
                        dve.wait_ge(stored[i % 2], b * (16 * ST // 2) + 16 * (i // 2))
                        dve.wait_ge(x1_norm_done, b * ST + (i - 1))
                    nc.vector.tensor_tensor(x1_out[:, i % 2, :], general_psum[:, bank, :], residual[:, i % 2, :],
                                            ALU.add).then_inc(emptied[bank], 1)
                    stats_of_x1(use, b)
                if kind == "x1t":
                    i = use[1]
                    dve.wait_ge(x1_high_ready, b * ST + (i + 1))
                    nc.vector.tensor_tensor(x1_parts[:, i % 2, 1], transpose_psum[:, i % 2, :].rearrange(
                        "p (k t) -> p k t", k=KT), x1_parts[:, i % 2, 0].bitcast(f32), ALU.subtract
                        ).then_inc(x1_split, 1)

            def stats_of_x1(use, b):
                i = use[1]
                s, before = i % 2, b * (4 * ST) + 4 * i
                dve.wait_ge(emptied[ring_of(b).bank[use]], empty(use, b))
                nc.vector.bn_stats(x1_stats[:, s, :], x1_out[:, s, :]).then_inc(x1_step, 1)
                dve.wait_ge(x1_step, before + 1)
                dve.sem_inc(x1_stats_seen, 1)
                nc.vector.bn_aggr(x1_mean_var[:, s, :], x1_stats[:, s, :]).then_inc(x1_step, 1)
                dve.wait_ge(x1_step, before + 2)
                nc.vector.tensor_scalar(x1_var_eps[:, s, :], x1_mean_var[:, s, 1:2], LN_EPS, None,
                                        ALU.add).then_inc(x1_step, 1)
                nc.vector.tensor_scalar(x1_minus_mean[:, s, :], x1_mean_var[:, s, 0:1], -1.0, None,
                                        ALU.mult).then_inc(x1_step, 1)

            def copy_transposed(g, b):
                _, st, h = unit(g)
                c = g // PV_UNITS
                dve.wait_ge(transposed, b * (2 * UNITS) + (2 * PROBS + 2 * g + 2))
                nc.vector.tensor_copy(probsT[:, c % 2, 4:8, h, st % 2 * P:(st % 2 + 1) * P],
                                      transpose_psum[:, 1, :].rearrange("p (k t) -> p k t", k=4)
                                      ).then_inc(copied_high, 1)
                if g % PV_UNITS == PV_UNITS - 1:
                    dve.wait_ge(exp_done, b * UNITS + (2 + g + 1))
                    nc.vector.reciprocal(recip[:, c % 2, :], sums[:, c % 2, :]).then_inc(recip_step, 1)
                    dve.wait_ge(recip_step, b * PV_CHUNKS + (c + 1))
                    nc.vector.tensor_copy(recip_wide[:, c % 2], recip[:, c % 2, :].rearrange(
                        "p (u o) -> p u o", o=1).to_broadcast([P, PV_UNITS, HD])).then_inc(recip_ready, 1)

            dve.sem_inc(copied_high, 1)
            dve.sem_inc(x1_split, 1)
            def first_statistics(half):
                tiles = range(half * ST // 2, (half + 1) * ST // 2)
                span = slice(tiles[0], tiles[-1] + 1)
                for i in tiles:
                    nc.vector.bn_stats(stats[:, i, :], x_first[:, i, :]).then_inc(first_step, 1)
                dve.wait_ge(first_step, half * ST + ST // 2)
                for i in tiles:
                    nc.vector.bn_aggr(mean_var[:, i, :], stats[:, i, :]).then_inc(first_step, 1)
                dve.wait_ge(first_step, half * ST + ST)
                nc.vector.tensor_scalar(var_eps[:, span], mean_var[:, span, 1], LN_EPS, None,
                                        ALU.add).then_inc(first_var_ready, 1)

            def first_normalise(half):
                tiles = range(half * ST // 2, (half + 1) * ST // 2)
                span = slice(tiles[0], tiles[-1] + 1)
                dve.wait_ge(first_rstd_ready, half + 1)
                nc.vector.scalar_tensor_tensor(shift[:, span], mean_var[:, span, 0], -1.0,
                                               rstd[:, span], ALU.mult, ALU.mult).then_inc(first_shift_ready, 1)
                dve.wait_ge(first_shift_ready, half + 1)
                for i in tiles:
                    if i >= 2:
                        dve.wait_ge(general_done, done(("xt", i - 2)))
                    nc.vector.tensor_scalar(xn[:, i % 2, :], x_first[:, i, :], rstd[:, i:i + 1],
                                            shift[:, i:i + 1], ALU.mult, ALU.add).then_inc(norm_done, 1)

            for half in range(2):
                first_statistics(half)
            for half in range(2):
                first_normalise(half)
            for n in range(4):
                high_parts(("qk", 0, n))
            dve.wait_ge(wv_loaded, 32)
            for i in range(EARLY_V):
                copy_out(("v", i))
            def program(b, filler, tail):
                for g in range(UNITS + LAG):
                    if g < UNITS:
                        dve.wait_ge(scores_done, b * UNITS + (g + 1))
                        nc.vector.tensor_reduce(neg_max[:, g % PROBS, :], score_psum[:, g % 2, :], AX.X, ALU.max,
                                                negate=True).then_inc(max_ready, 1)
                        for use in filler[g]:
                            copy_out(use, b)
                    if g >= LAG:
                        copy_transposed(g - LAG, b)
                    if g < UNITS:
                        for use in filler[g - 1] if g else []:
                            if use[0] == "qk":
                                high_parts(use, b)
                        if not isinstance(b, int):
                            if g in STATS_UNITS:
                                tile_stats(STATS_UNITS.index(g), b)
                            if g == SCALES_UNIT:
                                variances(b)
                            if g == SCALES_UNIT + 6:
                                shifts(b)
                            if g + 2 in XT_UNITS:
                                normalise(XT_UNITS.index(g + 2), b)
                for use in tail:
                    copy_out(use, b)

            batch_rows(dve, program)

        @block.tensor
        def _(pe):
            def project(use, b=None):
                ring = ring_of(b)
                bank = ring.bank[use]
                out_bank = general_psum[:, bank, :]
                if b is not None:
                    pe.wait_ge(emptied[bank], b * body.turns[0] + (first.turns[0] + ring.turn[use]))
                elif first.turn[use]:
                    pe.wait_ge(emptied[bank], first.turn[use])
                kind = use[0]
                if kind == "xt":
                    i = use[1]
                    pe.wait_ge(norm_done, (i + 1) if b is None else b * ST + (ST + i + 1))
                    for k in range(KT):
                        last = nc.tensor.transpose(out_bank[:, k * P:(k + 1) * P], xn[:, i % 2, k * P:(k + 1) * P],
                                                   ident[:])
                elif kind == "qk":
                    _, p, n = use
                    w = wq if n < 2 else wk
                    for k in range(KT):
                        last = nc.tensor.matmul(out_bank, w[:, k, p * P:(p + 1) * P],
                                                xnT[:, k, n % 2 * NC:(n % 2 + 1) * NC], start=k == 0,
                                                stop=k == KT - 1)
                elif kind == "v":
                    i = use[1]
                    for k in range(KT):
                        last = nc.tensor.matmul(out_bank, xnT[:, k, i * P:(i + 1) * P], wv[:, k, :], start=k == 0,
                                                stop=k == KT - 1)
                elif kind == "pv":
                    c = use[1]
                    p, _ = place(c)
                    g = c * PV_UNITS + PV_UNITS - 1
                    pe.wait_ge(copied_low, b * UNITS + (1 + g + 1))
                    pe.wait_ge(copied_high, b * UNITS + (1 + g + 1))
                    for t in range(ST):
                        for h in range(2):
                            nc.tensor.matmul(out_bank[h * HD:(h + 1) * HD, 0:PV_TOKENS],
                                             v[:, t, p * P + h * HD:p * P + (h + 1) * HD],
                                             probsT[:, c % 2, t, h, :], start=t == 0, stop=t == ST - 1)
                    pe.wait_ge(recip_ready, b * PV_CHUNKS + (c + 1))
                    for m in range(PV_UNITS // 2):
                        last = nc.tensor.transpose(out_bank[:, PV_TOKENS + m * P:PV_TOKENS + (m + 1) * P],
                                                   recip_wide[:, c % 2, 2 * m:2 * m + 2, :].rearrange(
                                                       "p u d -> p (u d)"), ident[:])
                elif kind == "wo":
                    i = use[1]
                    if i == ST - 2:
                        feats = ("pv", PV_CHUNKS - 1)
                        pe.wait_ge(emptied[ring.bank[feats]], empty(feats, b))
                    for p in range(PAIRS):
                        last = nc.tensor.matmul(out_bank, featsT[:, p, i * P:(i + 1) * P], wo[:, p, :],
                                                start=p == 0, stop=p == PAIRS - 1)
                last.then_inc(general_done, 1)

            def scores(g, b):
                p, st, h = unit(g)
                s = p % 2
                if g % PER_PAIR == 0:
                    pe.wait_ge(low_ready, b * low_ops(QK_ROW) + low_ops(4 * (p + 1)))
                pe.wait_ge(exp_done, b * UNITS + (g + 1))
                for n in range(2):
                    for k_part in (k_high, k_low):
                        last = nc.tensor.matmul(score_psum[:, g % 2, n * NC:(n + 1) * NC],
                                                q_parts[s][:, h, st * P:(st + 1) * P],
                                                k_part[s][:, h, n * NC:(n + 1) * NC], start=k_part is k_high,
                                                stop=k_part is k_low)
                last.then_inc(scores_done, 1)

            def transpose_x1(i, b):
                if i >= 2:
                    pe.wait_ge(x1_split, b * ST + (1 + i - 1))
                pe.wait_ge(x1_norm_done, b * ST + (i + 1))
                for k in range(KT):
                    last = nc.tensor.transpose(transpose_psum[:, i % 2, k * P:(k + 1) * P],
                                               x1n[:, i % 2, k * P:(k + 1) * P], ident[:])
                last.then_inc(x1_transposed, 1)

            def transposes(g, b):
                pe.wait_ge(exp_done, b * UNITS + (2 + g + 1))
                if g == 0:
                    pe.wait_ge(x1_split, b * ST + 1)
                for n, copied in enumerate((copied_low, copied_high)):
                    pe.wait_ge(copied, b * UNITS + (g + 1))
                    for k in range(4):
                        t = 4 * n + k
                        last = nc.tensor.transpose(transpose_psum[:, n, k * P:(k + 1) * P],
                                                   probs[:, g % PROBS, t * P:(t + 1) * P], ident[:])
                    last.then_inc(transposed, 1)

            pe.sem_inc(transposed, 2 * PROBS)
            for i in range(ST):
                project(("xt", i))
            pe.wait_ge(emptied[first.bank["xt", ST - 1]], empty(("xt", ST - 1)))
            pe.wait_ge(wqk_loaded, 32)
            for n in range(4):
                project(("qk", 0, n))
            pe.wait_ge(wv_loaded, 32)
            for i in range(EARLY_V):
                project(("v", i))
            pe.wait_ge(wo_loaded, 32)
            def program(b, filler, tail):
                for g in range(UNITS + LAG):
                    if g < UNITS:
                        scores(g, b)
                        for use in filler[g]:
                            if use in (("qk", 0, 0), ("qk", 0, 1)):
                                rows = ("xt", (use[2] + 1) * ST // 2 - 1)
                                pe.wait_ge(emptied[ring_of(b).bank[rows]], empty(rows, b))
                            project(use, b)
                    if g >= LAG:
                        transposes(g - LAG, b)
                for use in tail:
                    if use[0] == "x1t":
                        transpose_x1(use[1], b)
                    else:
                        project(use, b)

            batch_rows(pe, program)


def ffn_uses():
    gate_up = lambda i: [("gate_up", i, n) for n in range(2 * GROUPS)]
    down = lambda i: [("down", i, j) for j in range(KT)]
    back = [("y", r) for r in range(CT)]
    start = down(0) + [u for i in range(3, AHEAD) for u in gate_up(i) + down(i - 2)]
    start = start[:-KT]
    shared = down(LATE_DOWN) + [u for i in range(AHEAD, FI) for u in gate_up(i) + down(i - 2)]
    first = gate_up(0) + gate_up(1) + gate_up(2) + start
    body = shared + gate_up(0) + down(FI - 2) + gate_up(1) + down(FI - 1) + gate_up(2) + back + start
    last = shared + down(FI - 2) + down(FI - 1) + back
    return first, body, last


def build_ffn(nc, x1_scratch, x_parts_scratch, ffn_values, ident, consts_of, minus_half, out):
    f32, f32r = mybir.dt.float32, mybir.dt.float32r
    ALU, ACT, AX = mybir.AluOpType, mybir.ActivationFunctionType, mybir.AxisListType
    BANKS = 8
    first_uses, body_uses, last_uses = ffn_uses()
    first, body, last_ring = Ring(first_uses, BANKS), Ring(body_uses, BANKS), Ring(last_uses, BANKS)
    BODIES = CHUNKS - 1
    SLOTS = 3
    out_tiles = out.rearrange("b (t p) f -> (b t) p f", p=P)

    ctx = ExitStack()
    with ctx:
        sb = lambda name, shape, dt=f32: ctx.enter_context(nc.sbuf_tensor(name, shape, dt))
        sem = lambda name: ctx.enter_context(nc.semaphore(name))
        w = sb("w", [P, FI, 3 * KT, P], f32r)
        residual = sb("residual2", [P, CT, F])
        x_parts = sb("x_parts", [P, 2, 2, KT, NC], f32r)
        part = sb("part", [P, SLOTS, 4, NC])
        gate_up_sum = sb("gate_up_sum", [P, SLOTS, 2, NC])
        silu = sb("silu", [P, SLOTS, NC])
        h = sb("h", [P, SLOTS, NC])
        h_high = sb("h_high", [P, SLOTS, NC], f32r)
        h_low = sb("h_low", [P, SLOTS, NC], f32r)
        down_part = sb("down_part", [P, SLOTS, KT // 2, NC])
        yT = sb("yT", [P, KT, NC])
        y = sb("y", [P, CT, F])
        square = sb("square", [P, F])
        square_sum = sb("square_sum", [P, CT])
        mean_square = sb("mean_square", [P, CT])
        inv_rms = sb("inv_rms", [P, CT])
        psum = ctx.enter_context(nc.psum_tensor("ffn_psum", [P, BANKS, NC], f32))

        w_loaded = [sem(f"w_loaded{i}") for i in range(FI)]
        x_first_loaded = [sem(f"x_parts_first_loaded{k}") for k in range(KT)]
        x_loaded = sem("x_parts_loaded")
        residual_loaded = sem("residual2_loaded")
        products_done = sem("products_done")
        emptied = [sem(f"bank_emptied{n}") for n in range(BANKS)]
        gate_sum_ready = sem("gate_sum_ready")
        up_sum_ready = sem("up_sum_ready")
        silu_ready = sem("silu_ready")
        h_ready = sem("h_ready")
        h_high_ready = sem("h_high_ready")
        h_low_ready = sem("h_low_ready")
        y_added = sem("y_added")
        square_ready = sem("square_ready")
        mean_ready = sem("mean_ready")
        inv_rms_ready = sem("inv_rms_ready")
        out_ready = sem("out_ready")
        y_free = sem("y_free")
        out_stored = sem("out_stored")
        block = ctx.enter_context(nc.Block(name="ffn"))

        def tile_at(ap, n):
            return ap[bass.ds(n, 1)].rearrange("a p f -> (a p) f")

        class Phase:

            def __init__(self, c, ring, chunk):
                self.c, self.ring, self.chunk = c, ring, chunk

            def bank(self, use):
                return self.ring.bank[use]

            def done(self, use):
                return self.total(body.total, first.total) + self.ring.number[use] + 1

            def turn(self, use):
                bank = self.ring.bank[use]
                return self.total(body.turns[bank], first.turns[bank]) + self.ring.turn[use]

            def total(self, per_body, before):
                if self.ring is first:
                    return 0
                return self.chunk * per_body + before

            def chunk_of(self, use):
                kind, i = use[0], use[1]
                if self.ring is body and (kind == "gate_up" and i < AHEAD or kind == "down" and i < LATE_DOWN):
                    return self.chunk + 1
                return self.chunk

            def tile(self, use):
                return self.chunk_of(use) * FI + use[1]

        def phases(eng, program):
            program(Phase(None, first, 0), first_uses)
            with eng.Fori(0, BODIES) as c:
                program(Phase(c, body, c), body_uses)
            program(Phase(None, last_ring, BODIES), last_uses)


        def emptied_value(ph, use):
            return ph.turn(use) + 1

        def added(chunk, i, j):
            return chunk * ((FI - 1) * KT // 2) + ((i - 1) * KT // 2 + j // 2 + 1)

        def down_slot(i, j):
            return down_part[:, i % SLOTS, j // 2, :]

        def freed(i, count):
            back = {0: FI % SLOTS, 1: FI % SLOTS, 2: FI % SLOTS + SLOTS}.get(i, SLOTS)
            return None if isinstance(count, int) and count < back else count - (back - 1)

        def wait_freed(eng, semaphore, i, count):
            value = freed(i, count)
            if value is not None:
                eng.wait_ge(semaphore, value)

        def group_scale(use):
            _, i, n = use
            return consts_of["gu"](n % GROUPS, i + FI * (n // GROUPS))

        @block.sync
        def _(sp):
            x1_chunks = x1_scratch.rearrange("(c r) p f -> c p r f", r=CT)

            def chunk_at(c):
                return x1_chunks[c] if isinstance(c, int) else \
                    x1_chunks[bass.ds(c, 1)].rearrange("a p r f -> (a p) r f")

            def load_x(c):
                source = x_parts_scratch[c] if isinstance(c, int) else \
                    x_parts_scratch[bass.ds(c, 1)].rearrange("a p n k t -> (a p) n k t")
                slot = x_parts[:, c] if isinstance(c, int) else \
                    x_parts[:, bass.ds(c % 2, 1)].rearrange("p a n k t -> p (a n) k t")
                sp.dma_start(slot.bitcast(f32), source).then_inc(x_loaded, 16)

            def load_residual(c):
                sp.dma_start(residual[:], chunk_at(c)).then_inc(residual_loaded, 16)

            def store(c):
                for r in range(CT):
                    sp.wait_ge(out_ready, c * CT + (r + 1))
                    sp.dma_start(tile_at(out_tiles, c * CT + r), y[:, r, :]).then_inc(out_stored, 16)
                sp.wait_ge(out_stored, c * (16 * CT) + 16 * CT)
                sp.sem_inc(y_free, 1)

            def load_w(i):
                sp.dma_start(w[:, i].rearrange("p k n -> p (k n)").bitcast(f32),
                             ffn_values[i]).then_inc(w_loaded[i], 16)

            load_w(0)
            for k in range(KT):
                sp.dma_start(x_parts[:, 0, :, k, :].bitcast(f32), x_parts_scratch[0][:, :, k, :]
                             ).then_inc(x_first_loaded[k], 16)
            for i in range(1, FI):
                load_w(i)
            sp.sem_inc(y_free, 1)
            load_residual(0)
            load_x(1)
            with sp.Fori(0, BODIES - 1) as c:
                sp.wait_ge(products_done, Phase(c, body, c).done(("gate_up", FI - 1, 2 * GROUPS - 1)))
                sp.wait_ge(x_loaded, c * 16 + 16)
                load_x(c + 2)
                store(c)
                load_residual(c + 1)
            store(BODIES - 1)
            load_residual(BODIES)
            store(BODIES)

        @block.gpsimd
        def _(pool):
            def program(ph, uses):
                for use in uses:
                    kind = use[0]
                    if kind == "gate_up":
                        _, i, n = use
                        s, which = i % SLOTS, n // GROUPS
                        if n % GROUPS == GROUPS - 1:
                            tile = ph.tile(use)
                            pool.wait_ge(emptied[ph.bank(use)], emptied_value(ph, use))
                            wait_freed(pool, (silu_ready, h_ready)[which], i, tile)
                            nc.gpsimd.tensor_tensor(gate_up_sum[:, s, which, :], part[:, s, 2 * which, :],
                                                    part[:, s, 2 * which + 1, :], ALU.add
                                                    ).then_inc((gate_sum_ready, up_sum_ready)[which], 1)
                        if ph.ring is body and (i, n) == (5, 2):
                            inverse_rms(ph.chunk)
                    elif kind == "down":
                        _, i, j = use
                        if i and on_gpsimd(j):
                            pool.wait_ge(emptied[ph.bank(use)], emptied_value(ph, use))
                            if i > 1:
                                pool.wait_ge(y_added, added(ph.chunk_of(use), i - 1, j))
                            nc.gpsimd.tensor_tensor(yT[:, j, :], yT[:, j, :], down_slot(i, j), ALU.add
                                                    ).then_inc(y_added, 1)
                if ph.ring is last_ring:
                    inverse_rms(ph.chunk)

            def inverse_rms(chunk):
                pool.wait_ge(mean_ready, chunk + 1)
                nc.gpsimd.tensor_tensor(inv_rms[:], mean_square[:], minus_half[:, 0:CT], ALU.pow
                                        ).then_inc(inv_rms_ready, 1)

            phases(pool, program)

        @block.scalar
        def _(act):
            def program(ph, uses):
                for use in uses:
                    kind, bank = use[0], ph.bank(use)
                    if kind == "gate_up":
                        _, i, n = use
                        s = i % SLOTS
                        if n % 2 == 0:
                            wait_freed(act, gate_sum_ready if n < GROUPS else up_sum_ready, i, ph.tile(use))
                            act.wait_ge(products_done, ph.done(use))
                            nc.scalar.activation(part[:, s, n // 2, :], psum[:, bank, :], ACT.Copy,
                                                 scale=group_scale(use)).then_inc(emptied[bank], 1)
                        if n == 2 * GROUPS - 2 and (i or ph.ring is body):
                            round_h((i - 1) % FI, ph.tile(use) - 1)
                        if ph.ring is body and (i, n) in SQUARE_AT:
                            square_y(ph, SQUARE_AT.index((i, n)))
                        if n == 2 * GROUPS - 1:
                            act.wait_ge(gate_sum_ready, ph.tile(use) + 1)
                            nc.scalar.activation(silu[:, s, :], gate_up_sum[:, s, 0, :],
                                                 ACT.Silu).then_inc(silu_ready, 1)
                    elif kind == "down":
                        _, i, j = use
                        if on_gpsimd(j):
                            target = down_slot(i, j) if i else yT[:, j, :]
                            if i > SLOTS and on_gpsimd(j):
                                act.wait_ge(y_added, added(ph.chunk_of(use), i - SLOTS, j))
                            act.wait_ge(products_done, ph.done(use))
                            nc.scalar.activation(target, psum[:, bank, :], ACT.Copy,
                                                 scale=consts_of["down"](i, j)).then_inc(emptied[bank], 1)
                        if ph.ring is last_ring and (i, j) == (FI - 3, KT - 1):
                            round_h(FI - 1, ph.chunk * FI + (FI - 1))
                    elif kind == "y":
                        r = use[1]
                        act.wait_ge(products_done, ph.done(use))
                        if r == 0:
                            act.wait_ge(y_free, ph.chunk + 1)
                        nc.scalar.activation(y[:, r, :], psum[:, bank, :], ACT.Copy).then_inc(emptied[bank], 1)
                if ph.ring is last_ring:
                    for r in range(CT):
                        square_y(ph, r)

            SQUARE_AT = ((3, 1), (3, 5), (4, 1), (4, 5))

            def square_y(ph, r):
                use = ("y", r)
                act.wait_ge(emptied[ph.bank(use)], emptied_value(ph, use))
                if r or ph.ring is last_ring:
                    act.wait_ge(square_ready, ph.chunk * CT + r)
                nc.scalar.activation(square[:], y[:, r, :], ACT.Square, scale=F ** -0.5,
                                     accum_out=square_sum[:, r:r + 1]).then_inc(square_ready, 1)

            def round_h(i, tile):
                act.wait_ge(h_ready, tile + 1)
                nc.scalar.activation(h_high[:, i % SLOTS, :], h[:, i % SLOTS, :],
                                     ACT.Copy).then_inc(h_high_ready, 1)

            phases(act, program)

        @block.vector
        def _(dve):
            def multiply_h(i, tile):
                dve.wait_ge(silu_ready, tile + 1)
                dve.wait_ge(up_sum_ready, tile + 1)
                nc.vector.tensor_tensor(h[:, i % SLOTS, :], silu[:, i % SLOTS, :], gate_up_sum[:, i % SLOTS, 1, :],
                                        ALU.mult).then_inc(h_ready, 1)

            def low_h(i, tile):
                dve.wait_ge(h_high_ready, tile + 1)
                nc.vector.tensor_tensor(h_low[:, i % SLOTS, :], h[:, i % SLOTS, :],
                                        h_high[:, i % SLOTS, :].bitcast(f32), ALU.subtract
                                        ).then_inc(h_low_ready, 1)

            def add_eps(chunk):
                dve.wait_ge(square_ready, chunk * CT + CT)
                nc.vector.tensor_scalar(mean_square[:], square_sum[:], RMS_EPS, None, ALU.add
                                        ).then_inc(mean_ready, 1)

            def finish(chunk, r):
                dve.wait_ge(inv_rms_ready, chunk + 1)
                dve.wait_ge(residual_loaded, chunk * 16 + 16)
                nc.vector.scalar_tensor_tensor(y[:, r, :], y[:, r, :], inv_rms[:, r:r + 1], residual[:, r, :],
                                               ALU.mult, ALU.add).then_inc(out_ready, 1)

            def program(ph, uses):
                for use in uses:
                    kind, bank = use[0], ph.bank(use)
                    if kind == "gate_up":
                        _, i, n = use
                        s = i % SLOTS
                        tile = ph.tile(use)
                        if n % 2:
                            pair = ("gate_up", i, n - 1)
                            dve.wait_ge(emptied[ph.bank(pair)], emptied_value(ph, pair))
                            dve.wait_ge(products_done, ph.done(use))
                            nc.vector.scalar_tensor_tensor(part[:, s, n // 2, :], psum[:, bank, :],
                                                           group_scale(use), part[:, s, n // 2, :], ALU.mult,
                                                           ALU.add).then_inc(emptied[bank], 1)
                        if n == GROUPS - 1 and (i or ph.ring is body):
                            multiply_h((i - 1) % FI, tile - 1)
                        if n == 2 * GROUPS - 1 and i == 1 and ph.ring is first:
                            low_h(0, 0)
                        if ph.ring is body:
                            if (i, n) == (5, 0):
                                add_eps(ph.chunk)
                            if i in range(5, AHEAD) and n == 2 * GROUPS - 1:
                                finish(ph.chunk, i - 5)
                    elif kind == "down":
                        _, i, j = use
                        if not on_gpsimd(j):
                            scale = consts_of["down"](i, j)
                            if ph.ring is last_ring and i >= FI - 2:
                                own = ("down", i - 1, j)
                                dve.wait_ge(emptied[ph.bank(own)], emptied_value(ph, own))
                            dve.wait_ge(products_done, ph.done(use))
                            if i == 0:
                                op = nc.vector.tensor_scalar(yT[:, j, :], psum[:, bank, :], scale, None, ALU.mult)
                            else:
                                op = nc.vector.scalar_tensor_tensor(yT[:, j, :], psum[:, bank, :], scale,
                                                                    yT[:, j, :], ALU.mult, ALU.add)
                            op.then_inc(emptied[bank], 1)
                        if j == KT - 1:
                            if ph.ring is last_ring and i == FI - 3:
                                multiply_h(FI - 1, ph.chunk * FI + (FI - 1))
                                low_h(FI - 2, ph.chunk * FI + (FI - 2))
                            elif i < FI - 1 or ph.ring is body:
                                low_h((i + 1) % FI, ph.tile(use) + 1)
                if ph.ring is last_ring:
                    add_eps(ph.chunk)
                    for r in range(CT):
                        finish(ph.chunk, r)

            phases(dve, program)

        @block.tensor
        def _(pe):
            def program(ph, uses):
                for use in uses:
                    kind, bank = use[0], ph.bank(use)
                    if not (ph.ring is first and first.turn[use] == 0):
                        pe.wait_ge(emptied[bank], ph.turn(use))
                    if kind == "gate_up":
                        _, i, n = use
                        which, k = n // GROUPS, n % GROUPS
                        if i == 0 and ph.ring is first and n < GROUPS:
                            pe.wait_ge(x_first_loaded[n], 16)
                        if i == 0 and ph.ring is body and n == 0:
                            pe.wait_ge(x_loaded, ph.chunk_of(use) * 16)
                        if n == 0 and not (ph.ring is body and i < AHEAD):
                            pe.wait_ge(w_loaded[i], 16)
                        for part in range(2):
                            last = nc.tensor.matmul(psum[:, bank, :], w[:, i, which * KT + k, :],
                                                    x_part(ph.chunk_of(use), part, k), start=part == 0,
                                                    stop=part == 1)
                    elif kind == "down":
                        _, i, j = use
                        if j == 0:
                            pe.wait_ge(h_low_ready, ph.tile(use) + 1)
                        for moving in (h_high, h_low):
                            last = nc.tensor.matmul(psum[:, bank, :], w[:, i, 2 * KT + j, :],
                                                    moving[:, i % SLOTS, :], start=moving is h_high,
                                                    stop=moving is h_low)
                    elif kind == "y":
                        r = use[1]
                        if r == 0:
                            for j in range(KT):
                                if on_gpsimd(j):
                                    pe.wait_ge(y_added, added(ph.chunk, FI - 1, j))
                                else:
                                    own = ("down", FI - 1, j)
                                    pe.wait_ge(emptied[ph.bank(own)], emptied_value(ph, own))
                        for j in range(KT):
                            last = nc.tensor.transpose(psum[:, bank, j * P:(j + 1) * P],
                                                       yT[:, j, r * P:(r + 1) * P], ident[:])
                    last.then_inc(products_done, 1)

            def x_part(chunk, part, k):
                if isinstance(chunk, int):
                    return x_parts[:, chunk % 2, part, k, :]
                return x_parts[:, bass.ds(chunk % 2, 1), part, k, :].rearrange("p a t -> p (a t)")

            phases(pe, program)


_OUTS = [((BATCH, SEQ, F), "float32")]
_INS = ["L0_attn_x", "L0_attn_Wq", "L0_attn_bq", "L0_attn_Wk", "L0_attn_bk", "L0_attn_Wv", "L0_attn_bv", "L0_attn_Wo",
        "L0_attn_bo", "L0_ffn_gate_up_packed", "L0_ffn_gate_up_scales", "L0_ffn_down_packed", "L0_ffn_down_scales"]


def kernel(**inputs):
    import numpy as _np
    import concourse.bacc as _bacc
    from concourse import mybir as _mybir
    from concourse.bass_utils import run_bass_kernel_spmd as _run

    nc = _bacc.Bacc("TRN2", target_bir_lowering=False, num_devices=1)
    arrays, args = {}, []
    for name in _INS:
        a = _np.ascontiguousarray(inputs[name])
        arrays[f"in_{name}_dram"] = a
        args.append(nc.dram_tensor(f"in_{name}_dram", a.shape, _mybir.dt.from_np(a.dtype), kind="ExternalInput").ap())
    for i, (shape, dtype) in enumerate(_OUTS):
        dt = _mybir.dt.from_np(_np.dtype(dtype))
        args.append(nc.dram_tensor(f"out_{i}_dram", shape, dt, kind="ExternalOutput").ap())
    build(nc, *args)
    r = _run(nc, [arrays], core_ids=[0])
    return r.results[0]["out_0_dram"]
```
